# Optimizing a Trainium2 kernel written in Bass

```python
import numpy as np
import jax
import jax.numpy as jnp

def _softmax(x, axis=-1):
    return jax.nn.softmax(x, axis=axis)

def _gelu(x):
    return jax.nn.gelu(x, approximate=True)

def _silu(x):
    return jax.nn.silu(x)

def _sigmoid(x):
    return jax.nn.sigmoid(x)

def _layernorm(x, axis=-1, eps=1e-05):
    m = jnp.mean(x, axis=axis, keepdims=True)
    v = jnp.var(x, axis=axis, keepdims=True)
    return (x - m) / jnp.sqrt(v + eps)

def _scatter_add(tgt, idx, src, axis=0):
    return tgt.at[idx].add(src)

def _segment_sum(src, seg, n):
    return jax.ops.segment_sum(src, seg, n)
kernel_name = 'mk_gnn_resnorm_d4_gnn_r8_b9b66f'

def setup_inputs(seed: int=0):
    np.random.seed(seed)
    _w = jnp.asarray

    def _rec_inputs():
        import jax
        import jax.numpy as jnp
        _gk = jax.random.key(seed)
        x = -0.000202 + 1 * jax.random.normal(jax.random.fold_in(_gk, 1), (6250, 64), jnp.float32)
        src = jax.random.randint(jax.random.fold_in(_gk, 2), (200000,), 0, 6250, jnp.int32)
        dst = jnp.minimum((6250 * jax.random.uniform(jax.random.fold_in(_gk, 3), (200000,)) ** 2.0).astype(jnp.int32), 49999)
        _o = jnp.argsort(dst, stable=True)
        src = src[_o]
        dst = dst[_o]
        edge_attr_16 = 0.000196303 + 1.00016 * jax.random.normal(jax.random.fold_in(_gk, 13), (200000, 16), jnp.float32)
        edge_attr_64 = -5.16925e-05 + 1.00005 * jax.random.normal(jax.random.fold_in(_gk, 14), (200000, 64), jnp.float32)
        return (x, src, dst, edge_attr_16, edge_attr_64)
    x, src, dst, edge_attr_16, edge_attr_64 = _rec_inputs()

    def _L0_gnn_setup():
        import jax, jax.numpy as jnp
        import numpy as np
        N, E, D, ED, G = (12500, 200000, 64, 64, 512)
        LN_EPS = 1e-05

        def _gine_conv(x, src, dst, edge_attr, We, be, Wm, bm, eps):
            ea = jax.nn.silu(edge_attr @ We + be)
            msg = jax.nn.silu(jnp.maximum(x[src] + ea, 0.0) @ Wm + bm)
            agg = jax.ops.segment_sum(msg, dst, num_segments=x.shape[0])
            return agg + (1.0 + eps) * x

        def _graph_norm(x, g, gamma, beta):
            f = x.shape[1]
            cnt = jax.ops.segment_sum(jnp.ones((x.shape[0],), x.dtype), g, num_segments=G) * f
            cnt = jnp.maximum(cnt, 1.0)
            mean = jax.ops.segment_sum(x.sum(-1), g, num_segments=G) / cnt
            var = jax.ops.segment_sum((x * x).sum(-1), g, num_segments=G) / cnt - mean ** 2
            xn = (x - mean[g][:, None]) / jnp.sqrt(var + LN_EPS)[g][:, None]
            return xn * gamma + beta
        key = jax.random.key(seed)
        ks = jax.random.split(key, 16)
        s_e = 1.0 / np.sqrt(ED)
        s_n = 1.0 / np.sqrt(D)
        inp = {'x': jax.random.normal(ks[0], (N, D), jnp.float32), 'edge_index': jax.random.randint(ks[1], (2, E), 0, N, dtype=jnp.int32), 'edge_attr': jax.random.normal(ks[2], (E, ED), jnp.float32), 'node2graph': jnp.sort(jax.random.randint(ks[3], (N,), 0, G, dtype=jnp.int32)), 'We1': jax.random.normal(ks[4], (ED, D), jnp.float32) * s_e, 'be1': jnp.zeros((D,), jnp.float32), 'Wm1': jax.random.normal(ks[5], (D, D), jnp.float32) * s_n, 'bm1': jnp.zeros((D,), jnp.float32), 'eps1': jnp.array([0.1], jnp.float32), 'gamma1': jnp.ones((D,), jnp.float32), 'beta1': jnp.zeros((D,), jnp.float32), 'We2': jax.random.normal(ks[6], (ED, D), jnp.float32) * s_e, 'be2': jnp.zeros((D,), jnp.float32), 'Wm2': jax.random.normal(ks[7], (D, D), jnp.float32) * s_n, 'bm2': jnp.zeros((D,), jnp.float32), 'eps2': jnp.array([0.1], jnp.float32), 'gamma2': jnp.ones((D,), jnp.float32), 'beta2': jnp.zeros((D,), jnp.float32)}
        return inp
    _L0_gnn_all = _L0_gnn_setup()
    _L0_gnn_in = {k: v for k, v in _L0_gnn_all.items() if k in ('We1', 'be1', 'Wm1', 'bm1', 'eps1', 'gamma1', 'beta1', 'We2', 'be2', 'Wm2', 'bm2', 'eps2', 'gamma2', 'beta2')}
    del _L0_gnn_all

    def _L1_gnn_setup():
        import jax, jax.numpy as jnp
        import numpy as np
        N_NODES = 12500
        N_EDGES = 200000
        HIDDEN = 64
        LEAKY_SLOPE = 0.01
        key = jax.random.key(seed)
        k1, k2, k3, k4 = jax.random.split(key, 4)
        x = jax.random.normal(k1, (N_NODES, HIDDEN), dtype=jnp.float32)
        edge_index = jax.random.randint(k2, (2, N_EDGES), 0, N_NODES, dtype=jnp.int64)
        w_i = jax.random.normal(k3, (HIDDEN,), dtype=jnp.float32) * 0.1
        w_j = jax.random.normal(k4, (HIDDEN,), dtype=jnp.float32) * 0.1
        return {'x': x, 'edge_index': edge_index, 'w_i': w_i, 'w_j': w_j}
    _L1_gnn_all = _L1_gnn_setup()
    _L1_gnn_in = {k: v for k, v in _L1_gnn_all.items() if k in ('w_i', 'w_j')}
    del _L1_gnn_all

    def _L2_gnn_setup():
        import jax, jax.numpy as jnp
        import numpy as np
        N_NODES = 12500
        N_EDGES = 400000
        EMB_DIM = 64
        NUM_LAYERS = 3
        key = jax.random.key(seed)
        k1, k2, k3 = jax.random.split(key, 3)
        emb = jax.random.normal(k1, (N_NODES, EMB_DIM), dtype=jnp.float32) * 0.1
        src = jax.random.randint(k2, (N_EDGES,), 0, N_NODES, dtype=jnp.int32)
        dst = jax.random.randint(k3, (N_EDGES,), 0, N_NODES, dtype=jnp.int32)
        return {'emb': emb, 'src': src, 'dst': dst, 'num_layers': NUM_LAYERS}
    _L2_gnn_all = _L2_gnn_setup()
    _L2_gnn_in = {k: v for k, v in _L2_gnn_all.items() if k in ()}
    del _L2_gnn_all

    def _L3_gnn_setup():
        import jax, jax.numpy as jnp
        import numpy as np
        N_NODES = 12500
        EPS_GIN = 0.0
        BN_EPS = 1e-05
        key = jax.random.key(seed)
        ks = jax.random.split(key, 6)
        N, E, D, DE = (N_NODES, 200000, 64, 16)
        x = jax.random.normal(ks[0], (N, D), dtype=jnp.float32)
        edge_index = jax.random.randint(ks[1], (2, E), 0, N, dtype=jnp.int64)
        edge_attr = jax.random.normal(ks[2], (E, DE), dtype=jnp.float32)
        W_e = jax.random.normal(ks[3], (DE, D), dtype=jnp.float32) / np.sqrt(DE)
        b_e = jnp.zeros((D,), dtype=jnp.float32)
        W_gin = jax.random.normal(ks[4], (D, D), dtype=jnp.float32) / np.sqrt(D)
        b_gin = jnp.zeros((D,), dtype=jnp.float32)
        gamma = jnp.ones((D,), dtype=jnp.float32)
        beta = jnp.zeros((D,), dtype=jnp.float32)
        return {'x': x, 'edge_index': edge_index, 'edge_attr': edge_attr, 'W_e': W_e, 'b_e': b_e, 'W_gin': W_gin, 'b_gin': b_gin, 'gamma': gamma, 'beta': beta}
    _L3_gnn_all = _L3_gnn_setup()
    _L3_gnn_in = {k: v for k, v in _L3_gnn_all.items() if k in ('W_e', 'b_e', 'W_gin', 'b_gin', 'gamma', 'beta')}
    del _L3_gnn_all
    return {'x': x, 'src': src, 'dst': dst, 'edge_attr_16': edge_attr_16, 'edge_attr_64': edge_attr_64, 'L0_gnn_We1': _L0_gnn_in['We1'], 'L0_gnn_be1': _L0_gnn_in['be1'], 'L0_gnn_Wm1': _L0_gnn_in['Wm1'], 'L0_gnn_bm1': _L0_gnn_in['bm1'], 'L0_gnn_eps1': _L0_gnn_in['eps1'], 'L0_gnn_gamma1': _L0_gnn_in['gamma1'], 'L0_gnn_beta1': _L0_gnn_in['beta1'], 'L0_gnn_We2': _L0_gnn_in['We2'], 'L0_gnn_be2': _L0_gnn_in['be2'], 'L0_gnn_Wm2': _L0_gnn_in['Wm2'], 'L0_gnn_bm2': _L0_gnn_in['bm2'], 'L0_gnn_eps2': _L0_gnn_in['eps2'], 'L0_gnn_gamma2': _L0_gnn_in['gamma2'], 'L0_gnn_beta2': _L0_gnn_in['beta2'], 'L1_gnn_w_i': _L1_gnn_in['w_i'], 'L1_gnn_w_j': _L1_gnn_in['w_j'], 'L3_gnn_W_e': _L3_gnn_in['W_e'], 'L3_gnn_b_e': _L3_gnn_in['b_e'], 'L3_gnn_W_gin': _L3_gnn_in['W_gin'], 'L3_gnn_b_gin': _L3_gnn_in['b_gin'], 'L3_gnn_gamma': _L3_gnn_in['gamma'], 'L3_gnn_beta': _L3_gnn_in['beta']}

def reference(x, src, dst, edge_attr_16, edge_attr_64, L0_gnn_We1, L0_gnn_be1, L0_gnn_Wm1, L0_gnn_bm1, L0_gnn_eps1, L0_gnn_gamma1, L0_gnn_beta1, L0_gnn_We2, L0_gnn_be2, L0_gnn_Wm2, L0_gnn_bm2, L0_gnn_eps2, L0_gnn_gamma2, L0_gnn_beta2, L1_gnn_w_i, L1_gnn_w_j, L3_gnn_W_e, L3_gnn_b_e, L3_gnn_W_gin, L3_gnn_b_gin, L3_gnn_gamma, L3_gnn_beta):
    import jax
    import jax.numpy as jnp

    def _L0_gnn_ref(x, edge_index, edge_attr, node2graph, We1, be1, Wm1, bm1, eps1, gamma1, beta1, We2, be2, Wm2, bm2, eps2, gamma2, beta2):
        import jax, jax.numpy as jnp
        import numpy as np
        N, E, D, ED, G = (12500, 200000, 64, 64, 512)
        LN_EPS = 1e-05

        def _gine_conv(x, src, dst, edge_attr, We, be, Wm, bm, eps):
            ea = jax.nn.silu(edge_attr @ We + be)
            msg = jax.nn.silu(jnp.maximum(x[src] + ea, 0.0) @ Wm + bm)
            agg = jax.ops.segment_sum(msg, dst, num_segments=x.shape[0])
            return agg + (1.0 + eps) * x

        def _graph_norm(x, g, gamma, beta):
            f = x.shape[1]
            cnt = jax.ops.segment_sum(jnp.ones((x.shape[0],), x.dtype), g, num_segments=G) * f
            cnt = jnp.maximum(cnt, 1.0)
            mean = jax.ops.segment_sum(x.sum(-1), g, num_segments=G) / cnt
            var = jax.ops.segment_sum((x * x).sum(-1), g, num_segments=G) / cnt - mean ** 2
            xn = (x - mean[g][:, None]) / jnp.sqrt(var + LN_EPS)[g][:, None]
            return xn * gamma + beta
        src, dst = (edge_index[0], edge_index[1])
        identity = x
        out = _gine_conv(x, src, dst, edge_attr, We1, be1, Wm1, bm1, eps1)
        out = _graph_norm(out, node2graph, gamma1, beta1)
        out = jnp.maximum(out, 0.0)
        out = _gine_conv(x, src, dst, edge_attr, We2, be2, Wm2, bm2, eps2)
        out = _graph_norm(out, node2graph, gamma2, beta2)
        out = out + identity
        return jnp.maximum(out, 0.0)

    def _L1_gnn_ref(x, edge_index, w_i, w_j):
        import jax, jax.numpy as jnp
        import numpy as np
        N_NODES = 12500
        N_EDGES = 200000
        HIDDEN = 64
        LEAKY_SLOPE = 0.01
        n = x.shape[0]
        ej, ei = (edge_index[0], edge_index[1])
        s_i = x @ w_i
        s_j = x @ w_j
        e = jax.nn.leaky_relu(s_i[ei] + s_j[ej], LEAKY_SLOPE)
        emax = jax.ops.segment_max(e, ei, num_segments=n)
        ex = jnp.exp(e - emax[ei])
        denom = jax.ops.segment_sum(ex, ei, num_segments=n)
        alpha = ex / denom[ei]
        out = jax.ops.segment_sum(alpha[:, None] * x[ej], ei, num_segments=n)
        return jax.nn.relu(out)

    def _L2_gnn_ref(emb, src, dst, num_layers):
        import jax, jax.numpy as jnp
        import numpy as np
        N_NODES = 12500
        N_EDGES = 400000
        EMB_DIM = 64
        NUM_LAYERS = 3
        n = emb.shape[0]
        ones = jnp.ones(src.shape[0], dtype=emb.dtype)
        deg_out = jax.ops.segment_sum(ones, src, num_segments=n)
        deg_in = jax.ops.segment_sum(ones, dst, num_segments=n)
        inv_sqrt_out = jnp.where(deg_out > 0, deg_out, 1.0) ** (-0.5)
        inv_sqrt_in = jnp.where(deg_in > 0, deg_in, 1.0) ** (-0.5)
        h = emb * inv_sqrt_out[:, None]
        agg = jax.ops.segment_sum(h[src], dst, num_segments=n)
        prop = agg * inv_sqrt_in[:, None]
        alpha_total = sum((1.0 / (1.0 + k) for k in range(num_layers)))
        return prop * jnp.asarray(alpha_total, dtype=emb.dtype)

    def _L3_gnn_ref(x, edge_index, edge_attr, W_e, b_e, W_gin, b_gin, gamma, beta):
        import jax, jax.numpy as jnp
        import numpy as np
        N_NODES = 12500
        EPS_GIN = 0.0
        BN_EPS = 1e-05
        e = edge_attr @ W_e + b_e
        src, dst = (edge_index[0], edge_index[1])
        msg = jax.nn.relu(x[src] + e)
        agg = jax.ops.segment_sum(msg, dst, num_segments=x.shape[0])
        h = ((1.0 + EPS_GIN) * x + agg) @ W_gin + b_gin
        mean = jnp.mean(h, axis=0)
        var = jnp.var(h, axis=0)
        h = (h - mean) * jax.lax.rsqrt(var + BN_EPS) * gamma + beta
        return jax.nn.relu(h)
    edge_index = jnp.stack([src, dst])
    batch0 = jnp.zeros((6250,), jnp.int32)
    x = _layernorm(x + _L0_gnn_ref(x, edge_index, edge_attr_64, batch0, L0_gnn_We1, L0_gnn_be1, L0_gnn_Wm1, L0_gnn_bm1, L0_gnn_eps1, L0_gnn_gamma1, L0_gnn_beta1, L0_gnn_We2, L0_gnn_be2, L0_gnn_Wm2, L0_gnn_bm2, L0_gnn_eps2, L0_gnn_gamma2, L0_gnn_beta2), axis=-1)
    x = _layernorm(x + _L1_gnn_ref(x, edge_index, L1_gnn_w_i, L1_gnn_w_j), axis=-1)
    x = _layernorm(x + _L2_gnn_ref(x, src, dst, 3), axis=-1)
    x = _layernorm(x + _L3_gnn_ref(x, edge_index, edge_attr_16, L3_gnn_W_e, L3_gnn_b_e, L3_gnn_W_gin, L3_gnn_b_gin, L3_gnn_gamma, L3_gnn_beta), axis=-1)
    return x

_drawn_inputs = setup_inputs


def setup_inputs(seed=0):
    import zlib

    import numpy as np

    out = dict(_drawn_inputs(seed))
    spreads = {'L0_gnn_be1': (0.0, 0.1),
     'L0_gnn_bm1': (0.0, 0.1),
     'L0_gnn_gamma1': (1.0, 0.2),
     'L0_gnn_beta1': (0.0, 0.1),
     'L0_gnn_be2': (0.0, 0.1),
     'L0_gnn_bm2': (0.0, 0.1),
     'L0_gnn_gamma2': (1.0, 0.2),
     'L0_gnn_beta2': (0.0, 0.1),
     'L3_gnn_b_e': (0.0, 0.1),
     'L3_gnn_b_gin': (0.0, 0.1),
     'L3_gnn_gamma': (1.0, 0.2),
     'L3_gnn_beta': (0.0, 0.1)}
    factors = {}
    for name, (base, spread) in spreads.items():
        noise = np.random.default_rng([zlib.crc32(name.encode()), seed]).standard_normal(out[name].shape)
        drawn = base * np.exp(spread * noise) if base else spread * noise
        out[name] = jnp.asarray(drawn.astype(out[name].dtype))
    for name, factor in factors.items():
        out[name] = (out[name] * factor).astype(out[name].dtype)
    return out
```

```python
import concourse.bass as bass
from concourse import mybir
from contextlib import ExitStack

f32 = mybir.dt.float32
bf16 = mybir.dt.bfloat16
i32 = mybir.dt.int32
ALU = mybir.AluOpType
ACT = mybir.ActivationFunctionType
AX = mybir.AxisListType.X

P = 128
N = 6250
E = 200000
D = 64
D3 = 16
NT = -(-N // P)
NP = NT * P
LAST = N - (NT - 1) * P
C = 8
GE = C * P
RING = 4
G = -(-E // GE)
G += -G % RING
ROUNDS = G // RING
EP = G * GE
Q = G // 2
EPS = 1e-5
SLOPE = 0.01
ALPHA_TOTAL = 1.0 + 1.0 / 2.0 + 1.0 / 3.0
BANK = 512


def need(eng, sem, value):
    if isinstance(value, int) and value <= 0:
        return
    eng.wait_ge(sem, value)


def over_groups(eng, step, tail=None):
    for r in range(RING):
        step(0, r)
    with eng.Fori(1, ROUNDS) as i:
        for r in range(RING):
            step(i, r)
    if tail is not None:
        tail()


class Chain:

    def __init__(self, eng, sem):
        self.eng, self.sem, self.count = eng, sem, 0

    def then(self, instruction):
        instruction.then_inc(self.sem, 1)
        self.count += 1
        self.eng.wait_ge(self.sem, self.count)


def build_program(nc, x, src, dst, edge16, edge64, We2, be2, Wm2, bm2, eps2, gamma2, beta2,
                  w_i, w_j, W_e, b_e, W_gin, b_gin, gamma3, beta3, out):
    with ExitStack() as ctx:
        def sb(name, shape, dt=f32, where=ctx):
            return where.enter_context(nc.sbuf_tensor(name, shape, dt))

        def sem(name, where=ctx):
            return where.enter_context(nc.semaphore(name))

        bank = [ctx.enter_context(nc.psum_tensor(f"bank{j}", [P, BANK], f32)) for j in range(6)]
        wide = ctx.enter_context(nc.psum_tensor("wide", [P, 2 * BANK], f32))

        table = [x] + [nc.dram_tensor(f"table{n}", (NP, D), f32, kind="Internal").ap() for n in (1, 2, 3)]
        si_row = nc.dram_tensor("si_row", (NP,), f32, kind="Internal").ap()

        ident = sb("ident", [P, P])
        ones = sb("ones", [P, P])
        iota0 = sb("iota0", [P, P])
        iota = sb("iota", [P, P])
        real = sb("real", [P, 1])
        dst_rel = sb("dst_rel", [P, G * C])
        src_lo = sb("src_lo", [P, G * C])
        src_hi = sb("src_hi", [P, G * C])
        start0 = sb("start0", [1, G])
        start_f = sb("start_f", [1, G])
        start_i = sb("start_i", [1, G], i32)
        passes = sb("passes", [1, 1], i32)
        node_sum = sb("node_sum", [D + 1, NP + P])
        xn = sb("xn", [P, NT, D])
        out_deg = sb("out_deg", [P, NT])
        rows = sb("rows", [P, 2, NT, D])
        stat = sb("stat", [P, 8, NT])

        WeBD = sb("WeBD", [P, P])
        WmBD = sb("WmBD", [P, P])
        W3BD = sb("W3BD", [P, C * D])
        Wgin = sb("Wgin", [D, D])
        be_col = sb("be_col", [P, 1])
        bm_row = sb("bm_row", [1, C * D])
        eps_col = sb("eps_col", [P, 1])
        vec = {n: sb(n + "_b", [P, D]) for n in ("gamma2", "beta2", "w_i", "w_j", "b_e", "b_gin", "gamma3", "beta3")}

        with ExitStack() as ps:
            dst_i = sb("dst_i", [Q, 2 * GE], i32, ps)
            src_i = sb("src_i", [Q, 2 * GE], i32, ps)
            lo_i = sb("lo_i", [Q, 2 * GE], i32, ps)
            byrow = [sb(f"byrow{j}", [Q, 2 * GE], f32, ps) for j in range(3)]
            iota_i = sb("iota_i", [P, P + 1], i32, ps)
            part = sb("part", [P, 1], f32, ps)
            low = sb("low", [Q, 2], f32, ps)
            high = sb("high", [Q, 2], f32, ps)
            diag = sb("diag", [Q, 2, Q], f32, ps)
            span = sb("span", [1, 2], f32, ps)
            span_i = sb("span_i", [1, 1], i32, ps)
            s_idx, s_zero, s_w, s_iota, s_v = (sem(n, ps) for n in ("s_idx", "s_zero", "s_w", "s_iota", "s_v"))
            s_const, s_rows, s_turned, s_kept, s_ends, s_row1, s_diag, s_base = (
                sem(n, ps) for n in ("s_const", "s_rows", "s_turned", "s_kept", "s_ends", "s_row1", "s_diag", "s_base"))
            with nc.Block() as block:
                @block.sync
                def _(sp):
                    sp.dma_start(dst_i[:, :], dst.rearrange("(q e) -> q e", q=Q)).then_inc(s_idx, 16)
                    sp.dma_start(src_i[:, :], src.rearrange("(q e) -> q e", q=Q)).then_inc(s_idx, 16)
                    sp.dma_start(xn[:, :, :], x.rearrange("(t p) d -> p t d", p=P)).then_inc(s_w, 16)
                    given = {"gamma2": gamma2, "beta2": beta2, "w_i": w_i, "w_j": w_j, "b_e": b_e,
                             "b_gin": b_gin, "gamma3": gamma3, "beta3": beta3}
                    for name, v in given.items():
                        sp.dma_start(vec[name][:, :], v.partition_broadcast(P)).then_inc(s_w, 16)
                    sp.dma_start(eps_col[:, :], eps2.partition_broadcast(P)).then_inc(s_w, 16)
                    sp.dma_start(Wgin[:, :], W_gin).then_inc(s_w, 16)
                    for c in range(C):
                        sp.dma_start(bm_row[0:1, c * D:(c + 1) * D], bm2.unsqueeze(0)).then_inc(s_w, 16)
                    for h in range(2):
                        sp.dma_start(be_col[h * D:(h + 1) * D, :], be2.unsqueeze(1)).then_inc(s_w, 16)
                    sp.wait_ge(s_zero, 4)
                    for h in range(2):
                        at = slice(h * D, (h + 1) * D)
                        sp.dma_start(WeBD[at, at], We2).then_inc(s_w, 16)
                        sp.dma_start(WmBD[at, at], Wm2).then_inc(s_w, 16)
                    for c in range(C):
                        sp.dma_start(W3BD[c * D3:(c + 1) * D3, c * D:(c + 1) * D], W_e).then_inc(s_w, 16)
                    sp.wait_ge(s_w, 16 * (1 + 8 + 2 + C + 2 + 4 + C))

                @block.gpsimd
                def _(pool):
                    nc.gpsimd.memset(WeBD[:, :], 0.0).then_inc(s_zero, 1)
                    nc.gpsimd.memset(WmBD[:, :], 0.0).then_inc(s_zero, 1)
                    nc.gpsimd.memset(W3BD[:, :], 0.0).then_inc(s_zero, 1)
                    nc.gpsimd.memset(ones[:, :], 1.0).then_inc(s_zero, 1)
                    nc.gpsimd.iota(iota_i[:, 0:P], [[1, P]], base=0, channel_multiplier=0).then_inc(s_iota, 1)
                    nc.gpsimd.iota(iota_i[:, P:P + 1], [[0, 1]], base=0, channel_multiplier=1).then_inc(s_iota, 1)

                @block.vector
                def _(dve):
                    chain = Chain(dve, s_v)
                    dve.wait_ge(s_iota, 2)
                    nc.vector.tensor_copy(iota0[:, :], iota_i[:, 0:P])
                    chain.then(nc.vector.tensor_copy(part[:, :], iota_i[:, P:P + 1]))
                    nc.vector.tensor_scalar(real[:, :], part[:, :], float(LAST), None, ALU.is_lt)
                    nc.vector.tensor_scalar(ident[:, :], iota0[:, :], part[:, 0:1], None, ALU.is_equal).then_inc(s_const, 1)
                    dve.wait_ge(s_idx, 32)
                    nc.vector.tensor_copy(byrow[0][:, :], dst_i[:, :])
                    chain.then(nc.vector.tensor_scalar(lo_i[:, :], src_i[:, :], P - 1, None, ALU.bitwise_and))
                    chain.then(nc.vector.tensor_copy(byrow[1][:, :], lo_i[:, :]))
                    chain.then(nc.vector.tensor_scalar(lo_i[:, :], src_i[:, :], 7, None, ALU.arith_shift_right))
                    nc.vector.tensor_copy(byrow[2][:, :], lo_i[:, :]).then_inc(s_rows, 1)
                    two = byrow[0][:, :].rearrange("q (b e) -> q b e", b=2)
                    nc.vector.tensor_reduce(low[:, :], two, AX, ALU.min)
                    chain.then(nc.vector.tensor_reduce(high[:, :], two, AX, ALU.max))
                    chain.then(nc.vector.tensor_tensor(high[:, :], high[:, :], low[:, :], ALU.subtract))
                    for b in range(2):
                        last = nc.vector.tensor_scalar(diag[:, b, :], ident[0:Q, 0:Q], low[:, b:b + 1], None, ALU.mult)
                    last.then_inc(s_ends, 1)
                    dve.wait_ge(s_row1, 1)
                    chain.then(nc.vector.tensor_copy(start0[0:1, :].rearrange("o (q b) -> o b q", b=2),
                                                     bank[4][0:1, 0:2 * P].rearrange("o (b q) -> o b q", b=2)[:, :, 0:Q]))
                    chain.then(nc.vector.tensor_reduce(span[0:1, 0:1], bank[4][0:1, 2 * P:4 * P].rearrange("o (b q) -> o b q", b=2)[:, :, 0:Q],
                                                       mybir.AxisListType.XY, ALU.max))
                    chain.then(nc.vector.tensor_copy(span_i[0:1, :], span[0:1, 0:1]))
                    chain.then(nc.vector.tensor_scalar(span_i[0:1, :], span_i[0:1, :], 7, None, ALU.arith_shift_right))
                    chain.then(nc.vector.tensor_scalar(passes[0:1, :], span_i[0:1, :], 1, None, ALU.add))
                    for j, kept in enumerate((dst_rel, src_lo, src_hi)):
                        to = kept[:, :].rearrange("p (q b c) -> p b c q", b=2, c=C)
                        for b in range(2):
                            for h in range(2):
                                n = (j * 2 + b) * 2 + h
                                dve.wait_ge(s_turned, n + 1)
                                ps_view = bank[n % 2][:, :].rearrange("p (c q) -> p c q", c=4)[:, :, 0:Q]
                                nc.vector.tensor_copy(to[:, b, 4 * h:4 * h + 4, :], ps_view).then_inc(s_kept, 1)
                    dve.wait_ge(s_base, 1)
                    dve.wait_ge(s_kept, 12)
                    for b in range(2):
                        view = dst_rel[:, :].rearrange("p (q b c) -> p b q c", b=2, c=C)[:, b]
                        base = bank[5][:, b * P:b * P + Q].unsqueeze(2).to_broadcast([P, Q, C])
                        chain.then(nc.vector.tensor_tensor(view, view, base, ALU.subtract))

                @block.tensor
                def _(pe):
                    pe.wait_ge(s_const, 1)
                    pe.wait_ge(s_rows, 1)
                    pe.wait_ge(s_ends, 1)
                    pe.wait_ge(s_zero, 4)
                    for b in range(2):
                        nc.tensor.matmul(bank[4][0:1, b * P:b * P + Q], low[:, b:b + 1], ident[0:Q, 0:Q], start=True, stop=True)
                    for b in range(2):
                        last = nc.tensor.matmul(bank[4][0:1, (2 + b) * P:(2 + b) * P + Q], high[:, b:b + 1], ident[0:Q, 0:Q], start=True, stop=True)
                    last.then_inc(s_row1, 1)
                    for b in range(2):
                        last = nc.tensor.matmul(bank[5][:, b * P:b * P + Q], ones[0:Q, :], diag[:, b, :], start=True, stop=True)
                    last.then_inc(s_base, 1)
                    for j in range(3):
                        for b in range(2):
                            from_ = byrow[j][:, b * GE:(b + 1) * GE].rearrange("q (p c) -> q c p", c=C)
                            for h in range(2):
                                n = (j * 2 + b) * 2 + h
                                need(pe, s_kept, n - 1)
                                for c in range(4):
                                    last = nc.tensor.transpose(bank[n % 2][:, c * P:c * P + Q], from_[:, 4 * h + c, :], ident[0:Q, 0:Q])
                                last.then_inc(s_turned, 1)

        npasses = nc.values_load(passes[0:1, 0:1], min_val=1, max_val=NT)

        S = {n: sem(n) for n in (
            "attr_in", "idx_in", "gathered",
            "x_turned", "a_turned", "a_kept", "e_product", "e_done", "summed", "m_done", "m_product", "msg_done",
            "hot_done", "scattered", "added",
            "hist_done", "moved", "may_gather",
            "v_a", "v_b", "scaled", "keys_done", "masked", "keys_turned", "hot_turned", "hot_kept", "max_found",
            "diag_done", "max_spread", "factor_in", "factor_done", "cols_done", "looked_up", "exp_in", "exp_done",
        )}
        ring_sems = {n: [sem(f"{n}{r}") for r in range(RING)] for n in ("attr_in", "idx_in", "gathered")}

        def zero_state(layer):
            with nc.Block() as block:
                @block.vector
                def _(dve):
                    nc.vector.memset(node_sum[:, :], 0.0)
                    nc.vector.tensor_copy(iota[:, :], iota0[:, :])
                    nc.vector.tensor_copy(start_f[0:1, :], start0[0:1, :])
                    nc.vector.tensor_copy(start_i[0:1, :], start0[0:1, :])

        def next_pass():
            with nc.Block() as block:
                @block.vector
                def _(dve):
                    chain = Chain(dve, S["moved"])
                    nc.vector.tensor_scalar(iota[:, :], iota[:, :], float(P), None, ALU.add)
                    chain.then(nc.vector.tensor_scalar(start_f[0:1, :], start_f[0:1, :], float(P), float(NP), ALU.add, ALU.min))
                    nc.vector.tensor_copy(start_i[0:1, :], start_f[0:1, :])
            with nc.Block() as block:
                @block.sync
                def _(sp):
                    for s in S.values():
                        sp.sem_clear(s)
                    for name in ("attr_in", "idx_in"):
                        for s in ring_sems[name]:
                            sp.sem_clear(s)

                @block.gpsimd
                def _(pool):
                    for s in ring_sems["gathered"]:
                        pool.wait_ge(s, 16 * C * ROUNDS)
                    pool.dma_reset()
                    for s in ring_sems["gathered"]:
                        pool.sem_clear(s)

        def edge_loads(xg, idx, attr, attr_dram, width):
            idx_view = src.rearrange("(i r p c) -> i r p c", r=RING, p=P, c=C)
            attr_view = None if attr is None else attr_dram.rearrange("(i r p c) d -> i r p (c d)", r=RING, p=P, c=C)

            def program(sp, attr_used):
                def step(i, r):
                    need(sp, ring_sems["gathered"][r], 16 * C * i)
                    sp.dma_start(idx[:, r, :], idx_view[i, r]).then_inc(ring_sems["idx_in"][r], 16)
                    if attr is not None:
                        need(sp, attr_used, RING * i + r - (RING - 1))
                        sp.dma_start(attr[:, r, :], attr_view[i, r]).then_inc(ring_sems["attr_in"][r], 16)
                over_groups(sp, step)
            return program

        def gathers(layer, xg, idx):
            def program(pool, rows_used):
                def step(i, r):
                    pool.wait_ge(ring_sems["idx_in"][r], 16 * (i + 1))
                    need(pool, rows_used, RING * i + r - (RING - 1))
                    pool.sem_inc(S["may_gather"], 1)
                    for c in range(C):
                        nc.gpsimd.indirect_dma_start(xg[:, r, c, 0:D], None, table[layer][:, :],
                                                     bass.IndirectOffsetOnAxis(ap=idx[:, r, c:c + 1], axis=0),
                                                     ).then_inc(ring_sems["gathered"][r], 16)
                over_groups(pool, step)
            return program

        def one_hot(hot, i, r):
            n = RING * i + r
            col = dst_rel[:, bass.ds(n * C, C)] if not isinstance(n, int) else dst_rel[:, n * C:(n + 1) * C]
            return nc.vector.tensor_tensor(hot[:, r % 2], iota[:, :].unsqueeze(1).to_broadcast([P, C, P]),
                                           col.unsqueeze(2).to_broadcast([P, C, P]), ALU.is_equal)

        def window(eng, n):
            at = start_i[0:1, n:n + 1] if isinstance(n, int) else start_i[0:1, bass.ds(n, 1)]
            return eng.value_load(at, min_val=0, max_val=NP)

        with ExitStack() as ls:
            xg = sb("xg", [P, RING, C, D], f32, ls)
            idx = sb("idx", [P, RING, C], i32, ls)
            attr = sb("attr", [P, RING, C * D], f32, ls)
            attrT = sb("attrT", [P, 4 * P], f32, ls)
            eaT = sb("eaT", [P, 4 * P], f32, ls)
            sumT = sb("sumT", [P, 4 * P], f32, ls)
            mT = sb("mT", [P, 2, 4 * P], f32, ls)
            msg = sb("msg", [P, 2, C, D], f32, ls)
            hot = sb("hot", [P, 2, C, P], f32, ls)
            lo_hot = sb("lo_hot", [P, 2, C, P], bf16, ls)
            hi_hot = sb("hi_hot", [P, 2, C, NT], bf16, ls)
            pA, pE, pM, pG = bank[0], bank[1], bank[2], bank[3]
            pX = [bank[4], bank[5]]
            pH = wide
            zero_state(0)
            with nc.Fori(0, npasses):
                with nc.Block() as block:
                    load = edge_loads(xg, idx, attr, edge64, C * D)
                    gather = gathers(0, xg, idx)

                    @block.sync
                    def _(sp):
                        load(sp, S["a_turned"])

                    @block.gpsimd
                    def _(pool):
                        gather(pool, S["x_turned"])

                    @block.tensor
                    def _(pe):
                        def message(n, b):
                            pe.wait_ge(S["m_done"], n + 1)
                            need(pe, S["msg_done"], n)
                            nc.tensor.matmul(pM[:, :], ones[0:1, :], bm_row[0:1, :], start=True, stop=False)
                            for j in range(4):
                                last = nc.tensor.matmul(pM[:, j * P:(j + 1) * P], mT[:, b, j * P:(j + 1) * P], WmBD[:, :],
                                                        start=False, stop=(j == 3))
                            last.then_inc(S["m_product"], 1)

                        def scatter(n, b):
                            pe.wait_ge(S["msg_done"], n + 1)
                            pe.wait_ge(S["hot_done"], n + 1)
                            need(pe, S["added"], n)
                            for c in range(C):
                                last = nc.tensor.matmul(pG[0:D, 0:P], msg[:, b, c, :], hot[:, b, c, :], start=(c == 0), stop=(c == C - 1))
                            last.then_inc(S["scattered"], 1)

                        def step(i, r):
                            n, b = RING * i + r, r % 2
                            first = isinstance(n, int) and n == 0
                            pe.wait_ge(ring_sems["attr_in"][r], 16 * (i + 1))
                            need(pe, S["a_kept"], n)
                            for j in range(4):
                                last = nc.tensor.transpose(pA[:, j * P:(j + 1) * P], attr[:, r, j * P:(j + 1) * P], ident[:, :])
                            last.then_inc(S["a_turned"], 1)
                            pe.wait_ge(ring_sems["gathered"][r], 16 * C * (i + 1))
                            need(pe, S["m_done"], n - 1)
                            for j in range(4):
                                last = nc.tensor.transpose(pX[b][:, j * P:(j + 1) * P],
                                                           xg[:, r, 2 * j:2 * j + 2, :].rearrange("p c d -> p (c d)"), ident[:, :])
                            last.then_inc(S["x_turned"], 1)
                            if not first:
                                message(n - 1, 1 - b)
                            pe.wait_ge(S["a_kept"], n + 1)
                            need(pe, S["e_done"], n)
                            nc.tensor.matmul(pE[:, :], WeBD[:, :], attrT[:, :], start=True, stop=True).then_inc(S["e_product"], 1)
                            pe.wait_ge(S["keys_done"], n + 1)
                            for c in range(C):
                                last = nc.tensor.matmul(pH[:, 0:NT], lo_hot[:, b, c, :], hi_hot[:, b, c, :],
                                                        start=(first and c == 0), stop=False, skip_group_check=True)
                            last.then_inc(S["hist_done"], 1)
                            if not first:
                                scatter(n - 1, 1 - b)

                        def tail():
                            message(G - 1, 1)
                            scatter(G - 1, 1)
                        over_groups(pe, step, tail)

                    @block.scalar
                    def _(act):
                        def messages(n, b):
                            act.wait_ge(S["m_product"], n + 1)
                            need(act, S["scattered"], n - 1)
                            nc.scalar.activation(msg[:, b].rearrange("p c d -> p (c d)"), pM[:, :], ACT.Silu).then_inc(S["msg_done"], 1)

                        def step(i, r):
                            n, b = RING * i + r, r % 2
                            act.wait_ge(S["a_turned"], n + 1)
                            need(act, S["e_product"], n)
                            nc.scalar.copy(attrT[:, :], pA[:, :]).then_inc(S["a_kept"], 1)
                            if not (isinstance(n, int) and n == 0):
                                messages(n - 1, 1 - b)
                            act.wait_ge(S["e_product"], n + 1)
                            need(act, S["summed"], n)
                            nc.scalar.activation(eaT[:, :], pE[:, :], ACT.Silu, bias=be_col[:, 0:1]).then_inc(S["e_done"], 1)
                        over_groups(act, step, lambda: messages(G - 1, 1))

                    @block.vector
                    def _(dve):
                        def add(n):
                            w = window(dve, n)
                            dve.wait_ge(S["scattered"], n + 1)
                            need(dve, S["added"], n)
                            nc.vector.tensor_tensor(node_sum[0:D, bass.ds(w, P)], node_sum[0:D, bass.ds(w, P)],
                                                    pG[0:D, 0:P], ALU.add).then_inc(S["added"], 1)

                        def step(i, r):
                            n, b = RING * i + r, r % 2
                            cols = bass.ds(n * C, C) if not isinstance(n, int) else slice(n * C, (n + 1) * C)
                            need(dve, S["scattered"], n - 1)
                            one_hot(hot, i, r).then_inc(S["hot_done"], 1)
                            need(dve, S["hist_done"], n - 1)
                            nc.vector.tensor_tensor(lo_hot[:, b], iota0[:, :].unsqueeze(1).to_broadcast([P, C, P]),
                                                    src_lo[:, cols].unsqueeze(2).to_broadcast([P, C, P]), ALU.is_equal)
                            nc.vector.tensor_tensor(hi_hot[:, b], iota0[:, 0:NT].unsqueeze(1).to_broadcast([P, C, NT]),
                                                    src_hi[:, cols].unsqueeze(2).to_broadcast([P, C, NT]), ALU.is_equal).then_inc(S["keys_done"], 1)
                            if not (isinstance(n, int) and n == 0):
                                add(n - 1)
                            dve.wait_ge(S["x_turned"], n + 1)
                            dve.wait_ge(S["e_done"], n + 1)
                            need(dve, S["m_done"], n)
                            nc.vector.tensor_tensor(sumT[:, :], pX[b][:, :], eaT[:, :], ALU.add).then_inc(S["summed"], 1)
                            dve.wait_ge(S["summed"], n + 1)
                            need(dve, S["m_product"], n - 1)
                            nc.vector.tensor_scalar(mT[:, b, :], sumT[:, :], 0.0, None, ALU.max).then_inc(S["m_done"], 1)
                        over_groups(dve, step, lambda: add(G - 1))
                next_pass()

        def turned_tiles(pe, dve, chain, features, per, done, used, use):
            pass

        def transposes(pe, features, per, s_turn, s_used):
            for j, t0 in enumerate(range(0, NT, per)):
                need(pe, s_used, j - 1)
                for t in range(t0, min(t0 + per, NT)):
                    last = nc.tensor.transpose(bank[j % 2][:, (t - t0) * features:(t - t0 + 1) * features],
                                               node_sum[0:features, t * P:(t + 1) * P], ident[0:features, 0:features])
                last.then_inc(s_turn, 1)

        def read_tiles(dve, features, per, s_turn, s_used, use):
            for j, t0 in enumerate(range(0, NT, per)):
                dve.wait_ge(s_turn, j + 1)
                k = min(per, NT - t0)
                view = bank[j % 2][:, 0:k * features].rearrange("p (t f) -> p t f", f=features)
                use(t0, t0 + k, view).then_inc(s_used, 1)

        def over_tiles(v, free=D):
            return v.unsqueeze(1).to_broadcast([P, NT, free])

        def over_features(v):
            return v.unsqueeze(2).to_broadcast([P, NT, D])

        def layer_norm(dve, chain, y, s_var, s_std, turn):
            mean, var = stat[:, 0, :], stat[:, 1, :]
            chain.then(nc.vector.tensor_reduce(mean, y, AX, ALU.add))
            chain.then(nc.vector.tensor_scalar(mean, mean, 1.0 / D, None, ALU.mult))
            chain.then(nc.vector.tensor_tensor(y, y, over_features(mean), ALU.subtract))
            chain.then(nc.vector.tensor_tensor(rows[:, 1], y, y, ALU.mult))
            chain.then(nc.vector.tensor_reduce(var, rows[:, 1], AX, ALU.add))
            nc.vector.tensor_scalar(var, var, 1.0 / D, EPS, ALU.mult, ALU.add).then_inc(s_var, 1)
            dve.wait_ge(s_std, turn)
            chain.then(nc.vector.reciprocal(var, var))
            chain.then(nc.vector.tensor_tensor(xn[:, :, :], y, over_features(var), ALU.mult))

        with ExitStack() as ls:
            names = ("s_v", "s_turn", "s_used", "s_part", "s_total", "s_var", "s_std", "s_table", "s_si", "s_siT", "s_siK",
                     "s_least", "s_leastT", "s_leastR", "s_leastB", "s_row")
            (s_v, s_turn, s_used, s_part, s_total, s_var, s_std, s_table, s_si, s_siT, s_siK,
             s_least, s_leastT, s_leastR, s_leastB, s_row) = (sem(n, ls) for n in names)
            max_row = sb("max_row", [P, NP + P], f32, ls)
            si_all = sb("si_all", [P, NP + P], f32, ls)
            least = sb("least", [P, 1], f32, ls)
            least_row = sb("least_row", [1, P + 1], f32, ls)
            parts = sb("parts", [P, 2], f32, ls)
            tot = sb("tot", [P, 8], f32, ls)
            eps1 = sb("eps1", [P, 1], f32, ls)
            si_tiles = sb("si_tiles", [NT, P], f32, ls)
            y = rows[:, 0]
            with nc.Block() as block:
                @block.tensor
                def _(pe):
                    transposes(pe, D, 8, s_turn, s_used)
                    pe.wait_ge(s_part, 1)
                    nc.tensor.matmul(bank[2][:, 0:2], ones[:, :], parts[:, :], start=True, stop=True).then_inc(s_total, 1)
                    pe.wait_ge(s_least, 1)
                    nc.tensor.transpose(bank[3][0:1, 0:P], least[:, :], ident[:, :]).then_inc(s_leastT, 1)
                    pe.wait_ge(s_leastR, 1)
                    nc.tensor.matmul(bank[4][:, 0:1], ones[0:1, :], least_row[0:1, P:P + 1], start=True, stop=True).then_inc(s_leastB, 1)
                    pe.wait_ge(s_si, 1)
                    nc.tensor.transpose(bank[5][0:NT, 0:P], stat[:, 2, :], ident[:, :]).then_inc(s_siT, 1)

                @block.scalar
                def _(act):
                    act.wait_ge(s_var, 1)
                    nc.scalar.sqrt(tot[:, 4:5], tot[:, 3:4]).then_inc(s_std, 1)
                    act.wait_ge(s_var, 2)
                    nc.scalar.sqrt(stat[:, 1, :], stat[:, 1, :]).then_inc(s_std, 1)

                @block.sync
                def _(sp):
                    sp.wait_ge(s_table, 1)
                    sp.dma_start(table[1].rearrange("(t p) d -> p t d", p=P), xn[:, :, :]).then_inc(s_row, 16)
                    sp.wait_ge(s_siK, 1)
                    sp.wait_ge(s_row, 16)
                    sp.dma_start(si_row.rearrange("(t p) -> t p", p=P), si_tiles[:, :]).then_inc(s_row, 16)
                    sp.wait_ge(s_row, 32)
                    sp.dma_start(si_all[:, 0:NP], si_row.partition_broadcast(P)).then_inc(s_row, 16)
                    sp.wait_ge(s_row, 48)

                @block.vector
                def _(dve):
                    chain = Chain(dve, s_v)
                    nc.vector.tensor_copy(out_deg[:, :], pH[:, 0:NT])
                    nc.vector.memset(max_row[:, :], 0.0)
                    nc.vector.memset(si_all[:, NP:NP + P], 0.0)
                    chain.then(nc.vector.tensor_scalar(eps1[:, :], eps_col[:, :], 1.0, None, ALU.add))
                    read_tiles(dve, D, 8, s_turn, s_used, lambda a, z, v: nc.vector.scalar_tensor_tensor(
                        out=y[:, a:z, :], in0=xn[:, a:z, :], scalar=eps1[:, 0:1], in1=v, op0=ALU.mult, op1=ALU.add))
                    dve.wait_ge(s_used, -(-NT // 8))
                    chain.then(nc.vector.tensor_scalar(y[:, NT - 1, :], y[:, NT - 1, :], real[:, 0:1], None, ALU.mult))
                    flat = y.rearrange("p t d -> p (t d)")
                    square = rows[:, 1].rearrange("p t d -> p (t d)")
                    nc.vector.tensor_reduce(parts[:, 0:1], flat, AX, ALU.add)
                    chain.then(nc.vector.tensor_tensor(square, flat, flat, ALU.mult))
                    nc.vector.tensor_reduce(parts[:, 1:2], square, AX, ALU.add).then_inc(s_part, 1)
                    dve.wait_ge(s_total, 1)
                    chain.then(nc.vector.tensor_scalar(tot[:, 0:2], bank[2][:, 0:2], 1.0 / (N * D), None, ALU.mult))
                    chain.then(nc.vector.tensor_tensor(tot[:, 2:3], tot[:, 0:1], tot[:, 0:1], ALU.mult))
                    chain.then(nc.vector.tensor_tensor(tot[:, 3:4], tot[:, 1:2], tot[:, 2:3], ALU.subtract))
                    nc.vector.tensor_scalar(tot[:, 3:4], tot[:, 3:4], EPS, None, ALU.add).then_inc(s_var, 1)
                    dve.wait_ge(s_std, 1)
                    chain.then(nc.vector.reciprocal(tot[:, 5:6], tot[:, 4:5]))
                    chain.then(nc.vector.tensor_scalar(flat, flat, tot[:, 0:1], tot[:, 5:6], ALU.subtract, ALU.mult))
                    chain.then(nc.vector.tensor_tensor(y, y, over_tiles(vec["gamma2"][:, :]), ALU.mult))
                    chain.then(nc.vector.tensor_tensor(y, y, over_tiles(vec["beta2"][:, :]), ALU.add))
                    chain.then(nc.vector.tensor_tensor(y, y, xn[:, :, :], ALU.add))
                    chain.then(nc.vector.scalar_tensor_tensor(out=y, in0=y, scalar=0.0, in1=xn[:, :, :], op0=ALU.max, op1=ALU.add))
                    layer_norm(dve, chain, y, s_var, s_std, 2)
                    nc.vector.tensor_copy(tot[:, 6:7], tot[:, 5:6]).then_inc(s_table, 1)
                    chain.then(nc.vector.tensor_tensor(y, xn[:, :, :], over_tiles(vec["w_j"][:, :]), ALU.mult))
                    chain.then(nc.vector.tensor_reduce(stat[:, 2, :], y, AX, ALU.add))
                    nc.vector.tensor_reduce(least[:, :], stat[:, 2, :], AX, ALU.min).then_inc(s_least, 1)
                    dve.wait_ge(s_leastT, 1)
                    nc.vector.tensor_reduce(least_row[0:1, P:P + 1], bank[3][0:1, 0:P], AX, ALU.min).then_inc(s_leastR, 1)
                    chain.then(nc.vector.tensor_tensor(y, xn[:, :, :], over_tiles(vec["w_i"][:, :]), ALU.mult))
                    chain.then(nc.vector.tensor_reduce(stat[:, 2, :], y, AX, ALU.add))
                    dve.wait_ge(s_leastB, 1)
                    chain.then(nc.vector.tensor_copy(least[:, :], bank[4][:, 0:1]))
                    nc.vector.tensor_scalar(stat[:, 2, :], stat[:, 2, :], least[:, 0:1], None, ALU.add).then_inc(s_si, 1)
                    dve.wait_ge(s_siT, 1)
                    nc.vector.tensor_copy(si_tiles[:, :], bank[5][0:NT, 0:P]).then_inc(s_siK, 1)

            xg = sb("xg1", [P, RING, C, D], f32, ls)
            idx = sb("idx1", [P, RING, C], i32, ls)
            hot = sb("hot1", [P, 2, C, P], f32, ls)
            prod = sb("prod", [P, C, D], f32, ls)
            sj = sb("sj", [P, C], f32, ls)
            key = sb("key", [P, 2, C], f32, ls)
            mask = sb("mask", [P, C, P], f32, ls)
            hotT = sb("hotT", [P, 2, C * P], f32, ls)
            top = sb("top", [P, 2], f32, ls)
            topD = sb("topD", [P, P], f32, ls)
            newmax = sb("newmax", [P, P], f32, ls)
            sc = sb("sc", [P, 3, P], f32, ls)
            leaky = sb("leaky", [P, 2, P], f32, ls)
            drop = sb("drop", [P, P], f32, ls)
            fac = sb("fac", [P, P], f32, ls)
            picked = sb("picked", [P, 2, P], f32, ls)
            cols2 = sb("cols2", [P, 2], f32, ls)
            ea = sb("ea", [P, C], f32, ls)
            eb = sb("eb", [P, C], f32, ls)
            ec = sb("ec", [P, C], f32, ls)
            ex = sb("ex", [P, C], f32, ls)
            msg = sb("msg1", [P, 2, C, D + 1], f32, ls)
            pO = wide
            pK = [bank[0], bank[1]]
            pR, pL, pG = bank[2], bank[3], bank[4]
            zero_state(1)
            with nc.Fori(0, npasses):
                with nc.Block() as block:
                    load = edge_loads(xg, idx, None, None, 0)
                    gather = gathers(1, xg, idx)

                    @block.sync
                    def _(sp):
                        load(sp, None)

                    @block.gpsimd
                    def _(pool):
                        gather(pool, S["msg_done"])

                    @block.tensor
                    def _(pe):
                        def second(n, b):
                            pe.wait_ge(S["diag_done"], n + 1)
                            need(pe, S["v_b"], n)
                            nc.tensor.matmul(pR[:, 0:P], ones[:, :], topD[:, :], start=True, stop=True).then_inc(S["max_spread"], 1)
                            pe.wait_ge(S["cols_done"], n + 1)
                            pe.wait_ge(S["hot_kept"], n + 1)
                            need(pe, S["exp_in"], n)
                            for c in range(C):
                                last = nc.tensor.matmul(pL[:, 2 * c:2 * c + 2], hotT[:, b, c * P:(c + 1) * P], cols2[:, :], start=True, stop=True)
                            last.then_inc(S["looked_up"], 1)

                        def scatter(n, b):
                            pe.wait_ge(S["msg_done"], n + 1)
                            need(pe, S["added"], n)
                            for c in range(C):
                                last = nc.tensor.matmul(pG[0:D + 1, 0:P], msg[:, b, c, :], hot[:, b, c, :], start=(c == 0), stop=(c == C - 1))
                            last.then_inc(S["scattered"], 1)

                        def step(i, r):
                            n, b = RING * i + r, r % 2
                            first = isinstance(n, int) and n == 0
                            if not first:
                                second(n - 1, 1 - b)
                            pe.wait_ge(S["hot_done"], n + 1)
                            need(pe, S["hot_kept"], n)
                            for c in range(C):
                                last = nc.tensor.transpose(pO[:, c * P:(c + 1) * P], hot[:, b, c, :], ident[:, :])
                            last.then_inc(S["hot_turned"], 1)
                            if not first:
                                scatter(n - 1, 1 - b)
                            pe.wait_ge(S["masked"], n + 1)
                            need(pe, S["max_found"], n)
                            for c in range(C):
                                last = nc.tensor.transpose(pK[c // 4][:, (c % 4) * P:(c % 4 + 1) * P], mask[:, c, :], ident[:, :])
                            last.then_inc(S["keys_turned"], 1)

                        def tail():
                            second(G - 1, 1)
                            scatter(G - 1, 1)
                        over_groups(pe, step, tail)

                    @block.scalar
                    def _(act):
                        def factor(n):
                            act.wait_ge(S["factor_in"], n + 1)
                            need(act, S["scaled"], n)
                            nc.scalar.activation(fac[:, :], drop[:, :], ACT.Exp).then_inc(S["factor_done"], 1)
                            act.wait_ge(S["exp_in"], n + 1)
                            need(act, S["msg_done"], n)
                            nc.scalar.activation(ex[:, :], ec[:, :], ACT.Exp).then_inc(S["exp_done"], 1)

                        def step(i, r):
                            n, b = RING * i + r, r % 2
                            if not (isinstance(n, int) and n == 0):
                                factor(n - 1)
                            act.wait_ge(S["hot_done"], n + 1)
                            act.wait_ge(S["keys_done"], n + 1)
                            need(act, S["keys_turned"], n)
                            for c in range(C):
                                last = nc.scalar.activation(mask[:, c, :], hot[:, b, c, :], ACT.Copy, scale=key[:, b, c:c + 1])
                            last.then_inc(S["masked"], 1)
                            act.wait_ge(S["hot_turned"], n + 1)
                            need(act, S["looked_up"], n - 1)
                            for h in range(2):
                                last = nc.scalar.copy(hotT[:, b, h * BANK:(h + 1) * BANK], pO[:, h * BANK:(h + 1) * BANK])
                            last.then_inc(S["hot_kept"], 1)
                        over_groups(act, step, lambda: factor(G - 1))

                    @block.vector
                    def _(dve):
                        def spread(n, b):
                            dve.wait_ge(S["max_found"], n + 1)
                            need(dve, S["max_spread"], n)
                            nc.vector.tensor_scalar(topD[:, :], ident[:, :], top[:, b:b + 1], None, ALU.mult).then_inc(S["diag_done"], 1)

                        def scores(n, b):
                            w = window(dve, n)
                            k = 7 * n
                            dve.wait_ge(S["max_spread"], n + 1)
                            at = bass.ds(w, P)
                            nc.vector.tensor_tensor(newmax[:, :], max_row[:, at], pR[:, 0:P], ALU.max).then_inc(S["v_b"], 1)
                            nc.vector.tensor_tensor(sc[:, 0, :], max_row[:, at], si_all[:, at], ALU.add)
                            nc.vector.tensor_copy(sc[:, 1, :], si_all[:, at]).then_inc(S["v_a"], 1)
                            dve.wait_ge(S["v_b"], n + 1)
                            dve.wait_ge(S["v_a"], k + 1)
                            nc.vector.tensor_tensor(sc[:, 2, :], newmax[:, :], sc[:, 1, :], ALU.add)
                            nc.vector.tensor_copy(max_row[:, at], newmax[:, :]).then_inc(S["v_a"], 1)
                            dve.wait_ge(S["v_a"], k + 2)
                            two = sc[:, 0:3:2, :]
                            nc.vector.scalar_tensor_tensor(out=leaky[:, :, :], in0=two, scalar=SLOPE, in1=two,
                                                           op0=ALU.mult, op1=ALU.max).then_inc(S["v_a"], 1)
                            dve.wait_ge(S["v_a"], k + 3)
                            nc.vector.tensor_tensor(picked[:, 0, :], sc[:, 1, :], ident[:, :], ALU.mult)
                            nc.vector.tensor_tensor(picked[:, 1, :], leaky[:, 1, :], ident[:, :], ALU.mult).then_inc(S["v_a"], 1)
                            need(dve, S["factor_done"], n)
                            nc.vector.tensor_tensor(drop[:, :], leaky[:, 0, :], leaky[:, 1, :], ALU.subtract).then_inc(S["factor_in"], 1)
                            dve.wait_ge(S["v_a"], k + 4)
                            need(dve, S["looked_up"], n)
                            nc.vector.tensor_reduce(cols2[:, :], picked[:, :, :], AX, ALU.add).then_inc(S["cols_done"], 1)

                        def weights(n, b, r):
                            k = 7 * n
                            dve.wait_ge(S["looked_up"], n + 1)
                            found = pL[:, 0:2 * C].rearrange("p (c k) -> p c k", k=2)
                            nc.vector.tensor_tensor(ea[:, :], found[:, :, 0], key[:, b, :], ALU.add).then_inc(S["v_a"], 1)
                            dve.wait_ge(S["v_a"], k + 5)
                            nc.vector.scalar_tensor_tensor(out=eb[:, :], in0=ea[:, :], scalar=SLOPE, in1=ea[:, :],
                                                           op0=ALU.mult, op1=ALU.max).then_inc(S["v_a"], 1)
                            dve.wait_ge(S["v_a"], k + 6)
                            need(dve, S["exp_done"], n)
                            nc.vector.tensor_tensor(ec[:, :], eb[:, :], found[:, :, 1], ALU.subtract).then_inc(S["exp_in"], 1)
                            w = window(dve, n)
                            dve.wait_ge(S["factor_done"], n + 1)
                            need(dve, S["added"], n)
                            nc.vector.tensor_tensor(node_sum[:, bass.ds(w, P)], node_sum[:, bass.ds(w, P)], fac[0:D + 1, :],
                                                    ALU.mult).then_inc(S["scaled"], 1)
                            dve.wait_ge(S["exp_done"], n + 1)
                            need(dve, S["scattered"], n - 1)
                            nc.vector.tensor_copy(msg[:, b, :, D], ex[:, :]).then_inc(S["v_a"], 1)
                            nc.vector.tensor_tensor(msg[:, b, :, 0:D], xg[:, r, :, :], ex[:, :].unsqueeze(2).to_broadcast([P, C, D]),
                                                    ALU.mult).then_inc(S["msg_done"], 1)

                        def add(n):
                            w = window(dve, n)
                            dve.wait_ge(S["scattered"], n + 1)
                            dve.wait_ge(S["scaled"], n + 1)
                            nc.vector.tensor_tensor(node_sum[:, bass.ds(w, P)], node_sum[:, bass.ds(w, P)],
                                                    pG[0:D + 1, 0:P], ALU.add).then_inc(S["added"], 1)

                        def step(i, r):
                            n, b = RING * i + r, r % 2
                            first = isinstance(n, int) and n == 0
                            if not first:
                                spread(n - 1, 1 - b)
                            need(dve, S["scattered"], n - 1)
                            need(dve, S["hot_turned"], n - 1)
                            one_hot(hot, i, r).then_inc(S["hot_done"], 1)
                            if not first:
                                scores(n - 1, 1 - b)
                            dve.wait_ge(ring_sems["gathered"][r], 16 * C * (i + 1))
                            nc.vector.tensor_tensor(prod[:, :, :], xg[:, r, :, :], vec["w_j"][:, :].unsqueeze(1).to_broadcast([P, C, D]),
                                                    ALU.mult).then_inc(S["summed"], 1)
                            dve.wait_ge(S["summed"], 2 * n + 1)
                            nc.vector.tensor_reduce(sj[:, :], prod[:, :, :], AX, ALU.add).then_inc(S["summed"], 1)
                            dve.wait_ge(S["summed"], 2 * n + 2)
                            need(dve, S["masked"], n - 1)
                            nc.vector.tensor_scalar(key[:, b, :], sj[:, :], least[:, 0:1], None, ALU.subtract).then_inc(S["keys_done"], 1)
                            if not first:
                                weights(n - 1, 1 - b, (r - 1) % RING)
                            if not first:
                                add(n - 1)
                            dve.wait_ge(S["keys_turned"], n + 1)
                            for h in range(2):
                                last = nc.vector.tensor_reduce(sj[:, h:h + 1], pK[h][:, :], AX, ALU.max)
                            last.then_inc(S["m_done"], 1)
                            dve.wait_ge(S["m_done"], n + 1)
                            need(dve, S["diag_done"], n - 1)
                            nc.vector.tensor_tensor(top[:, b:b + 1], sj[:, 0:1], sj[:, 1:2], ALU.max).then_inc(S["max_found"], 1)

                        def tail():
                            spread(G - 1, 1)
                            scores(G - 1, 1)
                            weights(G - 1, 1, RING - 1)
                            add(G - 1)
                        over_groups(dve, step, tail)
                next_pass()

        with ExitStack() as ls:
            s_v, s_turn, s_used, s_var, s_std, s_table, s_store = (sem(n, ls) for n in (
                "n1_v", "n1_turn", "n1_used", "n1_var", "n1_std", "n1_table", "n1_store"))
            y, h = rows[:, 0], rows[:, 1]
            with nc.Block() as block:
                @block.tensor
                def _(pe):
                    transposes(pe, D + 1, 7, s_turn, s_used)

                @block.scalar
                def _(act):
                    act.wait_ge(s_var, 1)
                    nc.scalar.sqrt(stat[:, 1, :], stat[:, 1, :]).then_inc(s_std, 1)
                    act.wait_ge(s_var, 2)
                    nc.scalar.sqrt(stat[:, 4, :], stat[:, 3, :]).then_inc(s_std, 1)

                @block.sync
                def _(sp):
                    sp.wait_ge(s_table, 1)
                    sp.dma_start(table[2].rearrange("(t p) d -> p t d", p=P), h).then_inc(s_store, 16)
                    sp.wait_ge(s_store, 16)

                @block.vector
                def _(dve):
                    chain = Chain(dve, s_v)

                    def use(a, z, v):
                        chain.then(nc.vector.tensor_scalar(stat[:, 5, a:z], v[:, :, D], 1e-30, None, ALU.max))
                        chain.then(nc.vector.reciprocal(stat[:, 6, a:z], stat[:, 5, a:z]))
                        chain.then(nc.vector.tensor_tensor(y[:, a:z, :], v[:, :, 0:D], stat[:, 6, a:z].unsqueeze(2).to_broadcast([P, z - a, D]), ALU.mult))
                        return nc.vector.scalar_tensor_tensor(out=y[:, a:z, :], in0=y[:, a:z, :], scalar=0.0, in1=xn[:, a:z, :],
                                                              op0=ALU.max, op1=ALU.add)
                    read_tiles(dve, D + 1, 7, s_turn, s_used, use)
                    dve.wait_ge(s_used, NT // 7)
                    layer_norm(dve, chain, y, s_var, s_std, 1)
                    nc.vector.tensor_scalar(stat[:, 3, :], out_deg[:, :], 1.0, None, ALU.max).then_inc(s_var, 1)
                    dve.wait_ge(s_std, 2)
                    chain.then(nc.vector.reciprocal(stat[:, 4, :], stat[:, 4, :]))
                    nc.vector.tensor_tensor(h, xn[:, :, :], over_features(stat[:, 4, :]), ALU.mult).then_inc(s_table, 1)

        with ExitStack() as ls:
            xg = sb("xg2", [P, RING, C, D + 1], f32, ls)
            idx = sb("idx2", [P, RING, C], i32, ls)
            hot = sb("hot2", [P, 2, C, P], f32, ls)
            pG2 = [bank[0], bank[1]]
            zero_state(2)
            with nc.Block() as block:
                @block.vector
                def _(dve):
                    nc.vector.memset(xg[:, :, :, D:D + 1], 1.0)
            with nc.Fori(0, npasses):
                with nc.Block() as block:
                    load = edge_loads(xg, idx, None, None, 0)
                    gather = gathers(2, xg, idx)

                    @block.sync
                    def _(sp):
                        load(sp, None)

                    @block.gpsimd
                    def _(pool):
                        gather(pool, S["scattered"])

                    @block.tensor
                    def _(pe):
                        def step(i, r):
                            n, b = RING * i + r, r % 2
                            pe.wait_ge(ring_sems["gathered"][r], 16 * C * (i + 1))
                            pe.wait_ge(S["hot_done"], n + 1)
                            need(pe, S["added"], n - 1)
                            for c in range(C):
                                last = nc.tensor.matmul(pG2[b][0:D + 1, 0:P], xg[:, r, c, :], hot[:, b, c, :], start=(c == 0), stop=(c == C - 1))
                            last.then_inc(S["scattered"], 1)
                        over_groups(pe, step)

                    @block.vector
                    def _(dve):
                        def add(n, b):
                            w = window(dve, n)
                            dve.wait_ge(S["scattered"], n + 1)
                            need(dve, S["added"], n)
                            nc.vector.tensor_tensor(node_sum[:, bass.ds(w, P)], node_sum[:, bass.ds(w, P)],
                                                    pG2[b][0:D + 1, 0:P], ALU.add).then_inc(S["added"], 1)

                        def step(i, r):
                            n, b = RING * i + r, r % 2
                            need(dve, S["scattered"], n - 1)
                            one_hot(hot, i, r).then_inc(S["hot_done"], 1)
                            if not (isinstance(n, int) and n == 0):
                                add(n - 1, 1 - b)
                        over_groups(dve, step, lambda: add(G - 1, 1))
                next_pass()

        with ExitStack() as ls:
            s_v, s_turn, s_used, s_var, s_std, s_table, s_store, s_deg = (sem(n, ls) for n in (
                "n2_v", "n2_turn", "n2_used", "n2_var", "n2_std", "n2_table", "n2_store", "n2_deg"))
            y, h = rows[:, 0], rows[:, 1]
            in_deg = stat[:, 3, :]
            with nc.Block() as block:
                @block.tensor
                def _(pe):
                    transposes(pe, D + 1, 7, s_turn, s_used)

                @block.scalar
                def _(act):
                    act.wait_ge(s_var, 1)
                    nc.scalar.sqrt(stat[:, 4, :], in_deg).then_inc(s_std, 1)
                    act.wait_ge(s_var, 2)
                    nc.scalar.sqrt(stat[:, 1, :], stat[:, 1, :]).then_inc(s_std, 1)

                @block.sync
                def _(sp):
                    sp.wait_ge(s_table, 1)
                    sp.dma_start(table[3].rearrange("(t p) d -> p t d", p=P), h).then_inc(s_store, 16)
                    sp.wait_ge(s_store, 16)

                @block.vector
                def _(dve):
                    chain = Chain(dve, s_v)

                    def use(a, z, v):
                        chain.then(nc.vector.tensor_scalar(in_deg[:, a:z], v[:, :, D], 1.0, None, ALU.max))
                        return nc.vector.tensor_copy(y[:, a:z, :], v[:, :, 0:D])
                    read_tiles(dve, D + 1, 7, s_turn, s_used, use)
                    dve.wait_ge(s_used, NT // 7)
                    nc.vector.tensor_copy(stat[:, 5, :], in_deg).then_inc(s_var, 1)
                    dve.wait_ge(s_std, 1)
                    chain.then(nc.vector.reciprocal(stat[:, 4, :], stat[:, 4, :]))
                    chain.then(nc.vector.tensor_tensor(y, y, over_features(stat[:, 4, :]), ALU.mult))
                    chain.then(nc.vector.scalar_tensor_tensor(out=y, in0=y, scalar=ALPHA_TOTAL, in1=xn[:, :, :], op0=ALU.mult, op1=ALU.add))
                    layer_norm(dve, chain, y, s_var, s_std, 2)
                    nc.vector.tensor_tensor(h, xn[:, :, :], over_tiles(vec["b_e"][:, :]), ALU.add).then_inc(s_table, 1)

        with ExitStack() as ls:
            xg = sb("xg3", [P, RING, C, D], f32, ls)
            idx = sb("idx3", [P, RING, C], i32, ls)
            attr = sb("attr3", [P, RING, C * D3], f32, ls)
            attrT = sb("attrT3", [P, P], f32, ls)
            msg = sb("msg3", [P, 2, C, D], f32, ls)
            hot = sb("hot3", [P, 2, C, P], f32, ls)
            pA, pG = bank[0], bank[1]
            pE = [bank[2], bank[3]]
            zero_state(3)
            with nc.Fori(0, npasses):
                with nc.Block() as block:
                    load = edge_loads(xg, idx, attr, edge16, C * D3)
                    gather = gathers(3, xg, idx)

                    @block.sync
                    def _(sp):
                        load(sp, S["a_turned"])

                    @block.gpsimd
                    def _(pool):
                        gather(pool, S["e_product"])

                    @block.tensor
                    def _(pe):
                        def scatter(n, b):
                            pe.wait_ge(S["msg_done"], n + 1)
                            pe.wait_ge(S["hot_done"], n + 1)
                            need(pe, S["added"], n)
                            for c in range(C):
                                last = nc.tensor.matmul(pG[0:D, 0:P], msg[:, b, c, :], hot[:, b, c, :], start=(c == 0), stop=(c == C - 1))
                            last.then_inc(S["scattered"], 1)

                        def step(i, r):
                            n, b = RING * i + r, r % 2
                            pe.wait_ge(ring_sems["attr_in"][r], 16 * (i + 1))
                            need(pe, S["a_kept"], n)
                            nc.tensor.transpose(pA[:, 0:P], attr[:, r, :], ident[:, :]).then_inc(S["a_turned"], 1)
                            if not (isinstance(n, int) and n == 0):
                                scatter(n - 1, 1 - b)
                            pe.wait_ge(S["a_kept"], n + 1)
                            pe.wait_ge(ring_sems["gathered"][r], 16 * C * (i + 1))
                            need(pe, S["msg_done"], n - 1)
                            nc.tensor.matmul(pE[b][:, :], attrT[:, :], W3BD[:, :], start=True, stop=False)
                            nc.tensor.matmul(pE[b][:, :], ident[:, :], xg[:, r].rearrange("p c d -> p (c d)"),
                                             start=False, stop=True).then_inc(S["e_product"], 1)
                        over_groups(pe, step, lambda: scatter(G - 1, 1))

                    @block.scalar
                    def _(act):
                        def step(i, r):
                            n, b = RING * i + r, r % 2
                            act.wait_ge(S["a_turned"], n + 1)
                            need(act, S["e_product"], n)
                            nc.scalar.copy(attrT[:, :], pA[:, 0:P]).then_inc(S["a_kept"], 1)
                            act.wait_ge(S["e_product"], n + 1)
                            need(act, S["scattered"], n - 1)
                            nc.scalar.activation(msg[:, b].rearrange("p c d -> p (c d)"), pE[b][:, :], ACT.Relu).then_inc(S["msg_done"], 1)
                        over_groups(act, step)

                    @block.vector
                    def _(dve):
                        def add(n):
                            w = window(dve, n)
                            dve.wait_ge(S["scattered"], n + 1)
                            need(dve, S["added"], n)
                            nc.vector.tensor_tensor(node_sum[0:D, bass.ds(w, P)], node_sum[0:D, bass.ds(w, P)],
                                                    pG[0:D, 0:P], ALU.add).then_inc(S["added"], 1)

                        def step(i, r):
                            n = RING * i + r
                            need(dve, S["scattered"], n - 1)
                            one_hot(hot, i, r).then_inc(S["hot_done"], 1)
                            if not (isinstance(n, int) and n == 0):
                                add(n - 1)
                        over_groups(dve, step, lambda: add(G - 1))
                next_pass()

        with ExitStack() as ls:
            (s_v, s_turn, s_used, s_h, s_hused, s_part, s_total, s_var, s_std, s_out) = (sem(n, ls) for n in (
                "n3_v", "n3_turn", "n3_used", "n3_h", "n3_hused", "n3_part", "n3_total", "n3_var", "n3_std", "n3_out"))
            part = sb("n3_part_sb", [P, D], f32, ls)
            mean = sb("n3_mean", [P, D], f32, ls)
            var = sb("n3_var_sb", [P, D], f32, ls)
            std = sb("n3_std_sb", [P, D], f32, ls)
            y, z = rows[:, 0], rows[:, 1]
            by_feature = y.rearrange("p t d -> p d t")
            z_by_feature = z.rearrange("p t d -> p d t")
            with nc.Block() as block:
                @block.tensor
                def _(pe):
                    for j, t0 in enumerate(range(0, NT, 4)):
                        need(pe, s_used, j - 1)
                        for t in range(t0, min(t0 + 4, NT)):
                            last = nc.tensor.transpose(bank[j % 2][0:D, (t - t0) * P:(t - t0 + 1) * P], xn[:, t, :], ident[:, :])
                        last.then_inc(s_turn, 1)
                    pe.wait_ge(s_used, -(-NT // 4))
                    for j, t0 in enumerate(range(0, NT, 8)):
                        need(pe, s_hused, j - 1)
                        for t in range(t0, min(t0 + 8, NT)):
                            last = nc.tensor.matmul(bank[2 + j % 2][:, (t - t0) * D:(t - t0 + 1) * D], node_sum[0:D, t * P:(t + 1) * P],
                                                    Wgin[:, :], start=True, stop=True)
                        last.then_inc(s_h, 1)
                    pe.wait_ge(s_part, 1)
                    nc.tensor.matmul(bank[4][:, 0:D], ones[:, :], part[:, :], start=True, stop=True).then_inc(s_total, 1)
                    pe.wait_ge(s_part, 2)
                    nc.tensor.matmul(bank[5][:, 0:D], ones[:, :], part[:, :], start=True, stop=True).then_inc(s_total, 1)

                @block.scalar
                def _(act):
                    act.wait_ge(s_var, 1)
                    nc.scalar.sqrt(std[:, :], var[:, :]).then_inc(s_std, 1)
                    act.wait_ge(s_var, 2)
                    nc.scalar.sqrt(stat[:, 1, :], stat[:, 1, :]).then_inc(s_std, 1)

                @block.vector
                def _(dve):
                    chain = Chain(dve, s_v)
                    for j, t0 in enumerate(range(0, NT, 4)):
                        dve.wait_ge(s_turn, j + 1)
                        cols = slice(t0 * P, min(t0 + 4, NT) * P)
                        nc.vector.tensor_tensor(node_sum[0:D, cols], node_sum[0:D, cols], bank[j % 2][0:D, 0:cols.stop - cols.start],
                                                ALU.add).then_inc(s_used, 1)
                    for j, t0 in enumerate(range(0, NT, 8)):
                        dve.wait_ge(s_h, j + 1)
                        k = min(8, NT - t0)
                        nc.vector.tensor_tensor(y[:, t0:t0 + k, :], bank[2 + j % 2][:, 0:k * D].rearrange("p (t d) -> p t d", d=D),
                                                vec["b_gin"][:, :].unsqueeze(1).to_broadcast([P, k, D]), ALU.add).then_inc(s_hused, 1)
                    dve.wait_ge(s_hused, -(-NT // 8))
                    chain.then(nc.vector.tensor_scalar(y[:, NT - 1, :], y[:, NT - 1, :], real[:, 0:1], None, ALU.mult))
                    nc.vector.tensor_reduce(part[:, :], by_feature, AX, ALU.add).then_inc(s_part, 1)
                    dve.wait_ge(s_total, 1)
                    chain.then(nc.vector.tensor_scalar(mean[:, :], bank[4][:, 0:D], 1.0 / N, None, ALU.mult))
                    chain.then(nc.vector.tensor_tensor(y, y, over_tiles(mean[:, :]), ALU.subtract))
                    chain.then(nc.vector.tensor_tensor(z, y, y, ALU.mult))
                    chain.then(nc.vector.tensor_scalar(z[:, NT - 1, :], z[:, NT - 1, :], real[:, 0:1], None, ALU.mult))
                    nc.vector.tensor_reduce(part[:, :], z_by_feature, AX, ALU.add).then_inc(s_part, 1)
                    dve.wait_ge(s_total, 2)
                    nc.vector.tensor_scalar(var[:, :], bank[5][:, 0:D], 1.0 / N, EPS, ALU.mult, ALU.add).then_inc(s_var, 1)
                    dve.wait_ge(s_std, 1)
                    chain.then(nc.vector.reciprocal(std[:, :], std[:, :]))
                    chain.then(nc.vector.tensor_tensor(std[:, :], std[:, :], vec["gamma3"][:, :], ALU.mult))
                    chain.then(nc.vector.tensor_tensor(y, y, over_tiles(std[:, :]), ALU.mult))
                    chain.then(nc.vector.tensor_tensor(y, y, over_tiles(vec["beta3"][:, :]), ALU.add))
                    chain.then(nc.vector.scalar_tensor_tensor(out=y, in0=y, scalar=0.0, in1=xn[:, :, :], op0=ALU.max, op1=ALU.add))
                    layer_norm(dve, chain, y, s_var, s_std, 2)

            with nc.Block() as block:
                @block.sync
                def _(sp):
                    full = NT - 1
                    sp.dma_start(out[0:full * P, :].rearrange("(t p) d -> p t d", p=P), xn[:, 0:full, :]).then_inc(s_out, 16)
                    sp.dma_start(out[full * P:N, :], xn[0:LAST, full, :]).then_inc(s_out, 16)
                    sp.wait_ge(s_out, 32)


_FLOATS = ["edge_attr_16", "edge_attr_64", "L0_gnn_We2", "L0_gnn_be2", "L0_gnn_Wm2", "L0_gnn_bm2", "L0_gnn_eps2",
           "L0_gnn_gamma2", "L0_gnn_beta2", "L1_gnn_w_i", "L1_gnn_w_j", "L3_gnn_W_e", "L3_gnn_b_e", "L3_gnn_W_gin",
           "L3_gnn_b_gin", "L3_gnn_gamma", "L3_gnn_beta"]


def kernel(**inputs):
    import numpy as np
    import concourse.bacc as bacc
    from concourse.bass_utils import run_bass_kernel_spmd

    def padded(a, rows, fill):
        a = np.asarray(a)
        more = np.full((rows - a.shape[0],) + a.shape[1:], fill, a.dtype)
        return np.ascontiguousarray(np.concatenate([a, more]))

    arrays = {
        "x": padded(inputs["x"], NP, 0),
        "src": padded(inputs["src"], EP, N),
        "dst": padded(inputs["dst"], EP, N),
    }
    for name in _FLOATS:
        a = np.ascontiguousarray(np.asarray(inputs[name]))
        arrays[name] = padded(a, EP, 0) if name.startswith("edge") else a
    nc = bacc.Bacc("TRN2", target_bir_lowering=False, num_devices=1)
    args = [nc.dram_tensor("in_" + n, a.shape, mybir.dt.from_np(a.dtype), kind="ExternalInput").ap() for n, a in arrays.items()]
    out = nc.dram_tensor("out", (N, D), f32, kind="ExternalOutput").ap()
    build_program(nc, *args, out)
    r = run_bass_kernel_spmd(nc, [{"in_" + n: a for n, a in arrays.items()}], core_ids=[0])
    return r.results[0]["out"]
```

```python
import concourse.bass as bass
from concourse import mybir
from contextlib import ExitStack

f32 = mybir.dt.float32
bf16 = mybir.dt.bfloat16
i32 = mybir.dt.int32
ALU = mybir.AluOpType
ACT = mybir.ActivationFunctionType
AX = mybir.AxisListType.X

P = 128
W = 80
N = 6250
E = 200000
D = 64
D3 = 16
NT = -(-N // P)
NP = NT * P
LAST = N - (NT - 1) * P
C = 8
GE = C * P
RING = 4
G = -(-E // GE)
G += -G % RING
ROUNDS = G // RING
EP = G * GE
Q = G // 2
PASSES_MAX = -(-(N + 1) // W)
EPS = 1e-5
SLOPE = 0.01
ALPHA_TOTAL = 1.0 + 1.0 / 2.0 + 1.0 / 3.0
BANK = 512


def need(eng, sem, value):
    if isinstance(value, int) and value <= 0:
        return
    eng.wait_ge(sem, value)


def over_groups(eng, step, tail=None, begin=None):
    begin = begin or (lambda i: None)
    begin(0)
    for r in range(RING):
        step(0, r)
    with eng.Fori(1, ROUNDS) as i:
        begin(i)
        for r in range(RING):
            step(i, r)
    begin(ROUNDS)
    if tail is not None:
        tail()


class Chain:

    def __init__(self, eng, sem):
        self.eng, self.sem, self.count = eng, sem, 0

    def then(self, instruction):
        instruction.then_inc(self.sem, 1)
        self.count += 1
        self.eng.wait_ge(self.sem, self.count)


def build_program(nc, x, src, dst, edge16, edge64, We2, be2, Wm2, bm2, eps2, gamma2, beta2,
                  w_i, w_j, W_e, b_e, W_gin, b_gin, gamma3, beta3, out):
    with ExitStack() as ctx:
        def sb(name, shape, dt=f32, where=ctx):
            return where.enter_context(nc.sbuf_tensor(name, shape, dt))

        def sem(name, where=ctx):
            return where.enter_context(nc.semaphore(name))

        bank = [ctx.enter_context(nc.psum_tensor(f"bank{j}", [P, BANK], f32)) for j in range(6)]
        wide = ctx.enter_context(nc.psum_tensor("wide", [P, 2 * BANK], f32))

        table = [x] + [nc.dram_tensor(f"table{n}", (NP, D), f32, kind="Internal").ap() for n in (1, 2, 3)]
        si_row = nc.dram_tensor("si_row", (NP,), f32, kind="Internal").ap()

        ident = sb("ident", [P, P])
        ones = sb("ones", [P, P])
        iota0 = sb("iota0", [P, P])
        iota = sb("iota", [P, W])
        real = sb("real", [P, 1])
        dst_rel = sb("dst_rel", [P, G * C])
        src_lo = sb("src_lo", [P, G * C])
        src_hi = sb("src_hi", [P, G * C])
        start0 = sb("start0", [1, G])
        start_f = sb("start_f", [1, G])
        start_i = sb("start_i", [1, 2, G + 2 * RING], i32)
        passes = sb("passes", [1, 1], i32)
        node_sum = sb("node_sum", [D + 1, NP + W])
        xn = sb("xn", [P, NT, D])
        out_deg = sb("out_deg", [P, NT])
        rows = sb("rows", [P, 2, NT, D])
        stat = sb("stat", [P, 8, NT])

        WeBD = sb("WeBD", [P, P])
        WmBD = sb("WmBD", [P, P])
        W3BD = sb("W3BD", [P, C * D])
        Wgin = sb("Wgin", [D, D])
        be_col = sb("be_col", [P, 1])
        bm_row = sb("bm_row", [1, C * D])
        eps_col = sb("eps_col", [P, 1])
        vec = {n: sb(n + "_b", [P, D]) for n in ("gamma2", "beta2", "w_i", "w_j", "b_e", "b_gin", "gamma3", "beta3")}

        with ExitStack() as ps:
            dst_i = sb("dst_i", [Q, 2 * GE], i32, ps)
            src_i = sb("src_i", [Q, 2 * GE], i32, ps)
            lo_i = sb("lo_i", [Q, 2 * GE], i32, ps)
            byrow = [sb(f"byrow{j}", [Q, 2 * GE], f32, ps) for j in range(3)]
            iota_i = sb("iota_i", [P, P + 1], i32, ps)
            part = sb("part", [P, 1], f32, ps)
            low = sb("low", [Q, 2], f32, ps)
            high = sb("high", [Q, 2], f32, ps)
            diag = sb("diag", [Q, 2, Q], f32, ps)
            span = sb("span", [1, 2], f32, ps)
            steps = sb("steps", [1, P], f32, ps)
            s_idx, s_zero, s_w, s_iota, s_v = (sem(n, ps) for n in ("s_idx", "s_zero", "s_w", "s_iota", "s_v"))
            s_const, s_rows, s_turned, s_kept, s_ends, s_row1, s_diag, s_base = (
                sem(n, ps) for n in ("s_const", "s_rows", "s_turned", "s_kept", "s_ends", "s_row1", "s_diag", "s_base"))
            with nc.Block() as block:
                @block.sync
                def _(sp):
                    sp.dma_start(dst_i[:, :], dst.rearrange("(q e) -> q e", q=Q)).then_inc(s_idx, 16)
                    sp.dma_start(src_i[:, :], src.rearrange("(q e) -> q e", q=Q)).then_inc(s_idx, 16)
                    sp.dma_start(xn[:, :, :], x.rearrange("(t p) d -> p t d", p=P)).then_inc(s_w, 16)
                    given = {"gamma2": gamma2, "beta2": beta2, "w_i": w_i, "w_j": w_j, "b_e": b_e,
                             "b_gin": b_gin, "gamma3": gamma3, "beta3": beta3}
                    for name, v in given.items():
                        sp.dma_start(vec[name][:, :], v.partition_broadcast(P)).then_inc(s_w, 16)
                    sp.dma_start(eps_col[:, :], eps2.partition_broadcast(P)).then_inc(s_w, 16)
                    sp.dma_start(Wgin[:, :], W_gin).then_inc(s_w, 16)
                    for c in range(C):
                        sp.dma_start(bm_row[0:1, c * D:(c + 1) * D], bm2.unsqueeze(0)).then_inc(s_w, 16)
                    for h in range(2):
                        sp.dma_start(be_col[h * D:(h + 1) * D, :], be2.unsqueeze(1)).then_inc(s_w, 16)
                    sp.wait_ge(s_zero, 4)
                    for h in range(2):
                        at = slice(h * D, (h + 1) * D)
                        sp.dma_start(WeBD[at, at], We2).then_inc(s_w, 16)
                        sp.dma_start(WmBD[at, at], Wm2).then_inc(s_w, 16)
                    for c in range(C):
                        sp.dma_start(W3BD[c * D3:(c + 1) * D3, c * D:(c + 1) * D], W_e).then_inc(s_w, 16)
                    sp.wait_ge(s_w, 16 * (1 + 8 + 2 + C + 2 + 4 + C))

                @block.gpsimd
                def _(pool):
                    nc.gpsimd.memset(WeBD[:, :], 0.0).then_inc(s_zero, 1)
                    nc.gpsimd.memset(WmBD[:, :], 0.0).then_inc(s_zero, 1)
                    nc.gpsimd.memset(W3BD[:, :], 0.0).then_inc(s_zero, 1)
                    nc.gpsimd.memset(ones[:, :], 1.0).then_inc(s_zero, 1)
                    nc.gpsimd.iota(iota_i[:, 0:P], [[1, P]], base=0, channel_multiplier=0).then_inc(s_iota, 1)
                    nc.gpsimd.iota(iota_i[:, P:P + 1], [[0, 1]], base=0, channel_multiplier=1).then_inc(s_iota, 1)

                @block.vector
                def _(dve):
                    chain = Chain(dve, s_v)
                    dve.wait_ge(s_iota, 2)
                    nc.vector.tensor_copy(iota0[:, :], iota_i[:, 0:P])
                    chain.then(nc.vector.tensor_copy(part[:, :], iota_i[:, P:P + 1]))
                    nc.vector.tensor_scalar(real[:, :], part[:, :], float(LAST), None, ALU.is_lt)
                    nc.vector.tensor_scalar(ident[:, :], iota0[:, :], part[:, 0:1], None, ALU.is_equal).then_inc(s_const, 1)
                    dve.wait_ge(s_idx, 32)
                    nc.vector.tensor_copy(byrow[0][:, :], dst_i[:, :])
                    chain.then(nc.vector.tensor_scalar(lo_i[:, :], src_i[:, :], P - 1, None, ALU.bitwise_and))
                    chain.then(nc.vector.tensor_copy(byrow[1][:, :], lo_i[:, :]))
                    chain.then(nc.vector.tensor_scalar(lo_i[:, :], src_i[:, :], 7, None, ALU.arith_shift_right))
                    nc.vector.tensor_copy(byrow[2][:, :], lo_i[:, :]).then_inc(s_rows, 1)
                    two = byrow[0][:, :].rearrange("q (b e) -> q b e", b=2)
                    nc.vector.tensor_reduce(low[:, :], two, AX, ALU.min)
                    chain.then(nc.vector.tensor_reduce(high[:, :], two, AX, ALU.max))
                    chain.then(nc.vector.tensor_tensor(high[:, :], high[:, :], low[:, :], ALU.subtract))
                    for b in range(2):
                        last = nc.vector.tensor_scalar(diag[:, b, :], ident[0:Q, 0:Q], low[:, b:b + 1], None, ALU.mult)
                    last.then_inc(s_ends, 1)
                    dve.wait_ge(s_row1, 1)
                    chain.then(nc.vector.tensor_copy(start0[0:1, :].rearrange("o (q b) -> o b q", b=2),
                                                     bank[4][0:1, 0:2 * P].rearrange("o (b q) -> o b q", b=2)[:, :, 0:Q]))
                    chain.then(nc.vector.tensor_reduce(span[0:1, 0:1], bank[4][0:1, 2 * P:4 * P].rearrange("o (b q) -> o b q", b=2)[:, :, 0:Q],
                                                       mybir.AxisListType.XY, ALU.max))
                    chain.then(nc.vector.tensor_scalar(steps[0:1, :], iota0[0:1, :], float(W), span[0:1, 0:1], ALU.mult, ALU.is_le))
                    chain.then(nc.vector.tensor_reduce(span[0:1, 1:2], steps[0:1, :], AX, ALU.add))
                    chain.then(nc.vector.tensor_copy(passes[0:1, :], span[0:1, 1:2]))
                    for j, kept in enumerate((dst_rel, src_lo, src_hi)):
                        to = kept[:, :].rearrange("p (q b c) -> p b c q", b=2, c=C)
                        for b in range(2):
                            for h in range(2):
                                n = (j * 2 + b) * 2 + h
                                dve.wait_ge(s_turned, n + 1)
                                ps_view = bank[n % 2][:, :].rearrange("p (c q) -> p c q", c=4)[:, :, 0:Q]
                                nc.vector.tensor_copy(to[:, b, 4 * h:4 * h + 4, :], ps_view).then_inc(s_kept, 1)
                    dve.wait_ge(s_base, 1)
                    dve.wait_ge(s_kept, 12)
                    for b in range(2):
                        view = dst_rel[:, :].rearrange("p (q b c) -> p b q c", b=2, c=C)[:, b]
                        base = bank[5][:, b * P:b * P + Q].unsqueeze(2).to_broadcast([P, Q, C])
                        chain.then(nc.vector.tensor_tensor(view, view, base, ALU.subtract))

                @block.tensor
                def _(pe):
                    pe.wait_ge(s_const, 1)
                    pe.wait_ge(s_rows, 1)
                    pe.wait_ge(s_ends, 1)
                    pe.wait_ge(s_zero, 4)
                    for b in range(2):
                        nc.tensor.matmul(bank[4][0:1, b * P:b * P + Q], low[:, b:b + 1], ident[0:Q, 0:Q], start=True, stop=True)
                    for b in range(2):
                        last = nc.tensor.matmul(bank[4][0:1, (2 + b) * P:(2 + b) * P + Q], high[:, b:b + 1], ident[0:Q, 0:Q], start=True, stop=True)
                    last.then_inc(s_row1, 1)
                    for b in range(2):
                        last = nc.tensor.matmul(bank[5][:, b * P:b * P + Q], ones[0:Q, :], diag[:, b, :], start=True, stop=True)
                    last.then_inc(s_base, 1)
                    for j in range(3):
                        for b in range(2):
                            from_ = byrow[j][:, b * GE:(b + 1) * GE].rearrange("q (p c) -> q c p", c=C)
                            for h in range(2):
                                n = (j * 2 + b) * 2 + h
                                need(pe, s_kept, n - 1)
                                for c in range(4):
                                    last = nc.tensor.transpose(bank[n % 2][:, c * P:c * P + Q], from_[:, 4 * h + c, :], ident[0:Q, 0:Q])
                                last.then_inc(s_turned, 1)

        npasses = nc.values_load(passes[0:1, 0:1], min_val=1, max_val=PASSES_MAX)

        S = {n: sem(n) for n in (
            "attr_in", "idx_in", "gathered",
            "x_turned", "a_turned", "a_kept", "e_product", "e_done", "summed", "m_done", "m_product", "msg_done",
            "hot_done", "scattered", "added",
            "hist_done", "moved", "may_gather",
            "v_a", "v_b", "scaled", "keys_done", "masked", "keys_turned", "hot_turned", "hot_kept", "max_found",
            "diag_done", "max_spread", "factor_in", "factor_done", "cols_done", "looked_up", "exp_in", "exp_done", "rows_kept",
        )}
        ring_sems = {n: [sem(f"{n}{r}") for r in range(RING)] for n in ("attr_in", "idx_in", "gathered")}

        LAGS = (1, 3)

        def set_starts(start):
            for k, lag in enumerate(LAGS):
                nc.vector.tensor_copy(start_i[0:1, k, lag:lag + G], start[0:1, :])

        starts_zero = sem("starts_zero")

        def zero_state(layer):
            with nc.Block() as block:
                @block.vector
                def _(dve):
                    nc.vector.memset(node_sum[:, :], 0.0)
                    if layer == 0:
                        nc.vector.memset(start_i[0:1, :, :], 0).then_inc(starts_zero, 1)
                        dve.wait_ge(starts_zero, 1)
                    nc.vector.tensor_copy(iota[:, :], iota0[:, 0:W])
                    nc.vector.tensor_copy(start_f[0:1, :], start0[0:1, :])
                    set_starts(start0)

        def next_pass():
            with nc.Block() as block:
                @block.vector
                def _(dve):
                    chain = Chain(dve, S["moved"])
                    nc.vector.tensor_scalar(iota[:, :], iota[:, :], float(W), None, ALU.add)
                    chain.then(nc.vector.tensor_scalar(start_f[0:1, :], start_f[0:1, :], float(W), float(NP), ALU.add, ALU.min))
                    set_starts(start_f)
            with nc.Block() as block:
                @block.sync
                def _(sp):
                    for s in S.values():
                        sp.sem_clear(s)
                    for name in ("attr_in", "idx_in"):
                        for s in ring_sems[name]:
                            sp.sem_clear(s)

                @block.gpsimd
                def _(pool):
                    for s in ring_sems["gathered"]:
                        pool.wait_ge(s, 16 * C * ROUNDS)
                    pool.dma_reset()
                    for s in ring_sems["gathered"]:
                        pool.sem_clear(s)

        def edge_loads(xg, idx, attr, attr_dram, width):
            idx_view = src.rearrange("(i r p c) -> i r p c", r=RING, p=P, c=C)
            attr_view = None if attr is None else attr_dram.rearrange("(i r p c) d -> i r p (c d)", r=RING, p=P, c=C)

            def program(sp, attr_used):
                def step(i, r):
                    need(sp, ring_sems["gathered"][r], 16 * C * i)
                    sp.dma_start(idx[:, r, :], idx_view[i, r]).then_inc(ring_sems["idx_in"][r], 16)
                    if attr is not None:
                        need(sp, attr_used, RING * i + r - (RING - 1))
                        sp.dma_start(attr[:, r, :], attr_view[i, r]).then_inc(ring_sems["attr_in"][r], 16)
                over_groups(sp, step)
            return program

        def gathers(layer, xg, idx):
            def program(pool, rows_used):
                def step(i, r):
                    pool.wait_ge(ring_sems["idx_in"][r], 16 * (i + 1))
                    need(pool, rows_used, RING * i + r - (RING - 1))
                    pool.sem_inc(S["may_gather"], 1)
                    for c in range(C):
                        nc.gpsimd.indirect_dma_start(xg[:, r, c, 0:D], None, table[layer][:, :],
                                                     bass.IndirectOffsetOnAxis(ap=idx[:, r, c:c + 1], axis=0),
                                                     ).then_inc(ring_sems["gathered"][r], 16)
                over_groups(pool, step)
            return program

        def one_hot(hot, i, r, ring=2):
            n = RING * i + r
            col = dst_rel[:, bass.ds(n * C, C)] if not isinstance(n, int) else dst_rel[:, n * C:(n + 1) * C]
            return nc.vector.tensor_tensor(hot[:, r % ring], iota[:, :].unsqueeze(1).to_broadcast([P, C, W]),
                                           col.unsqueeze(2).to_broadcast([P, C, W]), ALU.is_equal)

        class Windows:

            def __init__(self, lag):
                self.lag, self.count = lag, RING if lag == 1 else RING + 1

            def load(self, i):
                at = RING * i
                cols = slice(at, at + self.count) if isinstance(at, int) else bass.ds(at, self.count)
                self.held = nc.values_load_multi_w_load_instructions(
                    start_i[0:1, LAGS.index(self.lag), cols], engines=(mybir.EngineType.DVE,), min_val=0, max_val=NP)[1]

            def of(self, r, lag):
                return bass.ds(self.held[r - lag + self.lag], W)

        with ExitStack() as ls:
            xg = sb("xg", [P, RING, C, D], f32, ls)
            idx = sb("idx", [P, RING, C], i32, ls)
            attr = sb("attr", [P, RING, C * D], f32, ls)
            attrT = sb("attrT", [P, 4 * P], f32, ls)
            eaT = sb("eaT", [P, 4 * P], f32, ls)
            sumT = sb("sumT", [P, 4 * P], f32, ls)
            mT = sb("mT", [P, 2, 4 * P], f32, ls)
            msg = sb("msg", [P, 2, C, D], f32, ls)
            hot = sb("hot", [P, 2, C, W], f32, ls)
            lo_hot = sb("lo_hot", [P, 2, C, P], bf16, ls)
            hi_hot = sb("hi_hot", [P, 2, C, NT], bf16, ls)
            pA, pE, pM, pG = bank[0], bank[1], bank[2], bank[3]
            pX = [bank[4], bank[5]]
            pH = wide
            zero_state(0)
            with nc.Fori(0, npasses):
                with nc.Block() as block:
                    load = edge_loads(xg, idx, attr, edge64, C * D)
                    gather = gathers(0, xg, idx)

                    @block.sync
                    def _(sp):
                        load(sp, S["a_turned"])

                    @block.gpsimd
                    def _(pool):
                        gather(pool, S["x_turned"])

                    @block.tensor
                    def _(pe):
                        def message(n, b):
                            pe.wait_ge(S["m_done"], n + 1)
                            need(pe, S["msg_done"], n)
                            nc.tensor.matmul(pM[:, :], ones[0:1, :], bm_row[0:1, :], start=True, stop=False)
                            for j in range(4):
                                last = nc.tensor.matmul(pM[:, j * P:(j + 1) * P], mT[:, b, j * P:(j + 1) * P], WmBD[:, :],
                                                        start=False, stop=(j == 3))
                            last.then_inc(S["m_product"], 1)

                        def scatter(n, b):
                            pe.wait_ge(S["msg_done"], n + 1)
                            pe.wait_ge(S["hot_done"], n + 1)
                            need(pe, S["added"], n)
                            for c in range(C):
                                last = nc.tensor.matmul(pG[0:D, 0:W], msg[:, b, c, :], hot[:, b, c, :], start=(c == 0), stop=(c == C - 1))
                            last.then_inc(S["scattered"], 1)

                        def step(i, r):
                            n, b = RING * i + r, r % 2
                            first = isinstance(n, int) and n == 0
                            pe.wait_ge(ring_sems["attr_in"][r], 16 * (i + 1))
                            need(pe, S["a_kept"], n)
                            for j in range(4):
                                last = nc.tensor.transpose(pA[:, j * P:(j + 1) * P], attr[:, r, j * P:(j + 1) * P], ident[:, :])
                            last.then_inc(S["a_turned"], 1)
                            pe.wait_ge(ring_sems["gathered"][r], 16 * C * (i + 1))
                            need(pe, S["m_done"], n - 1)
                            for j in range(4):
                                last = nc.tensor.transpose(pX[b][:, j * P:(j + 1) * P],
                                                           xg[:, r, 2 * j:2 * j + 2, :].rearrange("p c d -> p (c d)"), ident[:, :])
                            last.then_inc(S["x_turned"], 1)
                            if not first:
                                message(n - 1, 1 - b)
                            pe.wait_ge(S["a_kept"], n + 1)
                            need(pe, S["e_done"], n)
                            nc.tensor.matmul(pE[:, :], WeBD[:, :], attrT[:, :], start=True, stop=True).then_inc(S["e_product"], 1)
                            pe.wait_ge(S["keys_done"], n + 1)
                            for c in range(C):
                                last = nc.tensor.matmul(pH[:, 0:NT], lo_hot[:, b, c, :], hi_hot[:, b, c, :],
                                                        start=(first and c == 0), stop=False, skip_group_check=True)
                            last.then_inc(S["hist_done"], 1)
                            if not first:
                                scatter(n - 1, 1 - b)

                        def tail():
                            message(G - 1, 1)
                            scatter(G - 1, 1)
                        over_groups(pe, step, tail)

                    @block.scalar
                    def _(act):
                        def messages(n, b):
                            act.wait_ge(S["m_product"], n + 1)
                            need(act, S["scattered"], n - 1)
                            nc.scalar.activation(msg[:, b].rearrange("p c d -> p (c d)"), pM[:, :], ACT.Silu).then_inc(S["msg_done"], 1)

                        def step(i, r):
                            n, b = RING * i + r, r % 2
                            act.wait_ge(S["a_turned"], n + 1)
                            need(act, S["e_product"], n)
                            nc.scalar.copy(attrT[:, :], pA[:, :]).then_inc(S["a_kept"], 1)
                            if not (isinstance(n, int) and n == 0):
                                messages(n - 1, 1 - b)
                            act.wait_ge(S["e_product"], n + 1)
                            need(act, S["summed"], n)
                            nc.scalar.activation(eaT[:, :], pE[:, :], ACT.Silu, bias=be_col[:, 0:1]).then_inc(S["e_done"], 1)
                        over_groups(act, step, lambda: messages(G - 1, 1))

                    @block.vector
                    def _(dve):
                        windows = Windows(1)

                        def add(n, r):
                            at = windows.of(r, 1)
                            dve.wait_ge(S["scattered"], n + 1)
                            need(dve, S["added"], n)
                            nc.vector.tensor_tensor(node_sum[0:D, at], node_sum[0:D, at], pG[0:D, 0:W], ALU.add).then_inc(S["added"], 1)

                        def step(i, r):
                            n, b = RING * i + r, r % 2
                            cols = bass.ds(n * C, C) if not isinstance(n, int) else slice(n * C, (n + 1) * C)
                            need(dve, S["scattered"], n - 1)
                            one_hot(hot, i, r).then_inc(S["hot_done"], 1)
                            need(dve, S["hist_done"], n - 1)
                            nc.vector.tensor_tensor(lo_hot[:, b], iota0[:, :].unsqueeze(1).to_broadcast([P, C, P]),
                                                    src_lo[:, cols].unsqueeze(2).to_broadcast([P, C, P]), ALU.is_equal)
                            nc.vector.tensor_tensor(hi_hot[:, b], iota0[:, 0:NT].unsqueeze(1).to_broadcast([P, C, NT]),
                                                    src_hi[:, cols].unsqueeze(2).to_broadcast([P, C, NT]), ALU.is_equal).then_inc(S["keys_done"], 1)
                            if not (isinstance(n, int) and n == 0):
                                add(n - 1, r)
                            dve.wait_ge(S["x_turned"], n + 1)
                            dve.wait_ge(S["e_done"], n + 1)
                            need(dve, S["m_done"], n)
                            nc.vector.tensor_tensor(sumT[:, :], pX[b][:, :], eaT[:, :], ALU.add).then_inc(S["summed"], 1)
                            dve.wait_ge(S["summed"], n + 1)
                            need(dve, S["m_product"], n - 1)
                            nc.vector.tensor_scalar(mT[:, b, :], sumT[:, :], 0.0, None, ALU.max).then_inc(S["m_done"], 1)
                        over_groups(dve, step, lambda: add(G - 1, 0), windows.load)
                next_pass()

        def transposes(pe, features, per, s_turn, s_used):
            for j, t0 in enumerate(range(0, NT, per)):
                need(pe, s_used, j - 1)
                for t in range(t0, min(t0 + per, NT)):
                    last = nc.tensor.transpose(bank[j % 2][:, (t - t0) * features:(t - t0 + 1) * features],
                                               node_sum[0:features, t * P:(t + 1) * P], ident[0:features, 0:features])
                last.then_inc(s_turn, 1)

        def read_tiles(dve, features, per, s_turn, s_used, use):
            for j, t0 in enumerate(range(0, NT, per)):
                dve.wait_ge(s_turn, j + 1)
                k = min(per, NT - t0)
                view = bank[j % 2][:, 0:k * features].rearrange("p (t f) -> p t f", f=features)
                use(t0, t0 + k, view).then_inc(s_used, 1)

        def over_tiles(v, free=D):
            return v.unsqueeze(1).to_broadcast([P, NT, free])

        def over_features(v):
            return v.unsqueeze(2).to_broadcast([P, NT, D])

        def layer_norm(dve, chain, y, s_var, s_std, turn):
            mean, var = stat[:, 0, :], stat[:, 1, :]
            chain.then(nc.vector.tensor_reduce(mean, y, AX, ALU.add))
            chain.then(nc.vector.tensor_scalar(mean, mean, 1.0 / D, None, ALU.mult))
            chain.then(nc.vector.tensor_tensor(y, y, over_features(mean), ALU.subtract))
            chain.then(nc.vector.tensor_tensor(rows[:, 1], y, y, ALU.mult))
            chain.then(nc.vector.tensor_reduce(var, rows[:, 1], AX, ALU.add))
            nc.vector.tensor_scalar(var, var, 1.0 / D, EPS, ALU.mult, ALU.add).then_inc(s_var, 1)
            dve.wait_ge(s_std, turn)
            chain.then(nc.vector.reciprocal(var, var))
            chain.then(nc.vector.tensor_tensor(xn[:, :, :], y, over_features(var), ALU.mult))

        with ExitStack() as ls:
            names = ("s_v", "s_turn", "s_used", "s_part", "s_total", "s_var", "s_std", "s_table", "s_si", "s_siT", "s_siK",
                     "s_least", "s_leastT", "s_leastR", "s_leastB", "s_row")
            (s_v, s_turn, s_used, s_part, s_total, s_var, s_std, s_table, s_si, s_siT, s_siK,
             s_least, s_leastT, s_leastR, s_leastB, s_row) = (sem(n, ls) for n in names)
            max_row = sb("max_row", [P, NP + W], f32, ls)
            si_all = sb("si_all", [P, NP + W], f32, ls)
            least = sb("least", [P, 1], f32, ls)
            least_row = sb("least_row", [1, P + 1], f32, ls)
            parts = sb("parts", [P, 2], f32, ls)
            tot = sb("tot", [P, 8], f32, ls)
            eps1 = sb("eps1", [P, 1], f32, ls)
            si_tiles = sb("si_tiles", [NT, P], f32, ls)
            y = rows[:, 0]
            with nc.Block() as block:
                @block.tensor
                def _(pe):
                    transposes(pe, D, 8, s_turn, s_used)
                    pe.wait_ge(s_part, 1)
                    nc.tensor.matmul(bank[2][:, 0:2], ones[:, :], parts[:, :], start=True, stop=True).then_inc(s_total, 1)
                    pe.wait_ge(s_least, 1)
                    nc.tensor.transpose(bank[3][0:1, 0:P], least[:, :], ident[:, :]).then_inc(s_leastT, 1)
                    pe.wait_ge(s_leastR, 1)
                    nc.tensor.matmul(bank[4][:, 0:1], ones[0:1, :], least_row[0:1, P:P + 1], start=True, stop=True).then_inc(s_leastB, 1)
                    pe.wait_ge(s_si, 1)
                    nc.tensor.transpose(bank[5][0:NT, 0:P], stat[:, 2, :], ident[:, :]).then_inc(s_siT, 1)

                @block.scalar
                def _(act):
                    act.wait_ge(s_var, 1)
                    nc.scalar.sqrt(tot[:, 4:5], tot[:, 3:4]).then_inc(s_std, 1)
                    act.wait_ge(s_var, 2)
                    nc.scalar.sqrt(stat[:, 1, :], stat[:, 1, :]).then_inc(s_std, 1)

                @block.sync
                def _(sp):
                    sp.wait_ge(s_table, 1)
                    sp.dma_start(table[1].rearrange("(t p) d -> p t d", p=P), xn[:, :, :]).then_inc(s_row, 16)
                    sp.wait_ge(s_siK, 1)
                    sp.wait_ge(s_row, 16)
                    sp.dma_start(si_row.rearrange("(t p) -> t p", p=P), si_tiles[:, :]).then_inc(s_row, 16)
                    sp.wait_ge(s_row, 32)
                    sp.dma_start(si_all[:, 0:NP], si_row.partition_broadcast(P)).then_inc(s_row, 16)
                    sp.wait_ge(s_row, 48)

                @block.vector
                def _(dve):
                    chain = Chain(dve, s_v)
                    nc.vector.tensor_copy(out_deg[:, :], pH[:, 0:NT])
                    nc.vector.memset(max_row[:, :], 0.0)
                    nc.vector.memset(si_all[:, NP:NP + W], 0.0)
                    chain.then(nc.vector.tensor_scalar(eps1[:, :], eps_col[:, :], 1.0, None, ALU.add))
                    read_tiles(dve, D, 8, s_turn, s_used, lambda a, z, v: nc.vector.scalar_tensor_tensor(
                        out=y[:, a:z, :], in0=xn[:, a:z, :], scalar=eps1[:, 0:1], in1=v, op0=ALU.mult, op1=ALU.add))
                    dve.wait_ge(s_used, -(-NT // 8))
                    chain.then(nc.vector.tensor_scalar(y[:, NT - 1, :], y[:, NT - 1, :], real[:, 0:1], None, ALU.mult))
                    flat = y.rearrange("p t d -> p (t d)")
                    square = rows[:, 1].rearrange("p t d -> p (t d)")
                    nc.vector.tensor_reduce(parts[:, 0:1], flat, AX, ALU.add)
                    chain.then(nc.vector.tensor_tensor(square, flat, flat, ALU.mult))
                    nc.vector.tensor_reduce(parts[:, 1:2], square, AX, ALU.add).then_inc(s_part, 1)
                    dve.wait_ge(s_total, 1)
                    chain.then(nc.vector.tensor_scalar(tot[:, 0:2], bank[2][:, 0:2], 1.0 / (N * D), None, ALU.mult))
                    chain.then(nc.vector.tensor_tensor(tot[:, 2:3], tot[:, 0:1], tot[:, 0:1], ALU.mult))
                    chain.then(nc.vector.tensor_tensor(tot[:, 3:4], tot[:, 1:2], tot[:, 2:3], ALU.subtract))
                    nc.vector.tensor_scalar(tot[:, 3:4], tot[:, 3:4], EPS, None, ALU.add).then_inc(s_var, 1)
                    dve.wait_ge(s_std, 1)
                    chain.then(nc.vector.reciprocal(tot[:, 5:6], tot[:, 4:5]))
                    chain.then(nc.vector.tensor_scalar(flat, flat, tot[:, 0:1], tot[:, 5:6], ALU.subtract, ALU.mult))
                    chain.then(nc.vector.tensor_tensor(y, y, over_tiles(vec["gamma2"][:, :]), ALU.mult))
                    chain.then(nc.vector.tensor_tensor(y, y, over_tiles(vec["beta2"][:, :]), ALU.add))
                    chain.then(nc.vector.tensor_tensor(y, y, xn[:, :, :], ALU.add))
                    chain.then(nc.vector.scalar_tensor_tensor(out=y, in0=y, scalar=0.0, in1=xn[:, :, :], op0=ALU.max, op1=ALU.add))
                    layer_norm(dve, chain, y, s_var, s_std, 2)
                    nc.vector.tensor_copy(tot[:, 6:7], tot[:, 5:6]).then_inc(s_table, 1)
                    chain.then(nc.vector.tensor_tensor(y, xn[:, :, :], over_tiles(vec["w_j"][:, :]), ALU.mult))
                    chain.then(nc.vector.tensor_reduce(stat[:, 2, :], y, AX, ALU.add))
                    nc.vector.tensor_reduce(least[:, :], stat[:, 2, :], AX, ALU.min).then_inc(s_least, 1)
                    dve.wait_ge(s_leastT, 1)
                    nc.vector.tensor_reduce(least_row[0:1, P:P + 1], bank[3][0:1, 0:P], AX, ALU.min).then_inc(s_leastR, 1)
                    chain.then(nc.vector.tensor_tensor(y, xn[:, :, :], over_tiles(vec["w_i"][:, :]), ALU.mult))
                    chain.then(nc.vector.tensor_reduce(stat[:, 2, :], y, AX, ALU.add))
                    dve.wait_ge(s_leastB, 1)
                    chain.then(nc.vector.tensor_copy(least[:, :], bank[4][:, 0:1]))
                    nc.vector.tensor_scalar(stat[:, 2, :], stat[:, 2, :], least[:, 0:1], None, ALU.add).then_inc(s_si, 1)
                    dve.wait_ge(s_siT, 1)
                    nc.vector.tensor_copy(si_tiles[:, :], bank[5][0:NT, 0:P]).then_inc(s_siK, 1)

            xg = sb("xg1", [P, RING, C, D], f32, ls)
            idx = sb("idx1", [P, RING, C], i32, ls)
            hot = sb("hot1", [P, RING, C, W], f32, ls)
            kept = sb("kept", [P, RING, C, D], f32, ls)
            prod = sb("prod", [P, C, D], f32, ls)
            sj = sb("sj", [P, C], f32, ls)
            key = sb("key", [P, RING, C], f32, ls)
            mask = sb("mask", [P, C, W], f32, ls)
            hotT = sb("hotT", [W, 2, C * P], f32, ls)
            tops = sb("tops", [W, 2], f32, ls)
            top = sb("top", [W, 1], f32, ls)
            topD = sb("topD", [W, W], f32, ls)
            sc = sb("sc", [P, 2, W], f32, ls)
            leaky = sb("leaky", [P, 2, W], f32, ls)
            drop = sb("drop", [D + 1, W], f32, ls)
            fac = sb("fac", [D + 1, W], f32, ls)
            picked = sb("picked", [W, 2, W], f32, ls)
            cols2 = sb("cols2", [W, 2], f32, ls)
            ea = sb("ea", [P, C], f32, ls)
            eb = sb("eb", [P, C], f32, ls)
            ec = sb("ec", [P, C], f32, ls)
            ex = sb("ex", [P, C], f32, ls)
            msg = sb("msg1", [P, 2, C, D + 1], f32, ls)
            pO = wide
            pK = [bank[0], bank[1]]
            pR, pL, pG = bank[2], bank[3], bank[4]
            zero_state(1)
            with nc.Fori(0, npasses):
                with nc.Block() as block:
                    load = edge_loads(xg, idx, None, None, 0)
                    gather = gathers(1, xg, idx)

                    @block.sync
                    def _(sp):
                        load(sp, None)

                    @block.gpsimd
                    def _(pool):
                        gather(pool, S["rows_kept"])

                    def reached(n, lag):
                        return not (isinstance(n, int) and n < lag)

                    @block.tensor
                    def _(pe):
                        def look_up(n, b):
                            pe.wait_ge(S["cols_done"], n + 1)
                            pe.wait_ge(S["hot_kept"], n + 1)
                            need(pe, S["exp_in"], n)
                            for c in range(C):
                                last = nc.tensor.matmul(pL[:, 2 * c:2 * c + 2], hotT[:, b, c * P:(c + 1) * P], cols2[:, :], start=True, stop=True)
                            last.then_inc(S["looked_up"], 1)

                        def turn_keys(n):
                            pe.wait_ge(S["masked"], n + 1)
                            need(pe, S["max_found"], n)
                            for c in range(C):
                                last = nc.tensor.transpose(pK[c // 4][0:W, (c % 4) * P:(c % 4 + 1) * P], mask[:, c, :], ident[:, :])
                            last.then_inc(S["keys_turned"], 1)

                        def scatter(n, r):
                            pe.wait_ge(S["msg_done"], n + 1)
                            need(pe, S["added"], n)
                            for c in range(C):
                                last = nc.tensor.matmul(pG[0:D + 1, 0:W], msg[:, r % 2, c, :], hot[:, r, c, :], start=(c == 0), stop=(c == C - 1))
                            last.then_inc(S["scattered"], 1)

                        def spread_max(n):
                            pe.wait_ge(S["diag_done"], n + 1)
                            need(pe, S["v_b"], n)
                            nc.tensor.matmul(pR[:, 0:W], ones[0:W, :], topD[:, :], start=True, stop=True).then_inc(S["max_spread"], 1)

                        def step(i, r):
                            n = RING * i + r
                            if reached(n, 1):
                                turn_keys(n - 1)
                            pe.wait_ge(S["hot_done"], n + 1)
                            need(pe, S["hot_kept"], n)
                            for c in range(C):
                                last = nc.tensor.transpose(pO[0:W, c * P:(c + 1) * P], hot[:, r, c, :], ident[:, :])
                            last.then_inc(S["hot_turned"], 1)
                            if reached(n, 2):
                                look_up(n - 2, r % 2)
                            if reached(n, 1):
                                spread_max(n - 1)
                            if reached(n, 2):
                                scatter(n - 2, (r - 2) % RING)

                        def tail():
                            turn_keys(G - 1)
                            look_up(G - 2, 0)
                            spread_max(G - 1)
                            scatter(G - 2, (G - 2) % RING)
                            look_up(G - 1, 1)
                            scatter(G - 1, (G - 1) % RING)
                        over_groups(pe, step, tail)

                    @block.scalar
                    def _(act):
                        def exps(n):
                            act.wait_ge(S["factor_in"], n + 1)
                            need(act, S["scaled"], n)
                            nc.scalar.activation(fac[:, :], drop[:, :], ACT.Exp).then_inc(S["factor_done"], 1)
                            act.wait_ge(S["exp_in"], n + 1)
                            need(act, S["msg_done"], n)
                            nc.scalar.activation(ex[:, :], ec[:, :], ACT.Exp).then_inc(S["exp_done"], 1)

                        def keep_rows(i, r):
                            n = RING * i + r
                            act.wait_ge(ring_sems["gathered"][r], 16 * C * (i + 1))
                            need(act, S["msg_done"], n - 3)
                            nc.scalar.copy(kept[:, r].rearrange("p c d -> p (c d)"), xg[:, r].rearrange("p c d -> p (c d)")).then_inc(S["rows_kept"], 1)

                        def step(i, r):
                            n = RING * i + r
                            keep_rows(i, r)
                            if reached(n, 2):
                                exps(n - 2)
                            act.wait_ge(S["hot_done"], n + 1)
                            act.wait_ge(S["keys_done"], n + 1)
                            need(act, S["keys_turned"], n)
                            for c in range(C):
                                last = nc.scalar.activation(mask[:, c, :], hot[:, r, c, :], ACT.Copy, scale=key[:, r, c:c + 1])
                            last.then_inc(S["masked"], 1)
                            act.wait_ge(S["hot_turned"], n + 1)
                            need(act, S["looked_up"], n - 1)
                            for h in range(2):
                                last = nc.scalar.copy(hotT[:, r % 2, h * BANK:(h + 1) * BANK], pO[0:W, h * BANK:(h + 1) * BANK])
                            last.then_inc(S["hot_kept"], 1)

                        def tail():
                            exps(G - 2)
                            exps(G - 1)
                        over_groups(act, step, tail)

                    @block.vector
                    def _(dve):
                        windows = Windows(3)

                        def scores(n, at):
                            k = 6 * n
                            dve.wait_ge(S["max_spread"], n + 1)
                            nc.vector.tensor_tensor(sc[:, 0, :], max_row[:, at], si_all[:, at], ALU.add).then_inc(S["v_a"], 1)
                            nc.vector.tensor_tensor(picked[:, 0, :], si_all[0:W, at], ident[0:W, 0:W], ALU.mult)
                            dve.wait_ge(S["v_a"], k + 1)
                            nc.vector.tensor_tensor(max_row[:, at], max_row[:, at], pR[:, 0:W], ALU.max).then_inc(S["v_b"], 1)
                            dve.wait_ge(S["v_b"], n + 1)
                            nc.vector.tensor_tensor(sc[:, 1, :], max_row[:, at], si_all[:, at], ALU.add).then_inc(S["v_a"], 1)
                            dve.wait_ge(S["v_a"], k + 2)
                            two = sc[:, :, :]
                            nc.vector.scalar_tensor_tensor(out=leaky[:, :, :], in0=two, scalar=SLOPE, in1=two,
                                                           op0=ALU.mult, op1=ALU.max).then_inc(S["v_a"], 1)
                            dve.wait_ge(S["v_a"], k + 3)
                            nc.vector.tensor_tensor(picked[:, 1, :], leaky[0:W, 1, :], ident[0:W, 0:W], ALU.mult).then_inc(S["v_a"], 1)
                            need(dve, S["factor_done"], n)
                            nc.vector.tensor_tensor(drop[:, :], leaky[0:D + 1, 0, :], leaky[0:D + 1, 1, :], ALU.subtract).then_inc(S["factor_in"], 1)
                            dve.wait_ge(S["v_a"], k + 4)
                            need(dve, S["looked_up"], n)
                            nc.vector.tensor_reduce(cols2[:, :], picked[:, :, :], AX, ALU.add).then_inc(S["cols_done"], 1)

                        def exponents(n, r):
                            k = 6 * n
                            dve.wait_ge(S["looked_up"], n + 1)
                            found = pL[:, 0:2 * C].rearrange("p (c k) -> p c k", k=2)
                            nc.vector.tensor_tensor(ea[:, :], found[:, :, 0], key[:, r, :], ALU.add).then_inc(S["v_a"], 1)
                            dve.wait_ge(S["v_a"], k + 5)
                            nc.vector.scalar_tensor_tensor(out=eb[:, :], in0=ea[:, :], scalar=SLOPE, in1=ea[:, :],
                                                           op0=ALU.mult, op1=ALU.max).then_inc(S["v_a"], 1)
                            dve.wait_ge(S["v_a"], k + 6)
                            need(dve, S["exp_done"], n)
                            nc.vector.tensor_tensor(ec[:, :], eb[:, :], found[:, :, 1], ALU.subtract).then_inc(S["exp_in"], 1)

                        def messages(n, r, at):
                            dve.wait_ge(S["factor_done"], n + 1)
                            need(dve, S["added"], n)
                            nc.vector.tensor_tensor(node_sum[:, at], node_sum[:, at], fac[:, :],
                                                    ALU.mult).then_inc(S["scaled"], 1)
                            dve.wait_ge(S["exp_done"], n + 1)
                            need(dve, S["scattered"], n - 1)
                            nc.vector.tensor_copy(msg[:, r % 2, :, D], ex[:, :])
                            nc.vector.tensor_tensor(msg[:, r % 2, :, 0:D], kept[:, r, :, :], ex[:, :].unsqueeze(2).to_broadcast([P, C, D]),
                                                    ALU.mult).then_inc(S["msg_done"], 1)

                        def maxima(n):
                            dve.wait_ge(S["keys_turned"], n + 1)
                            for h in range(2):
                                last = nc.vector.tensor_reduce(tops[:, h:h + 1], pK[h][0:W, :], AX, ALU.max)
                            last.then_inc(S["m_done"], 1)
                            dve.wait_ge(S["m_done"], n + 1)
                            nc.vector.tensor_tensor(top[:, 0:1], tops[:, 0:1], tops[:, 1:2], ALU.max).then_inc(S["max_found"], 1)
                            dve.wait_ge(S["max_found"], n + 1)
                            need(dve, S["max_spread"], n)
                            nc.vector.tensor_scalar(topD[:, :], ident[0:W, 0:W], top[:, 0:1], None, ALU.mult).then_inc(S["diag_done"], 1)

                        def add(n, at):
                            dve.wait_ge(S["scattered"], n + 1)
                            dve.wait_ge(S["scaled"], n + 1)
                            nc.vector.tensor_tensor(node_sum[:, at], node_sum[:, at],
                                                    pG[0:D + 1, 0:W], ALU.add).then_inc(S["added"], 1)

                        def step(i, r):
                            n = RING * i + r
                            need(dve, S["scattered"], n - 3)
                            one_hot(hot, i, r, RING).then_inc(S["hot_done"], 1)
                            if reached(n, 2):
                                scores(n - 2, windows.of(r, 2))
                            dve.wait_ge(S["rows_kept"], n + 1)
                            nc.vector.tensor_tensor(prod[:, :, :], kept[:, r, :, :], vec["w_j"][:, :].unsqueeze(1).to_broadcast([P, C, D]),
                                                    ALU.mult).then_inc(S["summed"], 1)
                            dve.wait_ge(S["summed"], 2 * n + 1)
                            nc.vector.tensor_reduce(sj[:, :], prod[:, :, :], AX, ALU.add).then_inc(S["summed"], 1)
                            dve.wait_ge(S["summed"], 2 * n + 2)
                            nc.vector.tensor_scalar(key[:, r, :], sj[:, :], least[:, 0:1], None, ALU.subtract).then_inc(S["keys_done"], 1)
                            if reached(n, 1):
                                maxima(n - 1)
                            if reached(n, 3):
                                add(n - 3, windows.of(r, 3))
                            if reached(n, 2):
                                exponents(n - 2, (r - 2) % RING)
                                messages(n - 2, (r - 2) % RING, windows.of(r, 2))

                        def tail():
                            add(G - 3, windows.of(0, 3))
                            scores(G - 2, windows.of(0, 2))
                            maxima(G - 1)
                            exponents(G - 2, (G - 2) % RING)
                            messages(G - 2, (G - 2) % RING, windows.of(0, 2))
                            add(G - 2, windows.of(1, 3))
                            scores(G - 1, windows.of(1, 2))
                            exponents(G - 1, (G - 1) % RING)
                            messages(G - 1, (G - 1) % RING, windows.of(1, 2))
                            add(G - 1, windows.of(2, 3))
                        over_groups(dve, step, tail, windows.load)
                next_pass()

        with ExitStack() as ls:
            s_v, s_turn, s_used, s_var, s_std, s_table, s_store = (sem(n, ls) for n in (
                "n1_v", "n1_turn", "n1_used", "n1_var", "n1_std", "n1_table", "n1_store"))
            y, h = rows[:, 0], rows[:, 1]
            with nc.Block() as block:
                @block.tensor
                def _(pe):
                    transposes(pe, D + 1, 7, s_turn, s_used)

                @block.scalar
                def _(act):
                    act.wait_ge(s_var, 1)
                    nc.scalar.sqrt(stat[:, 1, :], stat[:, 1, :]).then_inc(s_std, 1)
                    act.wait_ge(s_var, 2)
                    nc.scalar.sqrt(stat[:, 4, :], stat[:, 3, :]).then_inc(s_std, 1)

                @block.sync
                def _(sp):
                    sp.wait_ge(s_table, 1)
                    sp.dma_start(table[2].rearrange("(t p) d -> p t d", p=P), h).then_inc(s_store, 16)
                    sp.wait_ge(s_store, 16)

                @block.vector
                def _(dve):
                    chain = Chain(dve, s_v)

                    def use(a, z, v):
                        chain.then(nc.vector.tensor_scalar(stat[:, 5, a:z], v[:, :, D], 1e-30, None, ALU.max))
                        chain.then(nc.vector.reciprocal(stat[:, 6, a:z], stat[:, 5, a:z]))
                        chain.then(nc.vector.tensor_tensor(y[:, a:z, :], v[:, :, 0:D], stat[:, 6, a:z].unsqueeze(2).to_broadcast([P, z - a, D]), ALU.mult))
                        return nc.vector.scalar_tensor_tensor(out=y[:, a:z, :], in0=y[:, a:z, :], scalar=0.0, in1=xn[:, a:z, :],
                                                              op0=ALU.max, op1=ALU.add)
                    read_tiles(dve, D + 1, 7, s_turn, s_used, use)
                    dve.wait_ge(s_used, NT // 7)
                    layer_norm(dve, chain, y, s_var, s_std, 1)
                    nc.vector.tensor_scalar(stat[:, 3, :], out_deg[:, :], 1.0, None, ALU.max).then_inc(s_var, 1)
                    dve.wait_ge(s_std, 2)
                    chain.then(nc.vector.reciprocal(stat[:, 4, :], stat[:, 4, :]))
                    nc.vector.tensor_tensor(h, xn[:, :, :], over_features(stat[:, 4, :]), ALU.mult).then_inc(s_table, 1)

        with ExitStack() as ls:
            xg = sb("xg2", [P, RING, C, D + 1], f32, ls)
            idx = sb("idx2", [P, RING, C], i32, ls)
            hot = sb("hot2", [P, 2, C, W], f32, ls)
            pG2 = [bank[0], bank[1]]
            zero_state(2)
            with nc.Block() as block:
                @block.vector
                def _(dve):
                    nc.vector.memset(xg[:, :, :, D:D + 1], 1.0)
            with nc.Fori(0, npasses):
                with nc.Block() as block:
                    load = edge_loads(xg, idx, None, None, 0)
                    gather = gathers(2, xg, idx)

                    @block.sync
                    def _(sp):
                        load(sp, None)

                    @block.gpsimd
                    def _(pool):
                        gather(pool, S["scattered"])

                    @block.tensor
                    def _(pe):
                        def step(i, r):
                            n, b = RING * i + r, r % 2
                            pe.wait_ge(ring_sems["gathered"][r], 16 * C * (i + 1))
                            pe.wait_ge(S["hot_done"], n + 1)
                            need(pe, S["added"], n - 1)
                            for c in range(C):
                                last = nc.tensor.matmul(pG2[b][0:D + 1, 0:W], xg[:, r, c, :], hot[:, b, c, :], start=(c == 0), stop=(c == C - 1))
                            last.then_inc(S["scattered"], 1)
                        over_groups(pe, step)

                    @block.vector
                    def _(dve):
                        windows = Windows(1)

                        def add(n, r):
                            at = windows.of(r, 1)
                            dve.wait_ge(S["scattered"], n + 1)
                            need(dve, S["added"], n)
                            nc.vector.tensor_tensor(node_sum[:, at], node_sum[:, at], pG2[(r - 1) % 2][0:D + 1, 0:W],
                                                    ALU.add).then_inc(S["added"], 1)

                        def step(i, r):
                            n, b = RING * i + r, r % 2
                            need(dve, S["scattered"], n - 1)
                            one_hot(hot, i, r).then_inc(S["hot_done"], 1)
                            if not (isinstance(n, int) and n == 0):
                                add(n - 1, r)
                        over_groups(dve, step, lambda: add(G - 1, 0), windows.load)
                next_pass()

        with ExitStack() as ls:
            s_v, s_turn, s_used, s_var, s_std, s_table, s_store, s_deg = (sem(n, ls) for n in (
                "n2_v", "n2_turn", "n2_used", "n2_var", "n2_std", "n2_table", "n2_store", "n2_deg"))
            y, h = rows[:, 0], rows[:, 1]
            in_deg = stat[:, 3, :]
            with nc.Block() as block:
                @block.tensor
                def _(pe):
                    transposes(pe, D + 1, 7, s_turn, s_used)

                @block.scalar
                def _(act):
                    act.wait_ge(s_var, 1)
                    nc.scalar.sqrt(stat[:, 4, :], in_deg).then_inc(s_std, 1)
                    act.wait_ge(s_var, 2)
                    nc.scalar.sqrt(stat[:, 1, :], stat[:, 1, :]).then_inc(s_std, 1)

                @block.sync
                def _(sp):
                    sp.wait_ge(s_table, 1)
                    sp.dma_start(table[3].rearrange("(t p) d -> p t d", p=P), h).then_inc(s_store, 16)
                    sp.wait_ge(s_store, 16)

                @block.vector
                def _(dve):
                    chain = Chain(dve, s_v)

                    def use(a, z, v):
                        chain.then(nc.vector.tensor_scalar(in_deg[:, a:z], v[:, :, D], 1.0, None, ALU.max))
                        return nc.vector.tensor_copy(y[:, a:z, :], v[:, :, 0:D])
                    read_tiles(dve, D + 1, 7, s_turn, s_used, use)
                    dve.wait_ge(s_used, NT // 7)
                    nc.vector.tensor_copy(stat[:, 5, :], in_deg).then_inc(s_var, 1)
                    dve.wait_ge(s_std, 1)
                    chain.then(nc.vector.reciprocal(stat[:, 4, :], stat[:, 4, :]))
                    chain.then(nc.vector.tensor_tensor(y, y, over_features(stat[:, 4, :]), ALU.mult))
                    chain.then(nc.vector.scalar_tensor_tensor(out=y, in0=y, scalar=ALPHA_TOTAL, in1=xn[:, :, :], op0=ALU.mult, op1=ALU.add))
                    layer_norm(dve, chain, y, s_var, s_std, 2)
                    nc.vector.tensor_tensor(h, xn[:, :, :], over_tiles(vec["b_e"][:, :]), ALU.add).then_inc(s_table, 1)

        with ExitStack() as ls:
            xg = sb("xg3", [P, RING, C, D], f32, ls)
            idx = sb("idx3", [P, RING, C], i32, ls)
            attr = sb("attr3", [P, RING, C * D3], f32, ls)
            attrT = sb("attrT3", [P, P], f32, ls)
            msg = sb("msg3", [P, 2, C, D], f32, ls)
            hot = sb("hot3", [P, 2, C, W], f32, ls)
            pA, pG = bank[0], bank[1]
            pE = [bank[2], bank[3]]
            zero_state(3)
            with nc.Fori(0, npasses):
                with nc.Block() as block:
                    load = edge_loads(xg, idx, attr, edge16, C * D3)
                    gather = gathers(3, xg, idx)

                    @block.sync
                    def _(sp):
                        load(sp, S["a_turned"])

                    @block.gpsimd
                    def _(pool):
                        gather(pool, S["e_product"])

                    @block.tensor
                    def _(pe):
                        def scatter(n, b):
                            pe.wait_ge(S["msg_done"], n + 1)
                            pe.wait_ge(S["hot_done"], n + 1)
                            need(pe, S["added"], n)
                            for c in range(C):
                                last = nc.tensor.matmul(pG[0:D, 0:W], msg[:, b, c, :], hot[:, b, c, :], start=(c == 0), stop=(c == C - 1))
                            last.then_inc(S["scattered"], 1)

                        def step(i, r):
                            n, b = RING * i + r, r % 2
                            pe.wait_ge(ring_sems["attr_in"][r], 16 * (i + 1))
                            need(pe, S["a_kept"], n)
                            nc.tensor.transpose(pA[:, 0:P], attr[:, r, :], ident[:, :]).then_inc(S["a_turned"], 1)
                            if not (isinstance(n, int) and n == 0):
                                scatter(n - 1, 1 - b)
                            pe.wait_ge(S["a_kept"], n + 1)
                            pe.wait_ge(ring_sems["gathered"][r], 16 * C * (i + 1))
                            need(pe, S["msg_done"], n - 1)
                            nc.tensor.matmul(pE[b][:, :], attrT[:, :], W3BD[:, :], start=True, stop=False)
                            nc.tensor.matmul(pE[b][:, :], ident[:, :], xg[:, r].rearrange("p c d -> p (c d)"),
                                             start=False, stop=True).then_inc(S["e_product"], 1)
                        over_groups(pe, step, lambda: scatter(G - 1, 1))

                    @block.scalar
                    def _(act):
                        def step(i, r):
                            n, b = RING * i + r, r % 2
                            act.wait_ge(S["a_turned"], n + 1)
                            need(act, S["e_product"], n)
                            nc.scalar.copy(attrT[:, :], pA[:, 0:P]).then_inc(S["a_kept"], 1)
                            act.wait_ge(S["e_product"], n + 1)
                            need(act, S["scattered"], n - 1)
                            nc.scalar.activation(msg[:, b].rearrange("p c d -> p (c d)"), pE[b][:, :], ACT.Relu).then_inc(S["msg_done"], 1)
                        over_groups(act, step)

                    @block.vector
                    def _(dve):
                        windows = Windows(1)

                        def add(n, r):
                            at = windows.of(r, 1)
                            dve.wait_ge(S["scattered"], n + 1)
                            need(dve, S["added"], n)
                            nc.vector.tensor_tensor(node_sum[0:D, at], node_sum[0:D, at], pG[0:D, 0:W], ALU.add).then_inc(S["added"], 1)

                        def step(i, r):
                            n = RING * i + r
                            need(dve, S["scattered"], n - 1)
                            one_hot(hot, i, r).then_inc(S["hot_done"], 1)
                            if not (isinstance(n, int) and n == 0):
                                add(n - 1, r)
                        over_groups(dve, step, lambda: add(G - 1, 0), windows.load)
                next_pass()

        with ExitStack() as ls:
            (s_v, s_turn, s_used, s_h, s_hused, s_part, s_total, s_var, s_std, s_out) = (sem(n, ls) for n in (
                "n3_v", "n3_turn", "n3_used", "n3_h", "n3_hused", "n3_part", "n3_total", "n3_var", "n3_std", "n3_out"))
            part = sb("n3_part_sb", [P, D], f32, ls)
            mean = sb("n3_mean", [P, D], f32, ls)
            var = sb("n3_var_sb", [P, D], f32, ls)
            std = sb("n3_std_sb", [P, D], f32, ls)
            y, z = rows[:, 0], rows[:, 1]
            by_feature = y.rearrange("p t d -> p d t")
            z_by_feature = z.rearrange("p t d -> p d t")
            with nc.Block() as block:
                @block.tensor
                def _(pe):
                    for j, t0 in enumerate(range(0, NT, 4)):
                        need(pe, s_used, j - 1)
                        for t in range(t0, min(t0 + 4, NT)):
                            last = nc.tensor.transpose(bank[j % 2][0:D, (t - t0) * P:(t - t0 + 1) * P], xn[:, t, :], ident[:, :])
                        last.then_inc(s_turn, 1)
                    pe.wait_ge(s_used, -(-NT // 4))
                    for j, t0 in enumerate(range(0, NT, 8)):
                        need(pe, s_hused, j - 1)
                        for t in range(t0, min(t0 + 8, NT)):
                            last = nc.tensor.matmul(bank[2 + j % 2][:, (t - t0) * D:(t - t0 + 1) * D], node_sum[0:D, t * P:(t + 1) * P],
                                                    Wgin[:, :], start=True, stop=True)
                        last.then_inc(s_h, 1)
                    pe.wait_ge(s_part, 1)
                    nc.tensor.matmul(bank[4][:, 0:D], ones[:, :], part[:, :], start=True, stop=True).then_inc(s_total, 1)
                    pe.wait_ge(s_part, 2)
                    nc.tensor.matmul(bank[5][:, 0:D], ones[:, :], part[:, :], start=True, stop=True).then_inc(s_total, 1)

                @block.scalar
                def _(act):
                    act.wait_ge(s_var, 1)
                    nc.scalar.sqrt(std[:, :], var[:, :]).then_inc(s_std, 1)
                    act.wait_ge(s_var, 2)
                    nc.scalar.sqrt(stat[:, 1, :], stat[:, 1, :]).then_inc(s_std, 1)

                @block.vector
                def _(dve):
                    chain = Chain(dve, s_v)
                    for j, t0 in enumerate(range(0, NT, 4)):
                        dve.wait_ge(s_turn, j + 1)
                        cols = slice(t0 * P, min(t0 + 4, NT) * P)
                        nc.vector.tensor_tensor(node_sum[0:D, cols], node_sum[0:D, cols], bank[j % 2][0:D, 0:cols.stop - cols.start],
                                                ALU.add).then_inc(s_used, 1)
                    for j, t0 in enumerate(range(0, NT, 8)):
                        dve.wait_ge(s_h, j + 1)
                        k = min(8, NT - t0)
                        nc.vector.tensor_tensor(y[:, t0:t0 + k, :], bank[2 + j % 2][:, 0:k * D].rearrange("p (t d) -> p t d", d=D),
                                                vec["b_gin"][:, :].unsqueeze(1).to_broadcast([P, k, D]), ALU.add).then_inc(s_hused, 1)
                    dve.wait_ge(s_hused, -(-NT // 8))
                    chain.then(nc.vector.tensor_scalar(y[:, NT - 1, :], y[:, NT - 1, :], real[:, 0:1], None, ALU.mult))
                    nc.vector.tensor_reduce(part[:, :], by_feature, AX, ALU.add).then_inc(s_part, 1)
                    dve.wait_ge(s_total, 1)
                    chain.then(nc.vector.tensor_scalar(mean[:, :], bank[4][:, 0:D], 1.0 / N, None, ALU.mult))
                    chain.then(nc.vector.tensor_tensor(y, y, over_tiles(mean[:, :]), ALU.subtract))
                    chain.then(nc.vector.tensor_tensor(z, y, y, ALU.mult))
                    chain.then(nc.vector.tensor_scalar(z[:, NT - 1, :], z[:, NT - 1, :], real[:, 0:1], None, ALU.mult))
                    nc.vector.tensor_reduce(part[:, :], z_by_feature, AX, ALU.add).then_inc(s_part, 1)
                    dve.wait_ge(s_total, 2)
                    nc.vector.tensor_scalar(var[:, :], bank[5][:, 0:D], 1.0 / N, EPS, ALU.mult, ALU.add).then_inc(s_var, 1)
                    dve.wait_ge(s_std, 1)
                    chain.then(nc.vector.reciprocal(std[:, :], std[:, :]))
                    chain.then(nc.vector.tensor_tensor(std[:, :], std[:, :], vec["gamma3"][:, :], ALU.mult))
                    chain.then(nc.vector.tensor_tensor(y, y, over_tiles(std[:, :]), ALU.mult))
                    chain.then(nc.vector.tensor_tensor(y, y, over_tiles(vec["beta3"][:, :]), ALU.add))
                    chain.then(nc.vector.scalar_tensor_tensor(out=y, in0=y, scalar=0.0, in1=xn[:, :, :], op0=ALU.max, op1=ALU.add))
                    layer_norm(dve, chain, y, s_var, s_std, 2)

            with nc.Block() as block:
                @block.sync
                def _(sp):
                    full = NT - 1
                    sp.dma_start(out[0:full * P, :].rearrange("(t p) d -> p t d", p=P), xn[:, 0:full, :]).then_inc(s_out, 16)
                    sp.dma_start(out[full * P:N, :], xn[0:LAST, full, :]).then_inc(s_out, 16)
                    sp.wait_ge(s_out, 32)


_FLOATS = ["edge_attr_16", "edge_attr_64", "L0_gnn_We2", "L0_gnn_be2", "L0_gnn_Wm2", "L0_gnn_bm2", "L0_gnn_eps2",
           "L0_gnn_gamma2", "L0_gnn_beta2", "L1_gnn_w_i", "L1_gnn_w_j", "L3_gnn_W_e", "L3_gnn_b_e", "L3_gnn_W_gin",
           "L3_gnn_b_gin", "L3_gnn_gamma", "L3_gnn_beta"]


def kernel(**inputs):
    import numpy as np
    import concourse.bacc as bacc
    from concourse.bass_utils import run_bass_kernel_spmd

    def padded(a, rows, fill):
        a = np.asarray(a)
        more = np.full((rows - a.shape[0],) + a.shape[1:], fill, a.dtype)
        return np.ascontiguousarray(np.concatenate([a, more]))

    arrays = {
        "x": padded(inputs["x"], NP, 0),
        "src": padded(inputs["src"], EP, N),
        "dst": padded(inputs["dst"], EP, N),
    }
    for name in _FLOATS:
        a = np.ascontiguousarray(np.asarray(inputs[name]))
        arrays[name] = padded(a, EP, 0) if name.startswith("edge") else a
    nc = bacc.Bacc("TRN2", target_bir_lowering=False, num_devices=1)
    args = [nc.dram_tensor("in_" + n, a.shape, mybir.dt.from_np(a.dtype), kind="ExternalInput").ap() for n, a in arrays.items()]
    out = nc.dram_tensor("out", (N, D), f32, kind="ExternalOutput").ap()
    build_program(nc, *args, out)
    r = run_bass_kernel_spmd(nc, [{"in_" + n: a for n, a in arrays.items()}], core_ids=[0])
    return r.results[0]["out"]
```

```python
import concourse.bass as bass
from concourse import mybir
from contextlib import ExitStack

f32 = mybir.dt.float32
bf16 = mybir.dt.bfloat16
i32 = mybir.dt.int32
ALU = mybir.AluOpType
ACT = mybir.ActivationFunctionType
AX = mybir.AxisListType.X

P = 128
W = 80
N = 6250
E = 200000
D = 64
D3 = 16
NT = -(-N // P)
NP = NT * P
LAST = N - (NT - 1) * P
C = 8
GE = C * P
RING = 4
G = -(-E // GE)
G += -G % RING
ROUNDS = G // RING
EP = G * GE
Q = G // 2
PASSES_MAX = -(-(N + 1) // W)
EPS = 1e-5
SLOPE = 0.01
ALPHA_TOTAL = 1.0 + 1.0 / 2.0 + 1.0 / 3.0
BANK = 512
LOOKED = ((0, C - 1), (1, C - 1), (2, C - 1), (3, C - 1), (0, C - 2))
LOOKED_UP = (1, 0, 5, 4)


def gathered_chunks(layer, r):
    return C - sum(1 for at, _ in LOOKED[:LOOKED_UP[layer]] if at == r)


def need(eng, sem, value):
    if isinstance(value, int) and value <= 0:
        return
    eng.wait_ge(sem, value)


def over_groups(eng, step, tail=None, begin=None, peel_last=False):
    begin = begin or (lambda i: None)
    begin(0)
    for r in range(RING):
        step(0, r)
    with eng.Fori(1, ROUNDS - peel_last) as i:
        begin(i)
        for r in range(RING):
            step(i, r)
    if peel_last:
        begin(ROUNDS - 1)
        for r in range(RING):
            step(ROUNDS - 1, r)
    begin(ROUNDS)
    if tail is not None:
        tail()


class Chain:

    def __init__(self, eng, sem):
        self.eng, self.sem, self.count = eng, sem, 0

    def then(self, instruction):
        instruction.then_inc(self.sem, 1)
        self.count += 1
        self.eng.wait_ge(self.sem, self.count)


def build_program(nc, x, src, src_looked_up, dst, edge16, edge64, We2, be2, Wm2, bm2, eps2, gamma2, beta2,
                  w_i, w_j, W_e, b_e, W_gin, b_gin, gamma3, beta3, out):
    with ExitStack() as ctx:
        def sb(name, shape, dt=f32, where=ctx):
            return where.enter_context(nc.sbuf_tensor(name, shape, dt))

        def sem(name, where=ctx):
            return where.enter_context(nc.semaphore(name))

        bank = [ctx.enter_context(nc.psum_tensor(f"bank{j}", [P, BANK], f32)) for j in range(6)]
        wide = ctx.enter_context(nc.psum_tensor("wide", [P, 2 * BANK], f32))

        table = [x] + [nc.dram_tensor(f"table{n}", (NP, D + (n == 1)), f32, kind="Internal").ap() for n in (1, 2, 3)]
        si_row = nc.dram_tensor("si_row", (NP,), f32, kind="Internal").ap()

        ident = sb("ident", [P, P])
        ones = sb("ones", [P, P])
        iota0 = sb("iota0", [P, P])
        iota = sb("iota", [P, W])
        part = sb("part", [P, 1])
        real = sb("real", [P, 1])
        dst_rel = sb("dst_rel", [P, G * C])
        src_lo = sb("src_lo", [P, G * C])
        src_hi = sb("src_hi", [P, G * C])
        start0 = sb("start0", [1, G])
        start_f = sb("start_f", [1, G])
        start_i = sb("start_i", [1, 2, G + 2 * RING], i32)
        passes = sb("passes", [1, 1], i32)
        node_sum = sb("node_sum", [D + 1, NP + W])
        xn = sb("xn", [P, NT, D])
        out_deg = sb("out_deg", [P, NT])
        rows = sb("rows", [P, 2, NT, D])
        stat = sb("stat", [P, 8, NT])

        WeBD = sb("WeBD", [P, P])
        WmBD = sb("WmBD", [P, P])
        W3BD = sb("W3BD", [P, C * D])
        Wgin = sb("Wgin", [D, D])
        be_col = sb("be_col", [P, 1])
        bm_row = sb("bm_row", [1, C * D])
        eps_col = sb("eps_col", [P, 1])
        least = sb("least", [P, 1])
        vec = {n: sb(n + "_b", [P, D]) for n in ("gamma2", "beta2", "w_i", "w_j", "b_e", "b_gin", "gamma3", "beta3")}

        LAGS = (1, 3)

        def set_starts(start):
            for k, lag in enumerate(LAGS):
                nc.vector.tensor_copy(start_i[0:1, k, lag:lag + G], start[0:1, :])

        def start_layer():
            nc.vector.tensor_copy(iota[:, :], iota0[:, 0:W])
            nc.vector.tensor_copy(start_f[0:1, :], start0[0:1, :])
            set_starts(start0)

        with ExitStack() as ps:
            dst_i = sb("dst_i", [Q, 2 * GE], i32, ps)
            src_i = sb("src_i", [Q, 2 * GE], i32, ps)
            lo_i = sb("lo_i", [Q, 2 * GE], i32, ps)
            byrow = [sb(f"byrow{j}", [Q, 2 * GE], f32, ps) for j in range(3)]
            iota_i = sb("iota_i", [P, P + 1], i32, ps)
            low = sb("low", [Q, 2], f32, ps)
            high = sb("high", [Q, 2], f32, ps)
            diag = sb("diag", [Q, 2, Q], f32, ps)
            span = sb("span", [1, 2], f32, ps)
            steps = sb("steps", [1, P], f32, ps)
            s_idx, s_zero, s_w, s_iota, s_v = (sem(n, ps) for n in ("s_idx", "s_zero", "s_w", "s_iota", "s_v"))
            s_norm = sem("s_norm", ps)
            S_W_ALL = 16 * (1 + 8 + 2 + C + 2 + 4 + C)
            wsq = sb("wsq", [P, D], f32, ps)
            norm = sb("norm", [P, 1], f32, ps)
            s_const, s_rows, s_turned, s_kept, s_ends, s_row1, s_diag, s_base = (
                sem(n, ps) for n in ("s_const", "s_rows", "s_turned", "s_kept", "s_ends", "s_row1", "s_diag", "s_base"))
            with nc.Block() as block:
                @block.sync
                def _(sp):
                    sp.dma_start(dst_i[:, :], dst.rearrange("(q e) -> q e", q=Q)).then_inc(s_idx, 16)
                    sp.dma_start(src_i[:, :], src.rearrange("(q e) -> q e", q=Q)).then_inc(s_idx, 16)
                    sp.dma_start(xn[:, :, :], x.rearrange("(t p) d -> p t d", p=P)).then_inc(s_w, 16)
                    given = {"gamma2": gamma2, "beta2": beta2, "w_i": w_i, "w_j": w_j, "b_e": b_e,
                             "b_gin": b_gin, "gamma3": gamma3, "beta3": beta3}
                    for name, v in given.items():
                        sp.dma_start(vec[name][:, :], v.partition_broadcast(P)).then_inc(s_w, 16)
                    sp.dma_start(eps_col[:, :], eps2.partition_broadcast(P)).then_inc(s_w, 16)
                    sp.dma_start(Wgin[:, :], W_gin).then_inc(s_w, 16)
                    for c in range(C):
                        sp.dma_start(bm_row[0:1, c * D:(c + 1) * D], bm2.unsqueeze(0)).then_inc(s_w, 16)
                    for h in range(2):
                        sp.dma_start(be_col[h * D:(h + 1) * D, :], be2.unsqueeze(1)).then_inc(s_w, 16)
                    sp.wait_ge(s_zero, 4)
                    for h in range(2):
                        at = slice(h * D, (h + 1) * D)
                        sp.dma_start(WeBD[at, at], We2).then_inc(s_w, 16)
                        sp.dma_start(WmBD[at, at], Wm2).then_inc(s_w, 16)
                    for c in range(C):
                        sp.dma_start(W3BD[c * D3:(c + 1) * D3, c * D:(c + 1) * D], W_e).then_inc(s_w, 16)
                    sp.wait_ge(s_w, S_W_ALL)

                @block.gpsimd
                def _(pool):
                    nc.gpsimd.iota(iota_i[:, 0:P], [[1, P]], base=0, channel_multiplier=0).then_inc(s_iota, 1)
                    nc.gpsimd.iota(iota_i[:, P:P + 1], [[0, 1]], base=0, channel_multiplier=1).then_inc(s_iota, 1)
                    nc.gpsimd.memset(WeBD[:, :], 0.0).then_inc(s_zero, 1)
                    nc.gpsimd.memset(WmBD[:, :], 0.0).then_inc(s_zero, 1)
                    nc.gpsimd.memset(W3BD[:, :], 0.0).then_inc(s_zero, 1)
                    nc.gpsimd.memset(ones[:, :], 1.0).then_inc(s_zero, 1)
                    nc.gpsimd.memset(node_sum[:, :], 0.0)

                @block.vector
                def _(dve):
                    chain = Chain(dve, s_v)
                    dve.wait_ge(s_iota, 2)
                    nc.vector.tensor_copy(iota0[:, :], iota_i[:, 0:P])
                    chain.then(nc.vector.tensor_copy(part[:, :], iota_i[:, P:P + 1]))
                    nc.vector.tensor_scalar(real[:, :], part[:, :], float(LAST), None, ALU.is_lt)
                    nc.vector.tensor_scalar(ident[:, :], iota0[:, :], part[:, 0:1], None, ALU.is_equal).then_inc(s_const, 1)
                    dve.wait_ge(s_idx, 32)
                    nc.vector.tensor_copy(byrow[0][:, :], dst_i[:, :]).then_inc(s_rows, 1)
                    chain.then(nc.vector.tensor_scalar(lo_i[:, :], src_i[:, :], P - 1, None, ALU.bitwise_and))
                    nc.vector.tensor_copy(byrow[1][:, :], lo_i[:, :]).then_inc(s_rows, 1)
                    dve.wait_ge(s_rows, 2)
                    chain.then(nc.vector.tensor_scalar(lo_i[:, :], src_i[:, :], 7, None, ALU.arith_shift_right))
                    nc.vector.tensor_copy(byrow[2][:, :], lo_i[:, :]).then_inc(s_rows, 1)
                    two = byrow[0][:, :].rearrange("q (b e) -> q b e", b=2)
                    nc.vector.tensor_reduce(low[:, :], two, AX, ALU.min)
                    chain.then(nc.vector.tensor_reduce(high[:, :], two, AX, ALU.max))
                    chain.then(nc.vector.tensor_tensor(high[:, :], high[:, :], low[:, :], ALU.subtract))
                    for b in range(2):
                        last = nc.vector.tensor_scalar(diag[:, b, :], ident[0:Q, 0:Q], low[:, b:b + 1], None, ALU.mult)
                    last.then_inc(s_ends, 1)
                    dve.wait_ge(s_row1, 1)
                    chain.then(nc.vector.tensor_copy(start0[0:1, :].rearrange("o (q b) -> o b q", b=2),
                                                     bank[4][0:1, 0:2 * P].rearrange("o (b q) -> o b q", b=2)[:, :, 0:Q]))
                    chain.then(nc.vector.tensor_reduce(span[0:1, 0:1], bank[4][0:1, 2 * P:4 * P].rearrange("o (b q) -> o b q", b=2)[:, :, 0:Q],
                                                       mybir.AxisListType.XY, ALU.max))
                    chain.then(nc.vector.tensor_scalar(steps[0:1, :], iota0[0:1, :], float(W), span[0:1, 0:1], ALU.mult, ALU.is_le))
                    chain.then(nc.vector.tensor_reduce(span[0:1, 1:2], steps[0:1, :], AX, ALU.add))
                    chain.then(nc.vector.tensor_copy(passes[0:1, :], span[0:1, 1:2]))
                    dve.wait_ge(s_w, S_W_ALL)
                    chain.then(nc.vector.tensor_tensor(wsq[:, :], vec["w_j"][:, :], vec["w_j"][:, :], ALU.mult))
                    nc.vector.tensor_reduce(least[:, :], wsq[:, :], AX, ALU.add).then_inc(s_norm, 1)
                    dve.wait_ge(s_norm, 2)
                    nc.vector.tensor_scalar(least[:, :], norm[:, :], -1.001 * float(D) ** 0.5, None, ALU.mult)
                    start_layer()
                    for k, lag in enumerate(LAGS):
                        nc.vector.memset(start_i[0:1, k, 0:lag], 0)
                        nc.vector.memset(start_i[0:1, k, lag + G:G + 2 * RING], 0)
                    dve.wait_ge(s_base, 1)
                    dve.wait_ge(s_kept, 12)
                    for b in range(2):
                        view = dst_rel[:, :].rearrange("p (q b c) -> p b q c", b=2, c=C)[:, b]
                        base = bank[5][:, b * P:b * P + Q].unsqueeze(2).to_broadcast([P, Q, C])
                        chain.then(nc.vector.tensor_tensor(view, view, base, ALU.subtract))

                @block.scalar
                def _(act):
                    for j, to_all in enumerate((dst_rel, src_lo, src_hi)):
                        to = to_all[:, :].rearrange("p (q b c) -> p b c q", b=2, c=C)
                        for b in range(2):
                            for h in range(2):
                                n = (j * 2 + b) * 2 + h
                                act.wait_ge(s_turned, n + 1)
                                ps_view = bank[n % 4][:, :].rearrange("p (c q) -> p c q", c=4)[:, :, 0:Q]
                                nc.scalar.copy(to[:, b, 4 * h:4 * h + 4, :], ps_view).then_inc(s_kept, 1)
                    act.wait_ge(s_norm, 1)
                    nc.scalar.sqrt(norm[:, :], least[:, :]).then_inc(s_norm, 1)

                @block.tensor
                def _(pe):
                    def turn(j):
                        pe.wait_ge(s_rows, j + 1)
                        for b in range(2):
                            from_ = byrow[j][:, b * GE:(b + 1) * GE].rearrange("q (p c) -> q c p", c=C)
                            for h in range(2):
                                n = (j * 2 + b) * 2 + h
                                need(pe, s_kept, n - 3)
                                for c in range(4):
                                    last = nc.tensor.transpose(bank[n % 4][:, c * P:c * P + Q], from_[:, 4 * h + c, :], ident[0:Q, 0:Q])
                                last.then_inc(s_turned, 1)

                    pe.wait_ge(s_const, 1)
                    pe.wait_ge(s_zero, 4)
                    for j in range(3):
                        turn(j)
                    pe.wait_ge(s_ends, 1)
                    for b in range(2):
                        nc.tensor.matmul(bank[4][0:1, b * P:b * P + Q], low[:, b:b + 1], ident[0:Q, 0:Q], start=True, stop=True)
                    for b in range(2):
                        last = nc.tensor.matmul(bank[4][0:1, (2 + b) * P:(2 + b) * P + Q], high[:, b:b + 1], ident[0:Q, 0:Q], start=True, stop=True)
                    last.then_inc(s_row1, 1)
                    for b in range(2):
                        last = nc.tensor.matmul(bank[5][:, b * P:b * P + Q], ones[0:Q, :], diag[:, b, :], start=True, stop=True)
                    last.then_inc(s_base, 1)

        npasses = nc.values_load(passes[0:1, 0:1], min_val=1, max_val=PASSES_MAX)

        S = {n: sem(n) for n in (
            "attr_in", "idx_in", "gathered",
            "x_turned", "a_turned", "a_kept", "e_product", "e_done", "summed", "m_done", "m_product", "msg_done",
            "hot_done", "scattered", "added",
            "hist_done", "moved", "may_gather",
            "v_a", "v_b", "scaled", "keys_done", "masked", "keys_turned", "hot_turned", "hot_kept", "max_found",
            "diag_done", "max_spread", "factor_in", "factor_done", "cols_done", "looked_up", "exp_in", "exp_done", "rows_kept",
            "src_in", "split", "keys_step", "keys_made", "matched", "looked", "chosen",
            "si_prod", "si_ready", "si_turned", "si_kept", "si_out", "si_in",
        )}
        ring_sems = {n: [sem(f"{n}{r}") for r in range(RING)] for n in ("attr_in", "idx_in", "gathered")}

        def gathered_by(layer, i, r):
            chunks = gathered_chunks(layer, r)
            return 16 * (C - chunks) + 16 * chunks * (i + 1)

        def next_pass(layer):
            with nc.Block() as block:
                @block.vector
                def _(dve):
                    chain = Chain(dve, S["moved"])
                    nc.vector.tensor_scalar(iota[:, :], iota[:, :], float(W), None, ALU.add)
                    chain.then(nc.vector.tensor_scalar(start_f[0:1, :], start_f[0:1, :], float(W), float(NP), ALU.add, ALU.min))
                    set_starts(start_f)
            with nc.Block() as block:
                @block.sync
                def _(sp):
                    for s in S.values():
                        sp.sem_clear(s)
                    for name in ("attr_in", "idx_in"):
                        for s in ring_sems[name]:
                            sp.sem_clear(s)

                @block.gpsimd
                def _(pool):
                    for r, s in enumerate(ring_sems["gathered"]):
                        pool.wait_ge(s, gathered_by(layer, ROUNDS - 1, r))
                    pool.dma_reset()
                    for s in ring_sems["gathered"]:
                        pool.sem_clear(s)

        def edge_loads(layer, idx, attr, attr_dram):
            idx_view = src.rearrange("(i r p c) -> i r p c", r=RING, p=P, c=C)
            attr_view = None if attr is None else attr_dram.rearrange("(i r p c) d -> i r p (c d)", r=RING, p=P, c=C)

            def program(sp, attr_used, after_round=lambda i: None, peel_last=False):
                def step(i, r):
                    if not (isinstance(i, int) and i == 0):
                        sp.wait_ge(ring_sems["gathered"][r], gathered_by(layer, i - 1, r))
                    sp.dma_start(idx[:, r, :], idx_view[i, r]).then_inc(ring_sems["idx_in"][r], 16)
                    if attr is not None:
                        need(sp, attr_used, RING * i + r - (RING - 1))
                        sp.dma_start(attr[:, r, :], attr_view[i, r]).then_inc(ring_sems["attr_in"][r], 16)
                    if r == RING - 1:
                        after_round(i)
                over_groups(sp, step, peel_last=peel_last)
            return program

        def gathers(layer, xg, idx):
            def program(pool, rows_used):
                def step(i, r):
                    pool.wait_ge(ring_sems["idx_in"][r], 16 * (i + 1))
                    need(pool, rows_used, RING * i + r - (RING - 1))
                    pool.sem_inc(S["may_gather"], 1)
                    for c in range(C if isinstance(i, int) and i == 0 else gathered_chunks(layer, r)):
                        nc.gpsimd.indirect_dma_start(xg[:, r, c, 0:D + (layer == 1)], None, table[layer][:, :],
                                                     bass.IndirectOffsetOnAxis(ap=idx[:, r, c:c + 1], axis=0),
                                                     ).then_inc(ring_sems["gathered"][r], 16)
                over_groups(pool, step)
            return program

        def one_hot(hot, i, r, ring=2):
            n = RING * i + r
            col = dst_rel[:, bass.ds(n * C, C)] if not isinstance(n, int) else dst_rel[:, n * C:(n + 1) * C]
            return nc.vector.tensor_tensor(hot[:, r % ring], iota[:, :].unsqueeze(1).to_broadcast([P, C, W]),
                                           col.unsqueeze(2).to_broadcast([P, C, W]), ALU.is_equal)

        class Windows:

            def __init__(self, lag):
                self.lag, self.count = lag, RING if lag == 1 else RING + 1

            def load(self, i):
                at = RING * i
                cols = slice(at, at + self.count) if isinstance(at, int) else bass.ds(at, self.count)
                self.held = nc.values_load_multi_w_load_instructions(
                    start_i[0:1, LAGS.index(self.lag), cols], engines=(mybir.EngineType.DVE,), min_val=0, max_val=NP)[1]

            def of(self, r, lag):
                return bass.ds(self.held[r - lag + self.lag], W)

        PIECE = -(-NT // RING)
        PIECES = [(r * PIECE, min((r + 1) * PIECE, NT)) for r in range(RING)]

        class Lookup:

            def __init__(self, layer, where, reader, banks):
                self.count, self.reader = LOOKED_UP[layer], reader
                self.edges = RE = self.count * P
                self.at = [banks[k // 2][:, (k % 2) * 3 * D:(k % 2 + 1) * 3 * D] for k in range(self.count)]
                self.banks = banks
                self.split = sb(f"split{layer}", [P, NT, 3, D], bf16, where)
                self.src_b = sb(f"src_b{layer}", [P, RE], i32, where)
                self.lo_b = sb(f"lo_b{layer}", [P, RE], i32, where)
                self.hi_b = sb(f"hi_b{layer}", [P, RE], i32, where)
                self.tile_b = sb(f"tile_b{layer}", [P, RE], f32, where)
                self.tile_key = sb(f"tile_key{layer}", [P, RE], bf16, where)
                self.match = sb(f"match{layer}", [P, 2, PIECE, RE], bf16, where)

            def load(self, sp, i):
                need(sp, S["keys_made"], i - 1)
                rounds = src_looked_up.rearrange("(i e) -> i e", e=len(LOOKED) * P)
                sp.dma_start(self.src_b[:, :], rounds[i][0:self.edges].partition_broadcast(P)).then_inc(S["src_in"], 16)

            def split_rows(self, dve, table_sb):
                split = self.split
                rest = rows[:, 0]
                for k in range(3):
                    from_ = table_sb if k == 0 else rest
                    nc.vector.tensor_copy(split[:, :, k, :], from_).then_inc(S["split"], 1)
                    dve.wait_ge(S["split"], 2 * k + 1)
                    if k < 2:
                        nc.vector.tensor_tensor(rest, from_, split[:, :, k, :], ALU.subtract).then_inc(S["split"], 1)
                        dve.wait_ge(S["split"], 2 * k + 2)

            def keys(self, dve, i):
                k = 3 * (i - 1)
                lo_b, hi_b, tile_b, tile_key = self.lo_b, self.hi_b, self.tile_b, self.tile_key
                dve.wait_ge(S["src_in"], 16 * i)
                nc.vector.tensor_scalar(lo_b[:, :], self.src_b[:, :], P - 1, None, ALU.bitwise_and)
                nc.vector.tensor_scalar(hi_b[:, :], self.src_b[:, :], 7, None, ALU.arith_shift_right).then_inc(S["keys_step"], 1)
                dve.wait_ge(S["keys_step"], k + 1)
                nc.vector.tensor_scalar(tile_b[:, :], hi_b[:, :], 1.0, None, ALU.add).then_inc(S["keys_step"], 1)
                dve.wait_ge(S["keys_step"], k + 2)
                nc.vector.scalar_tensor_tensor(out=tile_key[:, :], in0=lo_b[:, :], scalar=part[:, 0:1], in1=tile_b[:, :],
                                               op0=ALU.is_equal, op1=ALU.mult).then_inc(S["keys_step"], 1)
                dve.wait_ge(S["keys_step"], k + 3)
                dve.sem_inc(S["keys_made"], 1)

            def search(self, dve, i, r):
                q = RING * (i - 1) + r
                need(dve, S["looked"], q - 1)
                for t in range(*PIECES[r]):
                    last = nc.vector.tensor_scalar(self.match[:, r % 2, t - PIECES[r][0], :], self.tile_key[:, :], float(t + 1), None, ALU.is_equal)
                last.then_inc(S["matched"], 1)

            def look(self, pe, i, r):
                q = RING * (i - 1) + r
                pe.wait_ge(S["matched"], q + 1)
                if r == 0:
                    need(pe, S["chosen"], i - 1)
                for t in range(*PIECES[r]):
                    for c in range(self.count):
                        last = nc.tensor.matmul(self.at[c], self.match[:, r % 2, t - PIECES[r][0], c * P:(c + 1) * P],
                                                self.split[:, t].rearrange("p k d -> p (k d)"), start=(t == 0 and c % 2 == 0), stop=(t == NT - 1),
                                                skip_group_check=True)
                last.then_inc(S["looked"], 1)

            def choose(self, dve, i, xg):
                dve.wait_ge(S["looked"], RING * i)
                need(dve, S[self.reader], RING * i)
                for k in range(0, self.count, 2):
                    r, c = LOOKED[k]
                    n = 2 if (r + 1, c) in LOOKED[:self.count] else 1
                    parts = self.banks[k // 2][:, 0:n * 3 * D].rearrange("p (s k d) -> p s d k", s=n, k=3)
                    last = nc.vector.tensor_reduce(xg[:, r:r + n, c, 0:D], parts, AX, ALU.add)
                last.then_inc(S["chosen"], 1)

        def ahead(i):
            return not (isinstance(i, int) and i == ROUNDS - 1)

        with ExitStack() as ls:
            xg = sb("xg", [P, RING, C, D], f32, ls)
            idx = sb("idx", [P, RING, C], i32, ls)
            attr = sb("attr", [P, RING, C * D], f32, ls)
            attrT = sb("attrT", [P, 4 * P], f32, ls)
            eaT = sb("eaT", [P, 4 * P], f32, ls)
            sumT = sb("sumT", [P, 4 * P], f32, ls)
            mT = sb("mT", [P, 2, 4 * P], f32, ls)
            msg = sb("msg", [P, 2, C, D], f32, ls)
            hot = sb("hot", [P, 2, C, W], f32, ls)
            lo_hot = sb("lo_hot", [P, 2, C, P], bf16, ls)
            hi_hot = sb("hi_hot", [P, 2, C, NT], bf16, ls)
            pA, pE, pM, pG = bank[0], bank[1], bank[2], bank[3]
            pX = [bank[4], bank[5]]
            pH = wide
            lookup = Lookup(0, ls, "x_turned", [wide[:, BANK:2 * BANK]])
            with nc.Fori(0, npasses):
                with nc.Block() as block:
                    load = edge_loads(0, idx, attr, edge64)
                    gather = gathers(0, xg, idx)

                    @block.sync
                    def _(sp):
                        lookup.load(sp, 1)
                        load(sp, S["a_turned"], lambda i: lookup.load(sp, i + 2) if ahead(i) else None, peel_last=True)

                    @block.gpsimd
                    def _(pool):
                        gather(pool, S["x_turned"])

                    @block.tensor
                    def _(pe):
                        def message(n, b):
                            pe.wait_ge(S["m_done"], n + 1)
                            need(pe, S["msg_done"], n)
                            nc.tensor.matmul(pM[:, :], ones[0:1, :], bm_row[0:1, :], start=True, stop=False)
                            for j in range(4):
                                last = nc.tensor.matmul(pM[:, j * P:(j + 1) * P], mT[:, b, j * P:(j + 1) * P], WmBD[:, :],
                                                        start=False, stop=(j == 3))
                            last.then_inc(S["m_product"], 1)

                        def scatter(n, b):
                            pe.wait_ge(S["msg_done"], n + 1)
                            pe.wait_ge(S["hot_done"], n + 1)
                            need(pe, S["added"], n)
                            for c in range(C):
                                last = nc.tensor.matmul(pG[0:D, 0:W], msg[:, b, c, :], hot[:, b, c, :], start=(c == 0), stop=(c == C - 1))
                            last.then_inc(S["scattered"], 1)

                        def step(i, r):
                            n, b = RING * i + r, r % 2
                            first = isinstance(n, int) and n == 0
                            pe.wait_ge(ring_sems["attr_in"][r], 16 * (i + 1))
                            need(pe, S["a_kept"], n)
                            for j in range(4):
                                last = nc.tensor.transpose(pA[:, j * P:(j + 1) * P], attr[:, r, j * P:(j + 1) * P], ident[:, :])
                            last.then_inc(S["a_turned"], 1)
                            pe.wait_ge(ring_sems["gathered"][r], gathered_by(0, i, r))
                            need(pe, S["chosen"], i)
                            need(pe, S["m_done"], n - 1)
                            for j in range(4):
                                last = nc.tensor.transpose(pX[b][:, j * P:(j + 1) * P],
                                                           xg[:, r, 2 * j:2 * j + 2, :].rearrange("p c d -> p (c d)"), ident[:, :])
                            last.then_inc(S["x_turned"], 1)
                            if not first:
                                message(n - 1, 1 - b)
                            pe.wait_ge(S["a_kept"], n + 1)
                            need(pe, S["e_done"], n)
                            nc.tensor.matmul(pE[:, :], WeBD[:, :], attrT[:, :], start=True, stop=True).then_inc(S["e_product"], 1)
                            pe.wait_ge(S["keys_done"], n + 1)
                            for c in range(C):
                                last = nc.tensor.matmul(pH[:, 0:NT], lo_hot[:, b, c, :], hi_hot[:, b, c, :],
                                                        start=(first and c == 0), stop=False, skip_group_check=True)
                            last.then_inc(S["hist_done"], 1)
                            if not first:
                                scatter(n - 1, 1 - b)
                            if ahead(i):
                                lookup.look(pe, i + 1, r)

                        def tail():
                            message(G - 1, 1)
                            scatter(G - 1, 1)
                        pe.wait_ge(S["split"], 5)
                        over_groups(pe, step, tail, peel_last=True)

                    @block.scalar
                    def _(act):
                        def messages(n, b):
                            act.wait_ge(S["m_product"], n + 1)
                            need(act, S["scattered"], n - 1)
                            nc.scalar.activation(msg[:, b].rearrange("p c d -> p (c d)"), pM[:, :], ACT.Silu).then_inc(S["msg_done"], 1)

                        def step(i, r):
                            n, b = RING * i + r, r % 2
                            act.wait_ge(S["a_turned"], n + 1)
                            need(act, S["e_product"], n)
                            nc.scalar.copy(attrT[:, :], pA[:, :]).then_inc(S["a_kept"], 1)
                            if not (isinstance(n, int) and n == 0):
                                messages(n - 1, 1 - b)
                            act.wait_ge(S["e_product"], n + 1)
                            need(act, S["summed"], n)
                            nc.scalar.activation(eaT[:, :], pE[:, :], ACT.Silu, bias=be_col[:, 0:1]).then_inc(S["e_done"], 1)
                        over_groups(act, step, lambda: messages(G - 1, 1))

                    @block.vector
                    def _(dve):
                        windows = Windows(1)
                        lookup.keys(dve, 1)
                        lookup.split_rows(dve, xn[:, :, :])

                        def last_window(i):
                            if isinstance(i, int) and i == ROUNDS:
                                windows.load(i)

                        def add(n, r):
                            at = windows.of(r, 1)
                            dve.wait_ge(S["scattered"], n + 1)
                            need(dve, S["added"], n)
                            nc.vector.tensor_tensor(node_sum[0:D, at], node_sum[0:D, at], pG[0:D, 0:W], ALU.add).then_inc(S["added"], 1)

                        def step(i, r):
                            n, b = RING * i + r, r % 2
                            cols = bass.ds(n * C, C) if not isinstance(n, int) else slice(n * C, (n + 1) * C)
                            if ahead(i):
                                lookup.search(dve, i + 1, r)
                            if r == 0 and not (isinstance(i, int) and i == 0):
                                lookup.choose(dve, i, xg)
                            need(dve, S["scattered"], n - 1)
                            one_hot(hot, i, r).then_inc(S["hot_done"], 1)
                            need(dve, S["hist_done"], n - 1)
                            nc.vector.tensor_tensor(lo_hot[:, b], iota0[:, :].unsqueeze(1).to_broadcast([P, C, P]),
                                                    src_lo[:, cols].unsqueeze(2).to_broadcast([P, C, P]), ALU.is_equal)
                            nc.vector.tensor_tensor(hi_hot[:, b], iota0[:, 0:NT].unsqueeze(1).to_broadcast([P, C, NT]),
                                                    src_hi[:, cols].unsqueeze(2).to_broadcast([P, C, NT]), ALU.is_equal).then_inc(S["keys_done"], 1)
                            if ahead(i) and r == RING - 1:
                                lookup.keys(dve, i + 2)
                            if r == 0:
                                windows.load(i)
                            if not (isinstance(n, int) and n == 0):
                                add(n - 1, r)
                            dve.wait_ge(S["x_turned"], n + 1)
                            dve.wait_ge(S["e_done"], n + 1)
                            need(dve, S["m_done"], n)
                            nc.vector.tensor_tensor(sumT[:, :], pX[b][:, :], eaT[:, :], ALU.add).then_inc(S["summed"], 1)
                            dve.wait_ge(S["summed"], n + 1)
                            need(dve, S["m_product"], n - 1)
                            nc.vector.tensor_scalar(mT[:, b, :], sumT[:, :], 0.0, None, ALU.max).then_inc(S["m_done"], 1)
                        over_groups(dve, step, lambda: add(G - 1, 0), last_window, peel_last=True)
                next_pass(0)

        def transposes(pe, features, per, s_turn, s_used):
            for j, t0 in enumerate(range(0, NT, per)):
                need(pe, s_used, j - 1)
                for t in range(t0, min(t0 + per, NT)):
                    last = nc.tensor.transpose(bank[j % 2][:, (t - t0) * features:(t - t0 + 1) * features],
                                               node_sum[0:features, t * P:(t + 1) * P], ident[0:features, 0:features])
                last.then_inc(s_turn, 1)

        def read_tiles(dve, features, per, s_turn, s_used, use):
            for j, t0 in enumerate(range(0, NT, per)):
                dve.wait_ge(s_turn, j + 1)
                k = min(per, NT - t0)
                view = bank[j % 2][:, 0:k * features].rearrange("p (t f) -> p t f", f=features)
                use(t0, t0 + k, view).then_inc(s_used, 1)

        def over_tiles(v, free=D):
            return v.unsqueeze(1).to_broadcast([P, NT, free])

        def over_features(v):
            return v.unsqueeze(2).to_broadcast([P, NT, D])

        HALVES = ((0, (NT + 1) // 2), ((NT + 1) // 2, NT))

        class LayerNorm:

            def __init__(self, y, where):
                self.y = y
                self.centred, self.squared, self.var, self.root, self.own = (sem("ln_" + n, where) for n in (
                    "centred", "squared", "var", "root", "own"))

            def vector(self, dve, done):
                chain = Chain(dve, self.own)
                for a, z in HALVES:
                    y, mean = self.y[:, a:z, :], stat[:, 0, a:z]
                    chain.then(nc.vector.tensor_reduce(mean, y, AX, ALU.add))
                    chain.then(nc.vector.tensor_scalar(mean, mean, 1.0 / D, None, ALU.mult))
                    nc.vector.tensor_tensor(y, y, mean.unsqueeze(2).to_broadcast([P, z - a, D]), ALU.subtract).then_inc(self.centred, 1)
                for h, (a, z) in enumerate(HALVES):
                    var = stat[:, 1, a:z]
                    dve.wait_ge(self.squared, h + 1)
                    chain.then(nc.vector.tensor_reduce(var, rows[:, 1, a:z, :], AX, ALU.add))
                    nc.vector.tensor_scalar(var, var, 1.0 / D, EPS, ALU.mult, ALU.add).then_inc(self.var, 1)
                for h, (a, z) in enumerate(HALVES):
                    var = stat[:, 1, a:z]
                    dve.wait_ge(self.root, h + 1)
                    chain.then(nc.vector.reciprocal(var, var))
                    done(h, a, z, nc.vector.tensor_tensor(xn[:, a:z, :], self.y[:, a:z, :],
                                                          var.unsqueeze(2).to_broadcast([P, z - a, D]), ALU.mult))

            def scalar(self, act):
                for h, (a, z) in enumerate(HALVES):
                    act.wait_ge(self.centred, h + 1)
                    nc.scalar.square(rows[:, 1, a:z, :], self.y[:, a:z, :]).then_inc(self.squared, 1)
                for h, (a, z) in enumerate(HALVES):
                    act.wait_ge(self.var, h + 1)
                    nc.scalar.sqrt(stat[:, 1, a:z], stat[:, 1, a:z]).then_inc(self.root, 1)

        def store_halves(sp, table_dram, from_, ready, stored):
            for h, (a, z) in enumerate(HALVES):
                sp.wait_ge(ready, h + 1)
                sp.dma_start(table_dram[a * P:z * P, :].rearrange("(t p) d -> p t d", p=P), from_[:, a:z, :]).then_inc(stored, 16)
            sp.wait_ge(stored, 32)

        def clear_sums(pool, s_turn, banks):
            pool.wait_ge(s_turn, banks)
            nc.gpsimd.memset(node_sum[:, :], 0.0)

        with ExitStack() as ls:
            s_v, s_turn, s_used, s_o, s_part, s_total, s_var, s_std, s_xn, s_copied, s_key, s_ready, s_store = (
                sem("n0_" + n, ls) for n in ("v", "turn", "used", "o", "part", "total", "var", "std", "xn", "copied", "key",
                                             "ready", "store"))
            max_row = sb("max_row", [P, NP + W], f32, ls)
            si_all = sb("si_all", [P, NP + W], f32, ls)
            si_tiles = sb("si_tiles", [NT, P], f32, ls)
            with ExitStack() as ns:
                keyed = sb("keyed", [P, NT, D + 1], f32, ns)
                parts = sb("parts", [P, 2], f32, ns)
                tot = sb("tot", [P, 8], f32, ns)
                eps1 = sb("eps1", [P, 1], f32, ns)
                scale = sb("scale", [P, D], f32, ns)
                shift = sb("shift", [P, D], f32, ns)
                y = rows[:, 0]
                norm0 = LayerNorm(y, ns)
                with nc.Block() as block:
                    @block.tensor
                    def _(pe):
                        transposes(pe, D, 8, s_turn, s_used)
                        pe.wait_ge(s_part, 2)
                        nc.tensor.matmul(bank[2][:, 0:2], ones[:, :], parts[:, :], start=True, stop=True).then_inc(s_total, 1)

                    @block.gpsimd
                    def _(pool):
                        nc.gpsimd.memset(max_row[:, :], 0.0)
                        nc.gpsimd.memset(si_all[:, NP:NP + W], 0.0)
                        clear_sums(pool, s_turn, -(-NT // 8))

                    @block.scalar
                    def _(act):
                        act.wait_ge(s_o, 1)
                        nc.scalar.activation(rows[:, 1].rearrange("p t d -> p (t d)"), y.rearrange("p t d -> p (t d)"), ACT.Square,
                                             accum_out=parts[:, 1:2]).then_inc(s_part, 1)
                        act.wait_ge(s_var, 1)
                        nc.scalar.sqrt(tot[:, 4:5], tot[:, 3:4]).then_inc(s_std, 1)
                        norm0.scalar(act)
                        for h, (a, z) in enumerate(HALVES):
                            act.wait_ge(s_xn, h + 1)
                            nc.scalar.copy(keyed[:, a:z, 0:D], xn[:, a:z, :]).then_inc(s_copied, 1)

                    @block.sync
                    def _(sp):
                        sp.wait_ge(s_copied, 2)
                        store_halves(sp, table[1], keyed, s_ready, s_store)

                    @block.vector
                    def _(dve):
                        chain = Chain(dve, s_v)
                        nc.vector.tensor_copy(out_deg[:, :], pH[:, 0:NT])
                        chain.then(nc.vector.tensor_scalar(eps1[:, :], eps_col[:, :], 1.0, None, ALU.add))
                        read_tiles(dve, D, 8, s_turn, s_used, lambda a, z, v: nc.vector.scalar_tensor_tensor(
                            out=y[:, a:z, :], in0=xn[:, a:z, :], scalar=eps1[:, 0:1], in1=v, op0=ALU.mult, op1=ALU.add))
                        dve.wait_ge(s_used, -(-NT // 8))
                        nc.vector.tensor_scalar(y[:, NT - 1, :], y[:, NT - 1, :], real[:, 0:1], None, ALU.mult).then_inc(s_o, 1)
                        dve.wait_ge(s_o, 1)
                        nc.vector.tensor_reduce(parts[:, 0:1], y.rearrange("p t d -> p (t d)"), AX, ALU.add).then_inc(s_part, 1)
                        start_layer()
                        dve.wait_ge(s_total, 1)
                        chain.then(nc.vector.tensor_scalar(tot[:, 0:2], bank[2][:, 0:2], 1.0 / (N * D), None, ALU.mult))
                        chain.then(nc.vector.tensor_tensor(tot[:, 2:3], tot[:, 0:1], tot[:, 0:1], ALU.mult))
                        chain.then(nc.vector.tensor_tensor(tot[:, 3:4], tot[:, 1:2], tot[:, 2:3], ALU.subtract))
                        nc.vector.tensor_scalar(tot[:, 3:4], tot[:, 3:4], EPS, None, ALU.add).then_inc(s_var, 1)
                        dve.wait_ge(s_std, 1)
                        chain.then(nc.vector.reciprocal(tot[:, 5:6], tot[:, 4:5]))
                        chain.then(nc.vector.tensor_scalar(scale[:, :], vec["gamma2"][:, :], tot[:, 5:6], None, ALU.mult))
                        chain.then(nc.vector.tensor_scalar(shift[:, :], scale[:, :], tot[:, 0:1], None, ALU.mult))
                        chain.then(nc.vector.tensor_tensor(shift[:, :], vec["beta2"][:, :], shift[:, :], ALU.subtract))
                        chain.then(nc.vector.tensor_tensor(y, y, over_tiles(scale[:, :]), ALU.mult))
                        chain.then(nc.vector.tensor_tensor(y, y, over_tiles(shift[:, :]), ALU.add))
                        chain.then(nc.vector.tensor_tensor(y, y, xn[:, :, :], ALU.add))
                        chain.then(nc.vector.scalar_tensor_tensor(out=y, in0=y, scalar=0.0, in1=xn[:, :, :], op0=ALU.max, op1=ALU.add))
                        norm0.vector(dve, lambda h, a, z, last: last.then_inc(s_xn, 1))
                        for h, (a, z) in enumerate(HALVES):
                            dve.wait_ge(s_xn, h + 1)
                            chain.then(nc.vector.tensor_tensor(y[:, a:z, :], xn[:, a:z, :],
                                                               vec["w_j"][:, :].unsqueeze(1).to_broadcast([P, z - a, D]), ALU.mult))
                            chain.then(nc.vector.tensor_reduce(stat[:, 2, a:z], y[:, a:z, :], AX, ALU.add))
                            nc.vector.tensor_scalar(keyed[:, a:z, D], stat[:, 2, a:z], least[:, 0:1], None, ALU.subtract).then_inc(s_ready, 1)

            xg = sb("xg1", [P, RING, C, D + 1], f32, ls)
            idx = sb("idx1", [P, RING, C], i32, ls)
            hot = sb("hot1", [P, RING, C, W], f32, ls)
            kept = sb("kept", [P, RING, C, D + 1], f32, ls)
            key = kept[:, :, :, D]
            mask = sb("mask", [P, C, W], f32, ls)
            hotT = sb("hotT", [W, 2, C * P], f32, ls)
            tops = sb("tops", [W, 2], f32, ls)
            top = sb("top", [W, 1], f32, ls)
            topD = sb("topD", [W, W], f32, ls)
            sc = sb("sc", [P, 2, W], f32, ls)
            leaky = sb("leaky", [P, 2, W], f32, ls)
            drop = sb("drop", [D + 1, W], f32, ls)
            fac = sb("fac", [D + 1, W], f32, ls)
            picked = sb("picked", [W, 2, W], f32, ls)
            cols2 = sb("cols2", [W, 2], f32, ls)
            ea = sb("ea", [P, C], f32, ls)
            eb = sb("eb", [P, C], f32, ls)
            ec = sb("ec", [P, C], f32, ls)
            ex = sb("ex", [P, C], f32, ls)
            msg = sb("msg1", [P, 2, C, D + 1], f32, ls)
            pO = wide
            pK = [bank[0], bank[1]]
            pR, pL, pG = bank[2], bank[3], bank[4]
            with nc.Fori(0, npasses):
                with nc.Block() as block:
                    load = edge_loads(1, idx, None, None)
                    gather = gathers(1, xg, idx)

                    @block.sync
                    def _(sp):
                        def windows_si(i):
                            if not (isinstance(i, int) and i == 0):
                                return
                            sp.wait_ge(S["si_kept"], 1)
                            sp.dma_start(si_row.rearrange("(t p) -> t p", p=P), si_tiles[:, :]).then_inc(S["si_out"], 16)
                            sp.wait_ge(S["si_out"], 16)
                            sp.dma_start(si_all[:, 0:NP], si_row.partition_broadcast(P)).then_inc(S["si_in"], 16)
                        load(sp, None, windows_si)

                    @block.gpsimd
                    def _(pool):
                        gather(pool, S["rows_kept"])

                    def reached(n, lag):
                        return not (isinstance(n, int) and n < lag)

                    @block.tensor
                    def _(pe):
                        def look_up(n, b):
                            pe.wait_ge(S["cols_done"], n + 1)
                            pe.wait_ge(S["hot_kept"], n + 1)
                            need(pe, S["exp_in"], n)
                            for c in range(C):
                                last = nc.tensor.matmul(pL[:, 2 * c:2 * c + 2], hotT[:, b, c * P:(c + 1) * P], cols2[:, :], start=True, stop=True)
                            last.then_inc(S["looked_up"], 1)

                        def turn_keys(n):
                            pe.wait_ge(S["masked"], n + 1)
                            need(pe, S["max_found"], n)
                            for c in range(C):
                                last = nc.tensor.transpose(pK[c // 4][0:W, (c % 4) * P:(c % 4 + 1) * P], mask[:, c, :], ident[:, :])
                            last.then_inc(S["keys_turned"], 1)

                        def scatter(n, r):
                            pe.wait_ge(S["msg_done"], n + 1)
                            need(pe, S["added"], n)
                            for c in range(C):
                                last = nc.tensor.matmul(pG[0:D + 1, 0:W], msg[:, r % 2, c, :], hot[:, r, c, :], start=(c == 0), stop=(c == C - 1))
                            last.then_inc(S["scattered"], 1)

                        def spread_max(n):
                            pe.wait_ge(S["diag_done"], n + 1)
                            need(pe, S["v_b"], n)
                            nc.tensor.matmul(pR[:, 0:W], ones[0:W, :], topD[:, :], start=True, stop=True).then_inc(S["max_spread"], 1)

                        def step(i, r):
                            n = RING * i + r
                            if reached(n, 1):
                                turn_keys(n - 1)
                            pe.wait_ge(S["hot_done"], n + 1)
                            need(pe, S["hot_kept"], n)
                            for c in range(C):
                                last = nc.tensor.transpose(pO[0:W, c * P:(c + 1) * P], hot[:, r, c, :], ident[:, :])
                            last.then_inc(S["hot_turned"], 1)
                            if reached(n, 2):
                                look_up(n - 2, r % 2)
                            if reached(n, 1):
                                spread_max(n - 1)
                            if reached(n, 2):
                                scatter(n - 2, (r - 2) % RING)

                        def tail():
                            turn_keys(G - 1)
                            look_up(G - 2, 0)
                            spread_max(G - 1)
                            scatter(G - 2, (G - 2) % RING)
                            look_up(G - 1, 1)
                            scatter(G - 1, (G - 1) % RING)
                        pe.wait_ge(S["si_ready"], 1)
                        nc.tensor.transpose(bank[5][0:NT, 0:P], stat[:, 2, :], ident[:, :]).then_inc(S["si_turned"], 1)
                        over_groups(pe, step, tail)

                    @block.scalar
                    def _(act):
                        def exps(n):
                            act.wait_ge(S["factor_in"], n + 1)
                            need(act, S["scaled"], n)
                            nc.scalar.activation(fac[:, :], drop[:, :], ACT.Exp).then_inc(S["factor_done"], 1)
                            act.wait_ge(S["exp_in"], n + 1)
                            need(act, S["msg_done"], n)
                            nc.scalar.activation(ex[:, :], ec[:, :], ACT.Exp).then_inc(S["exp_done"], 1)

                        def keep_rows(i, r):
                            n = RING * i + r
                            act.wait_ge(ring_sems["gathered"][r], 16 * C * (i + 1))
                            need(act, S["msg_done"], n - 3)
                            nc.scalar.copy(kept[:, r].rearrange("p c d -> p (c d)"), xg[:, r].rearrange("p c d -> p (c d)")).then_inc(S["rows_kept"], 1)

                        def step(i, r):
                            n = RING * i + r
                            keep_rows(i, r)
                            if reached(n, 2):
                                exps(n - 2)
                            act.wait_ge(S["hot_done"], n + 1)
                            act.wait_ge(S["rows_kept"], n + 1)
                            need(act, S["keys_turned"], n)
                            for c in range(C):
                                last = nc.scalar.activation(mask[:, c, :], hot[:, r, c, :], ACT.Copy, scale=kept[:, r, c, D:D + 1])
                            last.then_inc(S["masked"], 1)
                            act.wait_ge(S["hot_turned"], n + 1)
                            need(act, S["looked_up"], n - 1)
                            for h in range(2):
                                last = nc.scalar.copy(hotT[:, r % 2, h * BANK:(h + 1) * BANK], pO[0:W, h * BANK:(h + 1) * BANK])
                            last.then_inc(S["hot_kept"], 1)

                        def tail():
                            exps(G - 2)
                            exps(G - 1)
                        over_groups(act, step, tail)

                    @block.vector
                    def _(dve):
                        windows = Windows(3)

                        def scores(n, at):
                            k = 6 * n
                            dve.wait_ge(S["max_spread"], n + 1)
                            if isinstance(n, int) and n == 0:
                                dve.wait_ge(S["si_in"], 16)
                            nc.vector.tensor_tensor(sc[:, 0, :], max_row[:, at], si_all[:, at], ALU.add).then_inc(S["v_a"], 1)
                            nc.vector.tensor_tensor(picked[:, 0, :], si_all[0:W, at], ident[0:W, 0:W], ALU.mult)
                            dve.wait_ge(S["v_a"], k + 1)
                            nc.vector.tensor_tensor(max_row[:, at], max_row[:, at], pR[:, 0:W], ALU.max).then_inc(S["v_b"], 1)
                            dve.wait_ge(S["v_b"], n + 1)
                            nc.vector.tensor_tensor(sc[:, 1, :], max_row[:, at], si_all[:, at], ALU.add).then_inc(S["v_a"], 1)
                            dve.wait_ge(S["v_a"], k + 2)
                            two = sc[:, :, :]
                            nc.vector.scalar_tensor_tensor(out=leaky[:, :, :], in0=two, scalar=SLOPE, in1=two,
                                                           op0=ALU.mult, op1=ALU.max).then_inc(S["v_a"], 1)
                            dve.wait_ge(S["v_a"], k + 3)
                            nc.vector.tensor_tensor(picked[:, 1, :], leaky[0:W, 1, :], ident[0:W, 0:W], ALU.mult).then_inc(S["v_a"], 1)
                            need(dve, S["factor_done"], n)
                            nc.vector.tensor_tensor(drop[:, :], leaky[0:D + 1, 0, :], leaky[0:D + 1, 1, :], ALU.subtract).then_inc(S["factor_in"], 1)
                            dve.wait_ge(S["v_a"], k + 4)
                            need(dve, S["looked_up"], n)
                            nc.vector.tensor_reduce(cols2[:, :], picked[:, :, :], AX, ALU.add).then_inc(S["cols_done"], 1)

                        def exponents(n, r):
                            k = 6 * n
                            dve.wait_ge(S["looked_up"], n + 1)
                            found = pL[:, 0:2 * C].rearrange("p (c k) -> p c k", k=2)
                            nc.vector.tensor_tensor(ea[:, :], found[:, :, 0], key[:, r, :], ALU.add).then_inc(S["v_a"], 1)
                            dve.wait_ge(S["v_a"], k + 5)
                            nc.vector.scalar_tensor_tensor(out=eb[:, :], in0=ea[:, :], scalar=SLOPE, in1=ea[:, :],
                                                           op0=ALU.mult, op1=ALU.max).then_inc(S["v_a"], 1)
                            dve.wait_ge(S["v_a"], k + 6)
                            need(dve, S["exp_done"], n)
                            nc.vector.tensor_tensor(ec[:, :], eb[:, :], found[:, :, 1], ALU.subtract).then_inc(S["exp_in"], 1)

                        def messages(n, r, at):
                            dve.wait_ge(S["factor_done"], n + 1)
                            need(dve, S["added"], n)
                            nc.vector.tensor_tensor(node_sum[:, at], node_sum[:, at], fac[:, :],
                                                    ALU.mult).then_inc(S["scaled"], 1)
                            dve.wait_ge(S["exp_done"], n + 1)
                            need(dve, S["scattered"], n - 1)
                            nc.vector.tensor_copy(msg[:, r % 2, :, D], ex[:, :])
                            nc.vector.tensor_tensor(msg[:, r % 2, :, 0:D], kept[:, r, :, 0:D], ex[:, :].unsqueeze(2).to_broadcast([P, C, D]),
                                                    ALU.mult).then_inc(S["msg_done"], 1)

                        def maxima(n):
                            dve.wait_ge(S["keys_turned"], n + 1)
                            for h in range(2):
                                last = nc.vector.tensor_reduce(tops[:, h:h + 1], pK[h][0:W, :], AX, ALU.max)
                            last.then_inc(S["m_done"], 1)
                            dve.wait_ge(S["m_done"], n + 1)
                            nc.vector.tensor_tensor(top[:, 0:1], tops[:, 0:1], tops[:, 1:2], ALU.max).then_inc(S["max_found"], 1)
                            dve.wait_ge(S["max_found"], n + 1)
                            need(dve, S["max_spread"], n)
                            nc.vector.tensor_scalar(topD[:, :], ident[0:W, 0:W], top[:, 0:1], None, ALU.mult).then_inc(S["diag_done"], 1)

                        def add(n, at):
                            dve.wait_ge(S["scattered"], n + 1)
                            dve.wait_ge(S["scaled"], n + 1)
                            nc.vector.tensor_tensor(node_sum[:, at], node_sum[:, at],
                                                    pG[0:D + 1, 0:W], ALU.add).then_inc(S["added"], 1)

                        def step(i, r):
                            n = RING * i + r
                            need(dve, S["scattered"], n - 3)
                            one_hot(hot, i, r, RING).then_inc(S["hot_done"], 1)
                            if reached(n, 2):
                                scores(n - 2, windows.of(r, 2))
                            if reached(n, 1):
                                maxima(n - 1)
                            if reached(n, 3):
                                add(n - 3, windows.of(r, 3))
                            if reached(n, 2):
                                exponents(n - 2, (r - 2) % RING)
                                messages(n - 2, (r - 2) % RING, windows.of(r, 2))

                        def tail():
                            add(G - 3, windows.of(0, 3))
                            scores(G - 2, windows.of(0, 2))
                            maxima(G - 1)
                            exponents(G - 2, (G - 2) % RING)
                            messages(G - 2, (G - 2) % RING, windows.of(0, 2))
                            add(G - 2, windows.of(1, 3))
                            scores(G - 1, windows.of(1, 2))
                            exponents(G - 1, (G - 1) % RING)
                            messages(G - 1, (G - 1) % RING, windows.of(1, 2))
                            add(G - 1, windows.of(2, 3))
                        nc.vector.tensor_tensor(rows[:, 0], xn[:, :, :], over_tiles(vec["w_i"][:, :]), ALU.mult).then_inc(S["si_prod"], 1)
                        dve.wait_ge(S["si_prod"], 1)
                        nc.vector.tensor_reduce(stat[:, 2, :], rows[:, 0], AX, ALU.add).then_inc(S["si_prod"], 1)
                        dve.wait_ge(S["si_prod"], 2)
                        nc.vector.tensor_scalar(stat[:, 2, :], stat[:, 2, :], least[:, 0:1], None, ALU.add).then_inc(S["si_ready"], 1)
                        dve.wait_ge(S["si_turned"], 1)
                        nc.vector.tensor_copy(si_tiles[:, :], bank[5][0:NT, 0:P]).then_inc(S["si_kept"], 1)
                        over_groups(dve, step, tail, windows.load)
                next_pass(1)

        with ExitStack() as ls:
            s_v, s_turn, s_used, s_deg, s_root, s_xn, s_table, s_store = (sem(n, ls) for n in (
                "n1_v", "n1_turn", "n1_used", "n1_deg", "n1_root", "n1_xn", "n1_table", "n1_store"))
            y = rows[:, 0]
            norm1 = LayerNorm(y, ls)
            xg2 = sb("xg2", [P, RING, C, D + 1])
            with nc.Block() as block:
                @block.tensor
                def _(pe):
                    transposes(pe, D + 1, 7, s_turn, s_used)

                @block.gpsimd
                def _(pool):
                    nc.gpsimd.memset(xg2[:, :, :, D:D + 1], 1.0)
                    clear_sums(pool, s_turn, NT // 7)

                @block.scalar
                def _(act):
                    act.wait_ge(s_deg, 1)
                    nc.scalar.sqrt(stat[:, 4, :], stat[:, 3, :]).then_inc(s_root, 1)
                    norm1.scalar(act)

                @block.sync
                def _(sp):
                    store_halves(sp, table[2], rows[:, 1], s_table, s_store)

                @block.vector
                def _(dve):
                    chain = Chain(dve, s_v)

                    def use(a, z, v):
                        chain.then(nc.vector.tensor_scalar(stat[:, 5, a:z], v[:, :, D], 1e-30, None, ALU.max))
                        chain.then(nc.vector.reciprocal(stat[:, 6, a:z], stat[:, 5, a:z]))
                        chain.then(nc.vector.tensor_tensor(y[:, a:z, :], v[:, :, 0:D], stat[:, 6, a:z].unsqueeze(2).to_broadcast([P, z - a, D]), ALU.mult))
                        return nc.vector.scalar_tensor_tensor(out=y[:, a:z, :], in0=y[:, a:z, :], scalar=0.0, in1=xn[:, a:z, :],
                                                              op0=ALU.max, op1=ALU.add)
                    nc.vector.tensor_scalar(stat[:, 3, :], out_deg[:, :], 1.0, None, ALU.max).then_inc(s_deg, 1)
                    read_tiles(dve, D + 1, 7, s_turn, s_used, use)
                    start_layer()
                    dve.wait_ge(s_root, 1)
                    chain.then(nc.vector.reciprocal(stat[:, 4, :], stat[:, 4, :]))
                    dve.wait_ge(s_used, NT // 7)
                    norm1.vector(dve, lambda h, a, z, last: last.then_inc(s_xn, 1))
                    for h, (a, z) in enumerate(HALVES):
                        dve.wait_ge(s_xn, h + 1)
                        nc.vector.tensor_tensor(rows[:, 1, a:z, :], xn[:, a:z, :], stat[:, 4, a:z].unsqueeze(2).to_broadcast([P, z - a, D]),
                                                ALU.mult).then_inc(s_table, 1)

        with ExitStack() as ls:
            xg = xg2
            idx = sb("idx2", [P, RING, C], i32, ls)
            hot = sb("hot2", [P, 2, C, W], f32, ls)
            pG2 = [bank[0], bank[1]]
            lookup = Lookup(2, ls, "scattered", [wide[:, 0:BANK], wide[:, BANK:2 * BANK], bank[5]])
            with nc.Fori(0, npasses):
                with nc.Block() as block:
                    load = edge_loads(2, idx, None, None)
                    gather = gathers(2, xg, idx)

                    @block.sync
                    def _(sp):
                        lookup.load(sp, 1)
                        load(sp, None, lambda i: lookup.load(sp, i + 2) if ahead(i) else None, peel_last=True)

                    @block.gpsimd
                    def _(pool):
                        gather(pool, S["scattered"])

                    @block.tensor
                    def _(pe):
                        def step(i, r):
                            n, b = RING * i + r, r % 2
                            pe.wait_ge(ring_sems["gathered"][r], gathered_by(2, i, r))
                            need(pe, S["chosen"], i)
                            pe.wait_ge(S["hot_done"], n + 1)
                            need(pe, S["added"], n - 1)
                            for c in range(C):
                                last = nc.tensor.matmul(pG2[b][0:D + 1, 0:W], xg[:, r, c, :], hot[:, b, c, :], start=(c == 0), stop=(c == C - 1))
                            last.then_inc(S["scattered"], 1)
                            if ahead(i):
                                lookup.look(pe, i + 1, r)
                        pe.wait_ge(S["split"], 5)
                        over_groups(pe, step, peel_last=True)

                    @block.vector
                    def _(dve):
                        windows = Windows(1)
                        lookup.keys(dve, 1)
                        lookup.split_rows(dve, rows[:, 1])

                        def last_window(i):
                            if isinstance(i, int) and i == ROUNDS:
                                windows.load(i)
                        def add(n, r):
                            at = windows.of(r, 1)
                            dve.wait_ge(S["scattered"], n + 1)
                            need(dve, S["added"], n)
                            nc.vector.tensor_tensor(node_sum[:, at], node_sum[:, at], pG2[(r - 1) % 2][0:D + 1, 0:W],
                                                    ALU.add).then_inc(S["added"], 1)

                        def step(i, r):
                            n, b = RING * i + r, r % 2
                            first = isinstance(i, int) and i == 0
                            if ahead(i):
                                lookup.search(dve, i + 1, r)
                            if r == 0 and not first:
                                lookup.choose(dve, i, xg)
                            need(dve, S["scattered"], n - 1)
                            one_hot(hot, i, r).then_inc(S["hot_done"], 1)
                            if ahead(i) and r == RING - 1:
                                lookup.keys(dve, i + 2)
                            if r == 0:
                                windows.load(i)
                            if not (isinstance(n, int) and n == 0):
                                add(n - 1, r)
                        over_groups(dve, step, lambda: add(G - 1, 0), last_window, peel_last=True)
                next_pass(2)

        with ExitStack() as ls:
            s_v, s_turn, s_used, s_deg, s_root, s_xn, s_table, s_store = (sem(n, ls) for n in (
                "n2_v", "n2_turn", "n2_used", "n2_deg", "n2_root", "n2_xn", "n2_table", "n2_store"))
            s_xturn, s_xkept = sem("n2_xturn", ls), sem("n2_xkept", ls)
            y = rows[:, 0]
            norm2 = LayerNorm(y, ls)
            in_deg = stat[:, 3, :]
            with nc.Block() as block:
                @block.tensor
                def _(pe):
                    transposes(pe, D + 1, 7, s_turn, s_used)
                    for j, t0 in enumerate(range(0, NT, 4)):
                        tiles = range(t0, min(t0 + 4, NT))
                        pe.wait_ge(s_xn, 1 if tiles[-1] < HALVES[0][1] else 2)
                        need(pe, s_xkept, j - 1)
                        for t in tiles:
                            last = nc.tensor.transpose(bank[2 + j % 2][0:D, (t - t0) * P:(t - t0 + 1) * P], xn[:, t, :], ident[:, :])
                        last.then_inc(s_xturn, 1)

                @block.gpsimd
                def _(pool):
                    nc.gpsimd.memset(node_sum[:, NP:NP + W], 0.0)

                @block.scalar
                def _(act):
                    act.wait_ge(s_deg, 1)
                    nc.scalar.sqrt(stat[:, 4, :], in_deg).then_inc(s_root, 1)
                    norm2.scalar(act)
                    for j, t0 in enumerate(range(0, NT, 4)):
                        act.wait_ge(s_xturn, j + 1)
                        cols = slice(t0 * P, min(t0 + 4, NT) * P)
                        nc.scalar.copy(node_sum[0:D, cols], bank[2 + j % 2][0:D, 0:cols.stop - cols.start]).then_inc(s_xkept, 1)

                @block.sync
                def _(sp):
                    store_halves(sp, table[3], rows[:, 1], s_table, s_store)

                @block.vector
                def _(dve):
                    chain = Chain(dve, s_v)

                    def use(a, z, v):
                        chain.then(nc.vector.tensor_scalar(in_deg[:, a:z], v[:, :, D], 1.0, None, ALU.max))
                        return nc.vector.tensor_copy(y[:, a:z, :], v[:, :, 0:D])
                    read_tiles(dve, D + 1, 7, s_turn, s_used, use)
                    dve.wait_ge(s_used, NT // 7)
                    nc.vector.tensor_copy(stat[:, 5, :], in_deg).then_inc(s_deg, 1)
                    start_layer()
                    dve.wait_ge(s_root, 1)
                    chain.then(nc.vector.reciprocal(stat[:, 4, :], stat[:, 4, :]))
                    chain.then(nc.vector.tensor_tensor(y, y, over_features(stat[:, 4, :]), ALU.mult))
                    chain.then(nc.vector.scalar_tensor_tensor(out=y, in0=y, scalar=ALPHA_TOTAL, in1=xn[:, :, :], op0=ALU.mult, op1=ALU.add))
                    norm2.vector(dve, lambda h, a, z, last: last.then_inc(s_xn, 1))
                    for h, (a, z) in enumerate(HALVES):
                        dve.wait_ge(s_xn, h + 1)
                        nc.vector.tensor_tensor(rows[:, 1, a:z, :], xn[:, a:z, :], vec["b_e"][:, :].unsqueeze(1).to_broadcast([P, z - a, D]),
                                                ALU.add).then_inc(s_table, 1)

        with ExitStack() as ls:
            xg = sb("xg3", [P, RING, C, D], f32, ls)
            idx = sb("idx3", [P, RING, C], i32, ls)
            attr = sb("attr3", [P, RING, C * D3], f32, ls)
            attrT = sb("attrT3", [P, P], f32, ls)
            msg = sb("msg3", [P, 2, C, D], f32, ls)
            hot = sb("hot3", [P, 2, C, W], f32, ls)
            pA, pG = bank[0], bank[1]
            pE = [bank[2], bank[3]]
            lookup = Lookup(3, ls, "summed", [wide[:, 0:BANK], wide[:, BANK:2 * BANK]])
            with nc.Fori(0, npasses):
                with nc.Block() as block:
                    load = edge_loads(3, idx, attr, edge16)
                    gather = gathers(3, xg, idx)

                    @block.sync
                    def _(sp):
                        lookup.load(sp, 1)
                        load(sp, S["a_turned"], lambda i: lookup.load(sp, i + 2) if ahead(i) else None, peel_last=True)

                    @block.gpsimd
                    def _(pool):
                        gather(pool, S["summed"])

                    @block.tensor
                    def _(pe):
                        def scatter(n, b):
                            pe.wait_ge(S["msg_done"], n + 1)
                            pe.wait_ge(S["hot_done"], n + 1)
                            need(pe, S["added"], n)
                            for c in range(C):
                                last = nc.tensor.matmul(pG[0:D, 0:W], msg[:, b, c, :], hot[:, b, c, :], start=(c == 0), stop=(c == C - 1))
                            last.then_inc(S["scattered"], 1)

                        def step(i, r):
                            n, b = RING * i + r, r % 2
                            pe.wait_ge(ring_sems["attr_in"][r], 16 * (i + 1))
                            need(pe, S["a_kept"], n)
                            nc.tensor.transpose(pA[:, 0:P], attr[:, r, :], ident[:, :]).then_inc(S["a_turned"], 1)
                            if not (isinstance(n, int) and n == 0):
                                scatter(n - 1, 1 - b)
                            pe.wait_ge(S["a_kept"], n + 1)
                            need(pe, S["summed"], n - 1)
                            nc.tensor.matmul(pE[b][:, :], attrT[:, :], W3BD[:, :], start=True, stop=True).then_inc(S["e_product"], 1)
                            if ahead(i):
                                lookup.look(pe, i + 1, r)
                        pe.wait_ge(S["split"], 5)
                        over_groups(pe, step, lambda: scatter(G - 1, 1), peel_last=True)

                    @block.scalar
                    def _(act):
                        def step(i, r):
                            n, b = RING * i + r, r % 2
                            act.wait_ge(S["a_turned"], n + 1)
                            need(act, S["e_product"], n)
                            nc.scalar.copy(attrT[:, :], pA[:, 0:P]).then_inc(S["a_kept"], 1)
                            act.wait_ge(S["summed"], n + 1)
                            nc.scalar.activation(msg[:, b].rearrange("p c d -> p (c d)"), msg[:, b].rearrange("p c d -> p (c d)"),
                                                 ACT.Relu).then_inc(S["msg_done"], 1)
                        over_groups(act, step)

                    @block.vector
                    def _(dve):
                        windows = Windows(1)
                        lookup.keys(dve, 1)
                        lookup.split_rows(dve, rows[:, 1])

                        def last_window(i):
                            if isinstance(i, int) and i == ROUNDS:
                                windows.load(i)
                        def add(n, r):
                            at = windows.of(r, 1)
                            dve.wait_ge(S["scattered"], n + 1)
                            need(dve, S["added"], n)
                            nc.vector.tensor_tensor(node_sum[0:D, at], node_sum[0:D, at], pG[0:D, 0:W], ALU.add).then_inc(S["added"], 1)

                        def step(i, r):
                            n = RING * i + r
                            first = isinstance(i, int) and i == 0
                            if ahead(i):
                                lookup.search(dve, i + 1, r)
                            if r == 0 and not first:
                                lookup.choose(dve, i, xg)
                            need(dve, S["scattered"], n - 1)
                            one_hot(hot, i, r).then_inc(S["hot_done"], 1)
                            dve.wait_ge(ring_sems["gathered"][r], gathered_by(3, i, r))
                            need(dve, S["chosen"], i)
                            dve.wait_ge(S["e_product"], n + 1)
                            nc.vector.tensor_tensor(msg[:, r % 2].rearrange("p c d -> p (c d)"), pE[r % 2][:, :],
                                                    xg[:, r].rearrange("p c d -> p (c d)"), ALU.add).then_inc(S["summed"], 1)
                            if ahead(i) and r == RING - 1:
                                lookup.keys(dve, i + 2)
                            if r == 0:
                                windows.load(i)
                            if not (isinstance(n, int) and n == 0):
                                add(n - 1, r)
                        over_groups(dve, step, lambda: add(G - 1, 0), last_window, peel_last=True)
                next_pass(3)

        with ExitStack() as ls:
            (s_v, s_h, s_hused, s_part, s_total, s_var, s_std, s_xn, s_out) = (sem(n, ls) for n in (
                "n3_v", "n3_h", "n3_hused", "n3_part", "n3_total", "n3_var", "n3_std", "n3_xn", "n3_out"))
            norm3 = LayerNorm(rows[:, 0], ls)
            part_sum = sb("n3_part_sum", [P, D], f32, ls)
            mean = sb("n3_mean", [P, D], f32, ls)
            var = sb("n3_var_sb", [P, D], f32, ls)
            std = sb("n3_std_sb", [P, D], f32, ls)
            y, z = rows[:, 0], rows[:, 1]
            by_feature = y.rearrange("p t d -> p d t")
            z_by_feature = z.rearrange("p t d -> p d t")
            with nc.Block() as block:
                @block.tensor
                def _(pe):
                    for j, t0 in enumerate(range(0, NT, 8)):
                        need(pe, s_hused, j - 1)
                        for t in range(t0, min(t0 + 8, NT)):
                            last = nc.tensor.matmul(bank[2 + j % 2][:, (t - t0) * D:(t - t0 + 1) * D], node_sum[0:D, t * P:(t + 1) * P],
                                                    Wgin[:, :], start=True, stop=True)
                        last.then_inc(s_h, 1)
                    pe.wait_ge(s_part, 1)
                    nc.tensor.matmul(bank[4][:, 0:D], ones[:, :], part_sum[:, :], start=True, stop=True).then_inc(s_total, 1)
                    pe.wait_ge(s_part, 2)
                    nc.tensor.matmul(bank[5][:, 0:D], ones[:, :], part_sum[:, :], start=True, stop=True).then_inc(s_total, 1)

                @block.scalar
                def _(act):
                    act.wait_ge(s_var, 1)
                    nc.scalar.sqrt(std[:, :], var[:, :]).then_inc(s_std, 1)
                    norm3.scalar(act)

                @block.sync
                def _(sp):
                    full = NT - 1
                    for h, (a, z) in enumerate(HALVES):
                        sp.wait_ge(s_xn, h + 1)
                        z = min(z, full)
                        sp.dma_start(out[a * P:z * P, :].rearrange("(t p) d -> p t d", p=P), xn[:, a:z, :]).then_inc(s_out, 16)
                    sp.dma_start(out[full * P:N, :], xn[0:LAST, full, :]).then_inc(s_out, 16)
                    sp.wait_ge(s_out, 48)

                @block.vector
                def _(dve):
                    chain = Chain(dve, s_v)
                    for j, t0 in enumerate(range(0, NT, 8)):
                        dve.wait_ge(s_h, j + 1)
                        k = min(8, NT - t0)
                        nc.vector.tensor_tensor(y[:, t0:t0 + k, :], bank[2 + j % 2][:, 0:k * D].rearrange("p (t d) -> p t d", d=D),
                                                vec["b_gin"][:, :].unsqueeze(1).to_broadcast([P, k, D]), ALU.add).then_inc(s_hused, 1)
                    dve.wait_ge(s_hused, -(-NT // 8))
                    chain.then(nc.vector.tensor_scalar(y[:, NT - 1, :], y[:, NT - 1, :], real[:, 0:1], None, ALU.mult))
                    nc.vector.tensor_reduce(part_sum[:, :], by_feature, AX, ALU.add).then_inc(s_part, 1)
                    dve.wait_ge(s_total, 1)
                    chain.then(nc.vector.tensor_scalar(mean[:, :], bank[4][:, 0:D], 1.0 / N, None, ALU.mult))
                    chain.then(nc.vector.tensor_tensor(y, y, over_tiles(mean[:, :]), ALU.subtract))
                    chain.then(nc.vector.tensor_tensor(z, y, y, ALU.mult))
                    chain.then(nc.vector.tensor_scalar(z[:, NT - 1, :], z[:, NT - 1, :], real[:, 0:1], None, ALU.mult))
                    nc.vector.tensor_reduce(part_sum[:, :], z_by_feature, AX, ALU.add).then_inc(s_part, 1)
                    dve.wait_ge(s_total, 2)
                    nc.vector.tensor_scalar(var[:, :], bank[5][:, 0:D], 1.0 / N, EPS, ALU.mult, ALU.add).then_inc(s_var, 1)
                    dve.wait_ge(s_std, 1)
                    chain.then(nc.vector.reciprocal(std[:, :], std[:, :]))
                    chain.then(nc.vector.tensor_tensor(std[:, :], std[:, :], vec["gamma3"][:, :], ALU.mult))
                    chain.then(nc.vector.tensor_tensor(y, y, over_tiles(std[:, :]), ALU.mult))
                    chain.then(nc.vector.tensor_tensor(y, y, over_tiles(vec["beta3"][:, :]), ALU.add))
                    chain.then(nc.vector.scalar_tensor_tensor(out=y, in0=y, scalar=0.0, in1=xn[:, :, :], op0=ALU.max, op1=ALU.add))
                    norm3.vector(dve, lambda h, a, z, last: last.then_inc(s_xn, 1))


_FLOATS = ["edge_attr_16", "edge_attr_64", "L0_gnn_We2", "L0_gnn_be2", "L0_gnn_Wm2", "L0_gnn_bm2", "L0_gnn_eps2",
           "L0_gnn_gamma2", "L0_gnn_beta2", "L1_gnn_w_i", "L1_gnn_w_j", "L3_gnn_W_e", "L3_gnn_b_e", "L3_gnn_W_gin",
           "L3_gnn_b_gin", "L3_gnn_gamma", "L3_gnn_beta"]


def kernel(**inputs):
    import numpy as np
    import concourse.bacc as bacc
    from concourse.bass_utils import run_bass_kernel_spmd

    def padded(a, rows, fill):
        a = np.asarray(a)
        more = np.full((rows - a.shape[0],) + a.shape[1:], fill, a.dtype)
        return np.ascontiguousarray(np.concatenate([a, more]))

    arrays = {
        "x": padded(inputs["x"], NP, 0),
        "src": padded(inputs["src"], EP, N),
        "dst": padded(inputs["dst"], EP, N),
    }
    by_round = arrays["src"].reshape(ROUNDS, RING, P, C)
    looked_up = padded(np.stack([by_round[:, r, :, c] for r, c in LOOKED], axis=1).reshape(-1), (ROUNDS + 1) * len(LOOKED) * P, N)
    arrays = {"x": arrays["x"], "src": arrays["src"], "src_looked_up": looked_up, "dst": arrays["dst"]}
    for name in _FLOATS:
        a = np.ascontiguousarray(np.asarray(inputs[name]))
        arrays[name] = padded(a, EP, 0) if name.startswith("edge") else a
    nc = bacc.Bacc("TRN2", target_bir_lowering=False, num_devices=1)
    args = [nc.dram_tensor("in_" + n, a.shape, mybir.dt.from_np(a.dtype), kind="ExternalInput").ap() for n, a in arrays.items()]
    out = nc.dram_tensor("out", (N, D), f32, kind="ExternalOutput").ap()
    build_program(nc, *args, out)
    r = run_bass_kernel_spmd(nc, [{"in_" + n: a for n, a in arrays.items()}], core_ids=[0])
    return r.results[0]["out"]
```
